# Optimizing a Trainium2 kernel written in Bass

```python
import numpy as np
import jax
import jax.numpy as jnp

def _softmax(x, axis=-1):
    return jax.nn.softmax(x, axis=axis)
def _gelu(x):
    return jax.nn.gelu(x, approximate=True)
def _silu(x):
    return jax.nn.silu(x)
def _sigmoid(x):
    return jax.nn.sigmoid(x)
def _layernorm(x, axis=-1, eps=1e-5):
    m = jnp.mean(x, axis=axis, keepdims=True)
    v = jnp.var(x, axis=axis, keepdims=True)
    return (x - m) / jnp.sqrt(v + eps)
def _scatter_add(tgt, idx, src, axis=0):
    return tgt.at[idx].add(src)
def _segment_sum(src, seg, n):
    return jax.ops.segment_sum(src, seg, n)

kernel_name = 'mk_conv_attn_hybrid_d2_conv_nchw128_2ee97e'

def setup_inputs(seed: int = 0):
    np.random.seed(seed)
    _w = jnp.asarray
    def _rec_inputs():
        import jax
        import jax.numpy as jnp
        _gk = jax.random.key(seed)
        x = -0.0005207 + 1.001 * jax.random.normal(jax.random.fold_in(_gk, 1), (4, 128, 64, 64), jnp.float32)
        return x
    x = _rec_inputs()
    def _L0_conv_setup():
        import jax, jax.numpy as jnp
        import numpy as np
        B, C, H, W = (4, 128, 64, 64)
        E, N, R, K = (256, 16, 8, 4)
        L = H * W
        EPS = 1e-05
        NEG_SLOPE = 0.01

        def _stage(x, i, bn_gamma, bn_beta, ln_gamma, ln_beta, W_in, conv_w, conv_b, W_xp, W_dt, b_dt, A_log, Dp, W_out):
            mu = x.mean((0, 2, 3))
            var = x.var((0, 2, 3))
            xn = (x - mu[None, :, None, None]) * jax.lax.rsqrt(var + EPS)[None, :, None, None]
            xn = xn * bn_gamma[i][None, :, None, None] + bn_beta[i][None, :, None, None]
            xn = jax.nn.leaky_relu(xn, NEG_SLOPE)
            u = xn.transpose(0, 2, 3, 1).reshape(B, L, C)
            mu2 = u.mean(-1, keepdims=True)
            v2 = u.var(-1, keepdims=True)
            un = (u - mu2) * jax.lax.rsqrt(v2 + EPS) * ln_gamma[i] + ln_beta[i]
            xz = un @ W_in[i]
            xm, z = (xz[..., :E], xz[..., E:])
            xc = xm.transpose(0, 2, 1)
            xc = jax.lax.conv_general_dilated(xc, conv_w[i][:, None, :], (1,), [(K - 1, 0)], feature_group_count=E)
            xm = jax.nn.silu(xc.transpose(0, 2, 1) + conv_b[i])
            dbl = xm @ W_xp[i]
            dt = jax.nn.softplus(dbl[..., :R] @ W_dt[i] + b_dt[i])
            Bm = dbl[..., R:R + N]
            Cm = dbl[..., R + N:]
            A = -jnp.exp(A_log[i])
            dA = jnp.exp(dt[..., None] * A)
            dBx = dt[..., None] * Bm[:, :, None, :] * xm[..., None]

            def step(h, inp):
                dA_t, dBx_t, C_t = inp
                h = dA_t * h + dBx_t
                y = jnp.einsum('ben,bn->be', h, C_t)
                return (h, y)
            h0 = jnp.zeros((B, E, N), xm.dtype)
            _, ys = jax.lax.scan(step, h0, (dA.transpose(1, 0, 2, 3), dBx.transpose(1, 0, 2, 3), Cm.transpose(1, 0, 2)))
            y = ys.transpose(1, 0, 2) + Dp[i] * xm
            y = y * jax.nn.silu(z)
            out = y @ W_out[i]
            out = u + out
            return out.reshape(B, H, W, C).transpose(0, 3, 1, 2)
        key = jax.random.key(seed)
        ks = jax.random.split(key, 8)
        p = {}
        p['x'] = jax.random.normal(ks[0], (B, C, H, W), jnp.float32)
        p['bn_gamma'] = jnp.ones((2, C), jnp.float32)
        p['bn_beta'] = jnp.zeros((2, C), jnp.float32)
        p['ln_gamma'] = jnp.ones((2, C), jnp.float32)
        p['ln_beta'] = jnp.zeros((2, C), jnp.float32)
        p['W_in'] = jax.random.normal(ks[1], (2, C, 2 * E), jnp.float32) * 0.02
        p['conv_w'] = jax.random.normal(ks[2], (2, E, K), jnp.float32) * 0.1
        p['conv_b'] = jnp.zeros((2, E), jnp.float32)
        p['W_xp'] = jax.random.normal(ks[3], (2, E, R + 2 * N), jnp.float32) * 0.02
        p['W_dt'] = jax.random.normal(ks[4], (2, R, E), jnp.float32) * 0.1
        p['b_dt'] = jax.random.uniform(ks[5], (2, E), jnp.float32, minval=-4.0, maxval=-2.0)
        p['A_log'] = jnp.broadcast_to(jnp.log(jnp.arange(1, N + 1, dtype=jnp.float32)), (2, E, N)) + jnp.zeros((2, E, N), jnp.float32)
        p['Dp'] = jnp.ones((2, E), jnp.float32)
        p['W_out'] = jax.random.normal(ks[6], (2, E, C), jnp.float32) * 0.02
        return p
    _L0_conv_all = _L0_conv_setup()
    _L0_conv_in = {k: v for k, v in _L0_conv_all.items() if k in ('bn_gamma', 'bn_beta', 'ln_gamma', 'ln_beta', 'W_in', 'conv_w', 'conv_b', 'W_xp', 'W_dt', 'b_dt', 'A_log', 'Dp', 'W_out', )}
    del _L0_conv_all

    def _L1_attn_setup():
        import jax, jax.numpy as jnp
        import numpy as np
        EMBED_DIM = 128
        GAMMA = 1.0
        B, S = (4, 4096)
        key = jax.random.key(seed)
        ks = jax.random.split(key, 6)
        return {'inputs': jax.random.normal(ks[0], (B, S, EMBED_DIM), dtype=jnp.float32), 'rotation_params': jax.random.normal(ks[1], (EMBED_DIM * EMBED_DIM,), dtype=jnp.float32), 'entangle_params': jax.random.normal(ks[2], (EMBED_DIM * EMBED_DIM,), dtype=jnp.float32), 'Wq': jax.random.normal(ks[3], (EMBED_DIM, EMBED_DIM), dtype=jnp.float32) / np.sqrt(EMBED_DIM), 'Wk': jax.random.normal(ks[4], (EMBED_DIM, EMBED_DIM), dtype=jnp.float32) / np.sqrt(EMBED_DIM), 'Wv': jax.random.normal(ks[5], (EMBED_DIM, EMBED_DIM), dtype=jnp.float32) / np.sqrt(EMBED_DIM)}
    _L1_attn_all = _L1_attn_setup()
    _L1_attn_in = {k: v for k, v in _L1_attn_all.items() if k in ('rotation_params', 'entangle_params', 'Wq', 'Wk', 'Wv', )}
    del _L1_attn_all

    def _L1_ffn_setup():
        import jax, jax.numpy as jnp
        import numpy as np
        B, N, D, C, E, K = (8, 8192, 128, 128, 8, 2)
        key = jax.random.key(seed)
        k0, k1, k2 = jax.random.split(key, 3)
        x = jax.random.normal(k0, (B, N, D), dtype=jnp.float32)
        router_w = jax.random.normal(k1, (D, E), dtype=jnp.float32) * 0.05
        router_b = jnp.zeros((E,), dtype=jnp.float32)
        expert_w = jax.random.normal(k2, (E, D, C), dtype=jnp.float32) * (1.0 / np.sqrt(D))
        expert_b = jnp.zeros((E, C), dtype=jnp.float32)
        return {'x': x, 'router_w': router_w, 'router_b': router_b, 'expert_w': expert_w, 'expert_b': expert_b}
    _L1_ffn_all = _L1_ffn_setup()
    _L1_ffn_in = {k: v for k, v in _L1_ffn_all.items() if k in ('router_w', 'router_b', 'expert_w', 'expert_b', )}
    del _L1_ffn_all

    return {
        "x": x,
        "L0_conv_bn_gamma": _L0_conv_in["bn_gamma"],
        "L0_conv_bn_beta": _L0_conv_in["bn_beta"],
        "L0_conv_ln_gamma": _L0_conv_in["ln_gamma"],
        "L0_conv_ln_beta": _L0_conv_in["ln_beta"],
        "L0_conv_W_in": _L0_conv_in["W_in"],
        "L0_conv_conv_w": _L0_conv_in["conv_w"],
        "L0_conv_conv_b": _L0_conv_in["conv_b"],
        "L0_conv_W_xp": _L0_conv_in["W_xp"],
        "L0_conv_W_dt": _L0_conv_in["W_dt"],
        "L0_conv_b_dt": _L0_conv_in["b_dt"],
        "L0_conv_A_log": _L0_conv_in["A_log"],
        "L0_conv_Dp": _L0_conv_in["Dp"],
        "L0_conv_W_out": _L0_conv_in["W_out"],
        "L1_attn_rotation_params": _L1_attn_in["rotation_params"],
        "L1_attn_entangle_params": _L1_attn_in["entangle_params"],
        "L1_attn_Wq": _L1_attn_in["Wq"],
        "L1_attn_Wk": _L1_attn_in["Wk"],
        "L1_attn_Wv": _L1_attn_in["Wv"],
        "L1_ffn_router_w": _L1_ffn_in["router_w"],
        "L1_ffn_router_b": _L1_ffn_in["router_b"],
        "L1_ffn_expert_w": _L1_ffn_in["expert_w"],
        "L1_ffn_expert_b": _L1_ffn_in["expert_b"],
    }

def reference(x, L0_conv_bn_gamma, L0_conv_bn_beta, L0_conv_ln_gamma, L0_conv_ln_beta, L0_conv_W_in, L0_conv_conv_w, L0_conv_conv_b, L0_conv_W_xp, L0_conv_W_dt, L0_conv_b_dt, L0_conv_A_log, L0_conv_Dp, L0_conv_W_out, L1_attn_rotation_params, L1_attn_entangle_params, L1_attn_Wq, L1_attn_Wk, L1_attn_Wv, L1_ffn_router_w, L1_ffn_router_b, L1_ffn_expert_w, L1_ffn_expert_b):
    import jax
    import jax.numpy as jnp
    def _L0_conv_ref(x, bn_gamma, bn_beta, ln_gamma, ln_beta, W_in, conv_w, conv_b, W_xp, W_dt, b_dt, A_log, Dp, W_out):
        import jax, jax.numpy as jnp
        import numpy as np
        B, C, H, W = (4, 128, 64, 64)
        E, N, R, K = (256, 16, 8, 4)
        L = H * W
        EPS = 1e-05
        NEG_SLOPE = 0.01

        def _stage(x, i, bn_gamma, bn_beta, ln_gamma, ln_beta, W_in, conv_w, conv_b, W_xp, W_dt, b_dt, A_log, Dp, W_out):
            mu = x.mean((0, 2, 3))
            var = x.var((0, 2, 3))
            xn = (x - mu[None, :, None, None]) * jax.lax.rsqrt(var + EPS)[None, :, None, None]
            xn = xn * bn_gamma[i][None, :, None, None] + bn_beta[i][None, :, None, None]
            xn = jax.nn.leaky_relu(xn, NEG_SLOPE)
            u = xn.transpose(0, 2, 3, 1).reshape(B, L, C)
            mu2 = u.mean(-1, keepdims=True)
            v2 = u.var(-1, keepdims=True)
            un = (u - mu2) * jax.lax.rsqrt(v2 + EPS) * ln_gamma[i] + ln_beta[i]
            xz = un @ W_in[i]
            xm, z = (xz[..., :E], xz[..., E:])
            xc = xm.transpose(0, 2, 1)
            xc = jax.lax.conv_general_dilated(xc, conv_w[i][:, None, :], (1,), [(K - 1, 0)], feature_group_count=E)
            xm = jax.nn.silu(xc.transpose(0, 2, 1) + conv_b[i])
            dbl = xm @ W_xp[i]
            dt = jax.nn.softplus(dbl[..., :R] @ W_dt[i] + b_dt[i])
            Bm = dbl[..., R:R + N]
            Cm = dbl[..., R + N:]
            A = -jnp.exp(A_log[i])
            dA = jnp.exp(dt[..., None] * A)
            dBx = dt[..., None] * Bm[:, :, None, :] * xm[..., None]

            def step(h, inp):
                dA_t, dBx_t, C_t = inp
                h = dA_t * h + dBx_t
                y = jnp.einsum('ben,bn->be', h, C_t)
                return (h, y)
            h0 = jnp.zeros((B, E, N), xm.dtype)
            _, ys = jax.lax.scan(step, h0, (dA.transpose(1, 0, 2, 3), dBx.transpose(1, 0, 2, 3), Cm.transpose(1, 0, 2)))
            y = ys.transpose(1, 0, 2) + Dp[i] * xm
            y = y * jax.nn.silu(z)
            out = y @ W_out[i]
            out = u + out
            return out.reshape(B, H, W, C).transpose(0, 3, 1, 2)
        residual = x
        out = _stage(x, 0, bn_gamma, bn_beta, ln_gamma, ln_beta, W_in, conv_w, conv_b, W_xp, W_dt, b_dt, A_log, Dp, W_out)
        out = _stage(out, 1, bn_gamma, bn_beta, ln_gamma, ln_beta, W_in, conv_w, conv_b, W_xp, W_dt, b_dt, A_log, Dp, W_out)
        return out + residual

    def _L1_attn_ref(inputs, rotation_params, entangle_params, Wq, Wk, Wv):
        import jax, jax.numpy as jnp
        import numpy as np
        EMBED_DIM = 128
        GAMMA = 1.0
        B, S = (4, 4096)
        D = EMBED_DIM
        rot = rotation_params.reshape(D, -1)
        ent = entangle_params.reshape(D, -1)
        rotated = jnp.einsum('bsd,de->bse', inputs, rot)
        entangled = jnp.einsum('bsd,de->bse', inputs, ent)
        Q = jnp.einsum('bsd,ed->bse', rotated, Wq)
        K = jnp.einsum('bsd,ed->bse', entangled, Wk)
        V = jnp.einsum('bsd,ed->bse', inputs, Wv)
        q2 = jnp.sum(Q * Q, axis=-1)
        k2 = jnp.sum(K * K, axis=-1)
        qk = jnp.einsum('bqd,bkd->bqk', Q, K)
        dist2 = q2[:, :, None] + k2[:, None, :] - 2.0 * qk
        scores = jnp.exp(-GAMMA * dist2)
        attn = jax.nn.softmax(scores, axis=-1)
        return jnp.einsum('bqk,bkd->bqd', attn, V)

    def _L1_ffn_ref(x, router_w, router_b, expert_w, expert_b):
        import jax, jax.numpy as jnp
        import numpy as np
        B, N, D, C, E, K = (8, 8192, 128, 128, 8, 2)
        router_probs = jax.nn.softmax(x @ router_w + router_b, axis=-1)
        top_p, top_i = jax.lax.top_k(router_probs, K)
        top_p = top_p / jnp.sum(top_p, axis=-1, keepdims=True)
        expert_out = jnp.einsum('bnd,edc->bnec', x, expert_w) + expert_b
        gathered = jnp.take_along_axis(expert_out, top_i[..., None], axis=2)
        return jnp.einsum('bnk,bnkc->bnc', top_p, gathered)

    def _gn(v, G=32, eps=1e-5):
        B_, C_, H_, W_ = v.shape
        g = v.reshape(B_, G, C_ // G, H_, W_)
        m = jnp.mean(g, axis=(2, 3, 4), keepdims=True)
        s = jnp.var(g, axis=(2, 3, 4), keepdims=True)
        return ((g - m) / jnp.sqrt(s + eps)).reshape(v.shape)

    def _ln_c(v, eps=1e-6):
        m = jnp.mean(v, axis=1, keepdims=True)
        s = jnp.var(v, axis=1, keepdims=True)
        return (v - m) / jnp.sqrt(s + eps)

    def _ln_t(v, eps=1e-5):
        m = jnp.mean(v, axis=-1, keepdims=True)
        s = jnp.var(v, axis=-1, keepdims=True)
        return (v - m) / jnp.sqrt(s + eps)

    def _to_tokens(v):
        B_, C_, H_, W_ = v.shape
        return v.reshape(B_, C_, H_ * W_).transpose(0, 2, 1)
    def _from_tokens(t, like):
        B_, C_, H_, W_ = like.shape
        return t.transpose(0, 2, 1).reshape(B_, C_, H_, W_)

    x = _L0_conv_ref(x, L0_conv_bn_gamma, L0_conv_bn_beta, L0_conv_ln_gamma, L0_conv_ln_beta, L0_conv_W_in, L0_conv_conv_w, L0_conv_conv_b, L0_conv_W_xp, L0_conv_W_dt, L0_conv_b_dt, L0_conv_A_log, L0_conv_Dp, L0_conv_W_out)
    t = _to_tokens(x)
    t = t + _L1_attn_ref(_ln_t(t), L1_attn_rotation_params, L1_attn_entangle_params, L1_attn_Wq, L1_attn_Wk, L1_attn_Wv)
    t = t + _L1_ffn_ref(_ln_t(t), L1_ffn_router_w, L1_ffn_router_b, L1_ffn_expert_w, L1_ffn_expert_b)
    x = _from_tokens(t, x)
    return x


_drawn_inputs = setup_inputs


def setup_inputs(seed=0):
    import zlib

    import numpy as np

    out = dict(_drawn_inputs(seed))
    spreads = {'L0_conv_bn_gamma': (1.0, 0.2),
     'L0_conv_bn_beta': (0.0, 0.1),
     'L0_conv_ln_gamma': (1.0, 0.6),
     'L0_conv_ln_beta': (0.0, 0.8),
     'L0_conv_conv_b': (0.0, 0.618),
     'L0_conv_Dp': (1.0, 0.6),
     'L1_ffn_router_b': (0.0, 2.0),
     'L1_ffn_expert_b': (0.0, 2.0)}
    factors = {'L0_conv_W_in': 4.919,
     'L0_conv_conv_w': 6.689,
     'L0_conv_W_xp': 8.0,
     'L0_conv_W_dt': 8.0,
     'L0_conv_b_dt': 8.0,
     'L0_conv_A_log': 8.0,
     'L0_conv_W_out': 4.322,
     'L1_attn_Wv': 39.463,
     'L1_ffn_router_w': 8.0,
     'L1_ffn_expert_w': 8.0}
    for name, (base, spread) in spreads.items():
        noise = np.random.default_rng([zlib.crc32(name.encode()), seed]).standard_normal(out[name].shape)
        drawn = base * np.exp(spread * noise) if base else spread * noise
        out[name] = jnp.asarray(drawn.astype(out[name].dtype))
    for name, factor in factors.items():
        out[name] = (out[name] * factor).astype(out[name].dtype)
    return out
```

```python
from contextlib import ExitStack

import concourse.bass as bass
from concourse import mybir

ALU = mybir.AluOpType
ACT = mybir.ActivationFunctionType
AX_X = mybir.AxisListType.X
F32 = mybir.dt.float32
BF16 = mybir.dt.bfloat16

P = 128
CH = 512
TABLES = "natural_log_exp_and_others"
SLOPE = 0.01
EPS = 1e-5
RING = 8
HRING = 4
CRING = 4
OPEN = 1
ATANH = (1.99999967, 0.66676006, 0.39589371, 0.34226697)


def hybrid_kernel(nc, x, bn_gamma, bn_beta, ln_gamma, ln_beta, W_in, conv_w, conv_b, W_xp, W_dt, b_dt, A_log, Dp,
                  W_out, rotation, entangle, Wq, Wk, Wv, router_w, router_b, expert_w, expert_b, out):
    NB, C, HH, WW = x.shape
    L = HH * WW
    LAYERS, _, E2 = W_in.shape
    E = E2 // 2
    TAPS = conv_w.shape[2]
    R = W_dt.shape[1]
    N = A_log.shape[2]
    NX = router_w.shape[1]
    HALVES = E // P
    NJ = L // CH
    NCH = NB * NJ
    KT = L // P
    SUB = CH // P
    BC = 2 * N
    PARTS = 3
    ROWS = PARTS * BC
    PAIRS = N * HALVES
    GROUP = RING // HALVES
    HIST = TAPS - 1
    FIN = NCH + 1
    assert C == P and HALVES == 2 and ROWS == 96 and NCH % 2 == 0

    x_in = x.rearrange("b c h w -> c b (h w)")
    out_v = out.rearrange("b c h w -> c b (h w)")

    with ExitStack() as ctx:
        def sb(name, shape, dt=F32):
            return ctx.enter_context(nc.sbuf_tensor(name, shape, dt))

        def sem(name):
            return ctx.enter_context(nc.semaphore(name))

        bank = [ctx.enter_context(nc.psum_tensor(f"bank{i}", [P, CH], F32)) for i in range(8)]

        X = sb("X", [P, (NCH + 1) * CH])
        ident = sb("ident", [P, P])
        identb = sb("identb", [P, P], BF16)
        mean_w = sb("mean_w", [P, P])
        ones = sb("ones", [P, P])
        onesb = sb("onesb", [PARTS, P], BF16)
        cols = sb("cols", [P, 8])
        eps_c, one_c, negone_c, two_c, atanh2_c = (cols[:, i:i + 1] for i in range(5))
        neghalf_c = cols[:, 5:8]

        zeros, consts = sem("zeros"), sem("consts")
        x_loaded = [sem(f"x_loaded{b}") for b in range(NB)]
        names = """weights_loaded folded d_diag a_exp a_ready nb_ready bn_stat bn_agg bn_lnv bn_rstd
            bn_part bn_ready aff_done u_ready mean_ready d_ready sq_ready var_ready lnv_ready rstd_ready dn_ready
            carry_ready un_ready z_ready0 z_ready1 ze0 ze1 zl0 zl1 zg0 zg1 zs_ready0 zs_ready1 cv_ready0 cv_ready1
            ce0 ce1 cl0 cl1 cg0 cg1 xm_ready0 xm_ready1 dbl_ready s_hi s_r1 s_mid s_r2 s_ready r_ready
            dp_ready0 dp_ready1 sa0 sa1 sr0 sr1 sz0 sz1 sl0 sl1 sw0 sw1 ss0 ss1 sq0 sq1 sp0 sp1 sm0 sm1 sn0 sn1
            so0 so1 dt_ready0 dt_ready1 dtx_ready0 dtx_ready1 b_ready c_ready c_copied u_done h_done da_ready hc_done
            sum_done skip_done kept hinit_done y_done out_ready resid_done
            w_att w_tr w_trc w_mm xr_loaded
            a_x a_mean a_d a_sq a_var a_ln a_rs a_xn a_q a_k a_v a_qc a_qs a_kc a_ks a_vc a_k2 a_q2 a_k2c
            a_split qk_ready e1_done p_ready pv_done acc_done den_ready rec_done o_done att_done
            f_mean f_d f_sq f_var f_ln f_rs f_xn f_log f_ch f_exp f_chain f_g3 f_tr f_trf f_gt f_gtf f_rep f_gx f_mm
            f_out stored w_cst""".split()
        S = {n: sem(n) for n in names}

        def chunk(q, n=1):
            return X[:, bass.ds((q + 1) * CH, n * CH)]

        stage_memory = ExitStack()

        def sbs(name, shape, dt=F32):
            return stage_memory.enter_context(nc.sbuf_tensor(name, shape, dt))

        decay = sbs("decay", [P, RING, CH])
        state = sbs("state", [P, RING, CH])
        hc = sbs("hc", [P, HRING, CH])
        csb = sbs("csb", [P, CRING, CH])
        dt_s = sbs("dt_s", [P, 2, HALVES, CH])
        dtx = sbs("dtx", [P, 2, HALVES, CH])
        xm = sbs("xm", [P, HALVES, CH])
        zs = sbs("zs", [P, 2, HALVES, CH])
        yg = sbs("yg", [P, HALVES, CH])
        bc3 = sbs("bc3", [ROWS, 2, CH], BF16)
        un = sbs("un", [P, HIST + CH])
        D, L1, L2, L3 = (sbs(f"ln{i}", [P, CH]) for i in range(4))
        G1, G2 = (sbs(f"sig{i}", [P, CH]) for i in range(2))
        sg = sbs("sg", [P, HALVES, CH])
        rrow = sbs("rrow", [P, CH])
        rest = rrow[0:2 * BC, :]
        pa, pz, pw, ps, pq, pp = (sbs(f"sp_{n}", [P, CH]) for n in "azwsqp")
        pr = sbs("sp_r", [P, HALVES, CH])
        sel = sbs("sel", [ROWS, BC, P], BF16)
        D_diag = sbs("D_diag", [P, HALVES, P])
        first = sbs("first", [P, NCH])
        w_z = sbs("w_z", [P, E2])
        cw_rows = decay[:, 0:E * TAPS // CH, :].rearrange("p a c -> p (a c)")
        w_cv = sbs("w_cv", [P, TAPS, E])
        w_xp = sbs("w_xp", [P, HALVES, ROWS + R])
        w_dt = sbs("w_dt", [P, E])
        w_out = sbs("w_out", [P, HALVES, C])
        vec = sbs("vec", [P, 4])
        evec = sbs("evec", [P, 4, HALVES])
        A_s = sbs("A_s", [P, HALVES, N])
        Aexp = sbs("Aexp", [P, HALVES, N])
        stats = sbs("stats", [P, NCH, 6])
        bn = sbs("bn", [P, 8])
        kept = sbs("kept", [P, PAIRS])
        hinit = sbs("hinit", [P, PAIRS])

        conv_b_c = [evec[:, 0, h:h + 1] for h in range(HALVES)]
        dt_b_c = [evec[:, 1, h:h + 1] for h in range(HALVES)]
        D_c = [evec[:, 2, h:h + 1] for h in range(HALVES)]
        nconv_b_c = [evec[:, 3, h:h + 1] for h in range(HALVES)]
        bn_mean, bn_var, bn_ln, bn_rs, bn_scale, bn_ms, bn_shift = (bn[:, i:i + 1] for i in range(7))

        psum_y = bank[0:2]
        psum_b = bank[2:4]
        psum_u = bank[4]
        psum_c = bank[5]
        bank_a, bank_b = bank[6], bank[7]

        with nc.Block() as block:
            @block.sync
            def _(sp):
                for b in range(NB):
                    sp.dma_start(X[:, (1 + b * NJ) * CH:(1 + (b + 1) * NJ) * CH], x_in[:, b, :]).then_inc(x_loaded[b], 16)
                for n in names:
                    sp.sem_inc(S[n], OPEN)

            @block.gpsimd
            def _(pool):
                pool.memset(ident[:, :], 0.0).then_inc(zeros, 1)
                pool.memset(identb[:, :], 0.0).then_inc(zeros, 1)
                pool.memset(sel[:, :, :], 0.0).then_inc(zeros, 1)
                pool.wait_ge(zeros, 3)
                for m in (ident, identb):
                    pool.affine_select(out=m[:, :], in_=m[:, :], compare_op=ALU.not_equal, fill=1.0, base=0,
                                       pattern=[[-1, P]], channel_multiplier=1).then_inc(zeros, 1)
                pool.wait_ge(zeros, 5)
                for k in range(PARTS):
                    pool.affine_select(out=sel[:, :, :], in_=sel[:, :, :], compare_op=ALU.not_equal, fill=1.0,
                                       base=-BC * k, pattern=[[-1, BC], [0, P]],
                                       channel_multiplier=1).then_inc(zeros, 1)
                    pool.wait_ge(zeros, 6 + k)

            @block.vector
            def _(dve):
                dve.memset(mean_w[:, :], 1.0 / C)
                dve.memset(ones[:, :], 1.0)
                dve.memset(onesb[:, :], 1.0)
                dve.memset(eps_c, EPS)
                dve.memset(one_c, 1.0)
                dve.memset(negone_c, -1.0)
                dve.memset(two_c, 2.0)
                dve.memset(atanh2_c, ATANH[2])
                dve.memset(neghalf_c, -0.5)
                dve.memset(first[:, :], 1.0).then_inc(consts, 1)
                dve.wait_ge(consts, 1)
                dve.memset(first[:, :].rearrange("p (b j) -> p b j", j=NJ)[:, :, 0:1], 0.0)
                dve.memset(X[:, 0:CH], 0.0)
                dve.memset(un[:, :], 0.0)
                dve.memset(kept[:, :], 0.0)
                for h in range(HALVES):
                    dve.memset(psum_y[h][:, :], 0.0)
                    dve.memset(zs[:, 1, h, :], 0.0)
                dve.sem_inc(S["h_done"], RING)
                dve.sem_inc(S["hc_done"], RING)
                dve.sem_inc(S["sum_done"], HRING)

            @block.scalar
            def _(act):
                act.preload_act_table_set(TABLES)

        with nc.Block() as block:

            @block.sync
            def _(sp):
                with sp.Fori(0, LAYERS) as s:
                    sp.wait_ge(S["resid_done"], OPEN + s * FIN)
                    w = S["weights_loaded"]

                    def of(a, pattern, **kw):
                        return a[bass.ds(s, 1)].rearrange(pattern, **kw)
                    for i, a in enumerate((bn_gamma, bn_beta, ln_gamma, ln_beta)):
                        sp.dma_start(vec[:, i:i + 1], of(a, "a c -> c a")).then_inc(w, 16)
                    sp.dma_start(w_z[:, :], of(W_in, "a c e -> (a c) e")).then_inc(w, 16)
                    sp.dma_start(cw_rows, of(conv_w, "a e k -> a (e k)").to_broadcast([P, E * TAPS])).then_inc(w, 16)
                    for i, a in enumerate((conv_b, b_dt, Dp)):
                        sp.dma_start(evec[:, i, :], of(a, "a (h p) -> (a p) h", p=P),
                                     allow_slow_non_contiguous=True).then_inc(w, 16)
                    for k in range(PARTS):
                        sp.dma_start(w_xp[:, :, k * BC:(k + 1) * BC],
                                     of(W_xp, "a (h p) r -> (a p) h r", p=P)[:, :, R:R + BC]).then_inc(w, 16)
                    sp.dma_start(w_xp[:, :, ROWS:ROWS + R],
                                 of(W_xp, "a (h p) r -> (a p) h r", p=P)[:, :, 0:R]).then_inc(w, 16)
                    sp.dma_start(w_dt[ROWS:ROWS + R, :], of(W_dt, "a r e -> (a r) e")).then_inc(w, 16)
                    sp.dma_start(A_s[:, :, :], of(A_log, "a (h p) n -> (a p) h n", p=P)).then_inc(w, 16)
                    sp.dma_start(w_out[:, :, :], of(W_out, "a (h p) c -> (a p) h c", p=P)).then_inc(w, 16)
            NW = 4 + 1 + 1 + 3 + PARTS + 1 + 1 + 1 + 1

            @block.tensor
            def _(pe):
                mm = pe.matmul

                def mean(tp, q):
                    pe.wait_ge(S["u_ready"], OPEN + tp + 1)
                    mm(bank_a[:, :], mean_w[:, :], chunk(q), start=True, stop=True).then_inc(S["mean_ready"], 1)

                def var(tp):
                    pe.wait_ge(S["sq_ready"], OPEN + tp + 1)
                    mm(bank_b[:, :], mean_w[:, :], L1[:, :], start=True, stop=True).then_inc(S["var_ready"], 1)

                def gate(tp, h):
                    pe.wait_ge(S["un_ready"], OPEN + tp + 1)
                    mm((bank_a, bank_b)[h][:, :], w_z[:, E + h * P:E + (h + 1) * P], un[:, HIST:HIST + CH],
                       start=True, stop=True).then_inc(S[f"z_ready{h}"], 1)

                def conv(tp, h, fin):
                    pe.wait_ge(S[f"zs_ready{1 - h}"], OPEN + tp + 1)
                    if h == 1:
                        pe.wait_ge(S["resid_done"], OPEN + fin)
                    for k in range(TAPS):
                        last = mm((bank_b, bank_a)[h][:, :], w_cv[:, k, h * P:(h + 1) * P], un[:, k:k + CH],
                                  start=k == 0, stop=k == TAPS - 1)
                    last.then_inc(S[f"cv_ready{h}"], 1)

                def dbl(tp):
                    pe.wait_ge(S["xm_ready0"], OPEN + tp + 1)
                    pe.wait_ge(S["xm_ready1"], OPEN + tp + 1)
                    for h in range(HALVES):
                        last = mm(bank_b[0:ROWS + R, :], w_xp[:, h, :], xm[:, h, :],
                                  start=h == 0, stop=h == HALVES - 1)
                    last.then_inc(S["dbl_ready"], 1)

                def step(tp, h):
                    pe.wait_ge(S["r_ready"], OPEN + tp + 1)
                    if h == 1:
                        pe.wait_ge(S["s_r1"], OPEN + tp + 1)
                    mm((bank_a, bank_b)[h][:, :], w_dt[ROWS:ROWS + R, h * P:(h + 1) * P], rrow[ROWS:ROWS + R, :],
                       start=True, stop=True).then_inc(S[f"dp_ready{h}"], 1)

                def finish(fin):
                    pe.wait_ge(S["y_done"], OPEN + fin * HALVES)
                    for h in range(HALVES):
                        last = mm(bank_a[:, :], w_out[:, h, :], yg[:, h, :],
                                  start=h == 0, stop=h == HALVES - 1)
                    last.then_inc(S["out_ready"], 1)

                def spread(t, n, par):
                    if n == 0:
                        pe.wait_ge(S["s_ready"], OPEN + t + 1)
                    pe.wait_ge(S["h_done"], OPEN + RING + t * PAIRS + 2 * n - 2)
                    mm(psum_b[n % 2][:, :], sel[:, n, :], bc3[:, par, :], start=True, stop=True).then_inc(S["b_ready"], 1)
                    pe.wait_ge(S["c_copied"], OPEN + t * N + n)
                    mm(psum_c[:, :], sel[:, N + n, :], bc3[:, par, :], start=True, stop=True).then_inc(S["c_ready"], 1)

                def skip(fin):
                    pe.wait_ge(S["y_done"], OPEN + fin * HALVES)
                    for h in range(HALVES):
                        mm(psum_y[h][:, :], D_diag[:, h, :], xm[:, h, :], start=True,
                           stop=False).then_inc(S["skip_done"], 1)

                def gather(t, n):
                    for h in range(HALVES):
                        k = 2 * n + h
                        pe.wait_ge(S["hc_done"], OPEN + RING + t * PAIRS + k + 1)
                        mm(psum_y[h][:, :], ident[:, :], hc[:, k % HRING, :], start=False,
                           stop=n == N - 1).then_inc(S["sum_done"], 1)

                def ssm(s, q, par, mid, norm):
                    t = s * NCH + q
                    fin = s * FIN + q + 1
                    for n in range(N):
                        if n + 1 < N:
                            spread(t, n + 1, par)
                        elif mid:
                            spread(t + 1, 0, 1 - par)
                        if n == 1:
                            skip(fin)
                        if n >= 1:
                            gather(t, n - 1)
                        if mid:
                            if n == 0:
                                gate(t + 1, 0)
                                gate(t + 1, 1)
                            if n == 4:
                                conv(t + 1, 0, fin)
                            if n == 6:
                                conv(t + 1, 1, fin)
                            if n == 8:
                                dbl(t + 1)
                            if n in (9, 10):
                                step(t + 1, n - 9)
                        if n == 3:
                            if mid:
                                pe.wait_ge(S["zs_ready0"], OPEN + t + 2)
                            finish(fin)
                        if norm:
                            if n == 12:
                                pe.wait_ge(S["sr0"], OPEN + t + 2)
                                mean(t + 2, q + 2)
                            if n == 13:
                                pe.wait_ge(S["sr1"], OPEN + t + 2)
                                var(t + 2)
                    gather(t, N - 1)

                with pe.Fori(0, LAYERS) as s:
                    pe.wait_ge(S["weights_loaded"], OPEN + (s + 1) * 16 * NW)
                    pe.wait_ge(S["folded"], OPEN + (s + 1) * TAPS)
                    pe.wait_ge(S["d_diag"], OPEN + (s + 1) * HALVES)
                    t0 = s * NCH
                    mean(t0, 0)
                    var(t0)
                    for h in range(HALVES):
                        gate(t0, h)
                    for h in range(HALVES):
                        conv(t0, h, s * FIN)
                    dbl(t0)
                    for h in range(HALVES):
                        step(t0, h)
                    pe.wait_ge(S["sr0"], OPEN + t0 + 1)
                    mean(t0 + 1, 1)
                    pe.wait_ge(S["sr1"], OPEN + t0 + 1)
                    var(t0 + 1)
                    spread(t0, 0, 0)
                    with pe.Fori(0, NCH // 2 - 1) as pair:
                        for par in range(2):
                            ssm(s, 2 * pair + par, par, True, True)
                    ssm(s, NCH - 2, 0, True, False)
                    pe.wait_ge(S["sr0"], OPEN + t0 + NCH)
                    pe.wait_ge(S["resid_done"], OPEN + s * FIN + NCH - 1)
                    ssm(s, NCH - 1, 1, False, False)
                    pe.wait_ge(S["resid_done"], OPEN + s * FIN + NCH)
                    finish(s * FIN + FIN)

            @block.scalar
            def _(act):
                go = act.activation

                def affine(tp, q):
                    go(chunk(q), chunk(q), ACT.Identity, bias=bn_shift, scale=bn_scale).then_inc(S["aff_done"], 1)

                def square(tp):
                    act.wait_ge(S["d_ready"], OPEN + tp + 1)
                    act.wait_ge(S["var_ready"], OPEN + tp)
                    go(L1[:, :], D[:, :], ACT.Square).then_inc(S["sq_ready"], 1)

                def rstd(tp):
                    act.wait_ge(S["var_ready"], OPEN + tp + 1)
                    go(L2[:, :], bank_b[:, :], ACT.Ln, bias=eps_c).then_inc(S["lnv_ready"], 1)
                    act.wait_ge(S["lnv_ready"], OPEN + tp + 1)
                    act.wait_ge(S["dn_ready"], OPEN + tp)
                    go(L3[:, :], L2[:, :], ACT.Exp, scale=-0.5).then_inc(S["rstd_ready"], 1)

                def normed(tp):
                    act.wait_ge(S["dn_ready"], OPEN + tp + 1)
                    act.wait_ge(S["carry_ready"], OPEN + tp + 1)
                    go(un[:, HIST:HIST + CH], D[:, :], ACT.Identity, bias=vec[:, 3:4],
                       scale=vec[:, 2:3]).then_inc(S["un_ready"], 1)

                def sigmoid(tp, src, h, ready, e, l, g, bias):
                    act.wait_ge(S[ready], OPEN + tp + 1)
                    if bias is None:
                        go(G1[:, :], src[:, :], ACT.Exp, scale=-1.0).then_inc(S[e], 1)
                    else:
                        go(G1[:, :], src[:, :], ACT.Exp, bias=bias, scale=-1.0).then_inc(S[e], 1)
                    act.wait_ge(S[e], OPEN + tp + 1)
                    go(G2[:, :], G1[:, :], ACT.Ln, bias=one_c).then_inc(S[l], 1)
                    act.wait_ge(S[l], OPEN + tp + 1)
                    go(sg[:, h, :], G2[:, :], ACT.Exp, scale=-1.0).then_inc(S[g], 1)

                def z_sigmoid(tp, h):
                    act.wait_ge(S[f"xm_ready{h}"], OPEN + tp)
                    act.wait_ge(S["zg0" if h else "cg1"], OPEN + tp + h)
                    sigmoid(tp, (bank_a, bank_b)[h], h, f"z_ready{h}", f"ze{h}", f"zl{h}", f"zg{h}", None)

                def x_sigmoid(tp, h):
                    act.wait_ge(S[f"zs_ready{h}"], OPEN + tp + 1)
                    act.wait_ge(S["cg0" if h else "zg1"], OPEN + tp + 1)
                    sigmoid(tp, (bank_b, bank_a)[h], h, f"cv_ready{h}", f"ce{h}", f"cl{h}", f"cg{h}", nconv_b_c[h])

                def rows(tp):
                    act.wait_ge(S["dbl_ready"], OPEN + tp + 1)
                    act.wait_ge(S["dp_ready1"], OPEN + tp)
                    act.copy(rrow[ROWS:ROWS + R, :], bank_b[ROWS:ROWS + R, :]).then_inc(S["r_ready"], 1)

                def softplus(tp, h):
                    act.wait_ge(S[f"dp_ready{h}"], OPEN + tp + 1)
                    act.wait_ge(S[f"sw{1 - h}"], OPEN + tp + h)
                    src = (bank_a, bank_b)[h]
                    go(pa[:, :], src[:, :], ACT.Abs, bias=dt_b_c[h]).then_inc(S[f"sa{h}"], 1)
                    act.wait_ge(S[f"dt_ready{h}"], OPEN + tp)
                    go(pr[:, h, :], src[:, :], ACT.Relu, bias=dt_b_c[h]).then_inc(S[f"sr{h}"], 1)
                    act.wait_ge(S[f"sa{h}"], OPEN + tp + 1)
                    act.wait_ge(S[f"ss{1 - h}"], OPEN + tp + h)
                    go(pz[:, :], pa[:, :], ACT.Exp, scale=-1.0).then_inc(S[f"sz{h}"], 1)
                    act.wait_ge(S[f"sz{h}"], OPEN + tp + 1)
                    go(pa[:, :], pz[:, :], ACT.Ln, bias=two_c).then_inc(S[f"sl{h}"], 1)
                    act.wait_ge(S[f"sl{h}"], OPEN + tp + 1)
                    go(pw[:, :], pa[:, :], ACT.Exp, scale=-1.0).then_inc(S[f"sw{h}"], 1)

                def series(tp, h):
                    act.wait_ge(S[f"ss{h}"], OPEN + tp + 1)
                    act.wait_ge(S[f"dt_ready{1 - h}"], OPEN + tp + h)
                    go(pq[:, :], ps[:, :], ACT.Square).then_inc(S[f"sq{h}"], 1)
                    act.wait_ge(S[f"sq{h}"], OPEN + tp + 1)
                    go(pp[:, :], pq[:, :], ACT.Identity, bias=atanh2_c, scale=ATANH[3]).then_inc(S[f"sp{h}"], 1)

                def decays(t, n, par):
                    if n == 0:
                        act.wait_ge(S["dt_ready0"], OPEN + t + 1)
                        act.wait_ge(S["dt_ready1"], OPEN + t + 1)
                    for h in range(HALVES):
                        k = 2 * n + h
                        act.wait_ge(S["h_done"], OPEN + t * PAIRS + k + 1)
                        go(decay[:, k % RING, :], dt_s[:, par, h, :], ACT.Exp,
                           scale=A_s[:, h, n:n + 1]).then_inc(S["da_ready"], 1)

                def c_copy(t, n):
                    act.wait_ge(S["c_ready"], OPEN + t * N + n + 1)
                    act.wait_ge(S["hc_done"], OPEN + RING + t * PAIRS + 2 * (n - CRING + 1))
                    act.copy(csb[:, n % CRING, :], psum_c[:, :]).then_inc(S["c_copied"], 1)

                def ssm(s, q, par, mid, norm):
                    t = s * NCH + q
                    for n in range(N):
                        decays(t, n, par)
                        c_copy(t, n)
                        if mid:
                            if n in (1, 2):
                                z_sigmoid(t + 1, n - 1)
                            if n in (5, 7):
                                x_sigmoid(t + 1, (n - 5) // 2)
                            if n == 9:
                                rows(t + 1)
                            if n in (10, 11):
                                softplus(t + 1, n - 10)
                            if n in (12, 14):
                                series(t + 1, (n - 12) // 2)
                        if norm:
                            if n == 10:
                                affine(t + 2, q + 2)
                            if n == 12:
                                square(t + 2)
                            if n == 14:
                                rstd(t + 2)
                            if n == 15:
                                normed(t + 2)

                with act.Fori(0, LAYERS) as s:
                    t0 = s * NCH
                    act.wait_ge(S["weights_loaded"], OPEN + (s + 1) * 16 * NW)
                    go(Aexp[:, :, :], A_s[:, :, :], ACT.Exp).then_inc(S["a_exp"], 1)
                    act.wait_ge(S["a_exp"], OPEN + s + 1)
                    act.mul(A_s[:, :, :], Aexp[:, :, :], -1.0).then_inc(S["a_ready"], 1)
                    act.mul(evec[:, 3, :], evec[:, 0, :], -1.0).then_inc(S["nb_ready"], 1)
                    act.wait_ge(S["bn_agg"], OPEN + s + 1)
                    go(bn_ln, bn_var, ACT.Ln, bias=eps_c).then_inc(S["bn_lnv"], 1)
                    act.wait_ge(S["bn_lnv"], OPEN + s + 1)
                    go(bn_rs, bn_ln, ACT.Exp, scale=-0.5).then_inc(S["bn_rstd"], 1)
                    act.wait_ge(S["bn_ready"], OPEN + s + 1)
                    act.wait_ge(S["a_ready"], OPEN + s + 1)
                    act.wait_ge(S["nb_ready"], OPEN + s + 1)
                    affine(t0, 0)
                    affine(t0 + 1, 1)
                    square(t0)
                    rstd(t0)
                    normed(t0)
                    for h in range(HALVES):
                        z_sigmoid(t0, h)
                    for h in range(HALVES):
                        x_sigmoid(t0, h)
                    rows(t0)
                    for h in range(HALVES):
                        softplus(t0, h)
                        series(t0, h)
                    square(t0 + 1)
                    rstd(t0 + 1)
                    normed(t0 + 1)
                    with act.Fori(0, NCH // 2 - 1) as pair:
                        for par in range(2):
                            ssm(s, 2 * pair + par, par, True, True)
                    ssm(s, NCH - 2, 0, True, False)
                    ssm(s, NCH - 1, 1, False, False)

            @block.vector
            def _(dve):
                def leaky(tp, q):
                    dve.wait_ge(S["aff_done"], OPEN + tp + 1)
                    dve.scalar_tensor_tensor(out=chunk(q), in0=chunk(q), scalar=SLOPE, in1=chunk(q), op0=ALU.mult,
                                             op1=ALU.max).then_inc(S["u_ready"], 1)

                def centre(tp, q):
                    dve.wait_ge(S["mean_ready"], OPEN + tp + 1)
                    dve.wait_ge(S["un_ready"], OPEN + tp)
                    dve.tensor_tensor(D[:, :], chunk(q), bank_a[:, :], ALU.subtract).then_inc(S["d_ready"], 1)

                def carry(tp, q):
                    dve.wait_ge(S["cv_ready1"], OPEN + tp)
                    dve.tensor_scalar(un[:, 0:HIST], un[:, CH:CH + HIST], first[:, bass.ds(q, 1)], None,
                                      ALU.mult).then_inc(S["carry_ready"], 1)

                def gate(tp, h, par):
                    dve.wait_ge(S[f"zg{h}"], OPEN + tp + 1)
                    dve.tensor_tensor(zs[:, par, h, :], sg[:, h, :], (bank_a, bank_b)[h][:, :],
                                      ALU.mult).then_inc(S[f"zs_ready{h}"], 1)

                def silu(tp, h):
                    dve.wait_ge(S[f"cg{h}"], OPEN + tp + 1)
                    dve.wait_ge(S["skip_done"], OPEN + tp * HALVES)
                    dve.wait_ge(S[f"dtx_ready{h}"], OPEN + tp)
                    dve.scalar_tensor_tensor(out=xm[:, h, :], in0=(bank_b, bank_a)[h][:, :], scalar=conv_b_c[h],
                                             in1=sg[:, h, :], op0=ALU.add, op1=ALU.mult).then_inc(S[f"xm_ready{h}"], 1)

                def split(tp, par):
                    dve.wait_ge(S["dbl_ready"], OPEN + tp + 1)
                    p = bc3[:, par, :]
                    dve.tensor_copy(p, bank_b[0:ROWS, :]).then_inc(S["s_hi"], 1)
                    dve.wait_ge(S["s_hi"], OPEN + tp + 1)
                    dve.tensor_tensor(rest, bank_b[0:2 * BC, :], p[0:2 * BC, :], ALU.subtract).then_inc(S["s_r1"], 1)
                    dve.wait_ge(S["s_r1"], OPEN + tp + 1)
                    dve.tensor_copy(p[0:2 * BC, :], rest).then_inc(S["s_mid"], 1)
                    dve.wait_ge(S["s_mid"], OPEN + tp + 1)
                    dve.tensor_tensor(rest[0:BC, :], rest[0:BC, :], p[0:BC, :], ALU.subtract).then_inc(S["s_r2"], 1)
                    dve.wait_ge(S["s_r2"], OPEN + tp + 1)
                    dve.tensor_copy(p[0:BC, :], rest[0:BC, :]).then_inc(S["s_ready"], 1)

                def series(tp, h):
                    dve.wait_ge(S[f"sm{h}"], OPEN + tp + 1)
                    dve.scalar_tensor_tensor(out=pp[:, :], in0=pp[:, :], scalar=ATANH[1], in1=pq[:, :], op0=ALU.add,
                                             op1=ALU.mult).then_inc(S[f"sn{h}"], 1)
                    dve.wait_ge(S[f"sn{h}"], OPEN + tp + 1)
                    dve.scalar_tensor_tensor(out=pp[:, :], in0=pp[:, :], scalar=ATANH[0], in1=ps[:, :], op0=ALU.add,
                                             op1=ALU.mult).then_inc(S[f"so{h}"], 1)

                def inputs(t, n, par):
                    dve.wait_ge(S["b_ready"], OPEN + t * N + n + 1)
                    if n == 0:
                        dve.wait_ge(S["dtx_ready0"], OPEN + t + 1)
                        dve.wait_ge(S["dtx_ready1"], OPEN + t + 1)
                    dve.wait_ge(S["h_done"], OPEN + RING + t * PAIRS + 2 * n - 1)
                    for h in range(HALVES):
                        dve.tensor_tensor((psum_u, psum_b[n % 2])[h][:, :], dtx[:, par, h, :], psum_b[n % 2][:, :],
                                          ALU.mult).then_inc(S["u_done"], 1)

                def scans(t, n):
                    for h in range(HALVES):
                        k = 2 * n + h
                        dve.wait_ge(S["da_ready"], OPEN + t * PAIRS + k + 1)
                        dve.wait_ge(S["u_done"], OPEN + t * PAIRS + k + 1)
                        dve.wait_ge(S["hc_done"], OPEN + t * PAIRS + k + 1)
                        dve.tensor_tensor_scan(state[:, k % RING, :], decay[:, k % RING, :],
                                               (psum_u, psum_b[n % 2])[h][:, :], hinit[:, k:k + 1], ALU.mult,
                                               ALU.add).then_inc(S["h_done"], 1)

                def keep(t, n):
                    g = n // GROUP
                    dve.wait_ge(S["h_done"], OPEN + RING + t * PAIRS + (g + 1) * RING)
                    dve.tensor_copy(kept[:, g * RING:(g + 1) * RING], state[:, :, CH - 1]).then_inc(S["kept"], 1)

                def start(t, q):
                    dve.wait_ge(S["kept"], OPEN + t * (N // GROUP))
                    dve.tensor_scalar(hinit[:, :], kept[:, :], first[:, bass.ds(q, 1)], None,
                                      ALU.mult).then_inc(S["hinit_done"], 1)
                    dve.wait_ge(S["hinit_done"], OPEN + t + 1)

                def gated(fin, t, par):
                    dve.wait_ge(S["sum_done"], OPEN + HRING + t * PAIRS)
                    dve.wait_ge(S["out_ready"], OPEN + fin - 1)
                    for h in range(HALVES):
                        dve.tensor_tensor(yg[:, h, :], zs[:, par, h, :], psum_y[h][:, :],
                                          ALU.mult).then_inc(S["y_done"], 1)

                def residual(fin, q):
                    dve.wait_ge(S["out_ready"], OPEN + fin)
                    dve.tensor_tensor(chunk(q), chunk(q), bank_a[:, :], ALU.add).then_inc(S["resid_done"], 1)

                def ssm(s, q, par, mid, norm):
                    t = s * NCH + q
                    fin = s * FIN + q + 1
                    start(t, q)
                    for n in range(N):
                        inputs(t, n, par)
                        if n == 1:
                            gated(fin, t, 1 - par)
                        scans(t, n)
                        if n % GROUP == GROUP - 1:
                            keep(t, n)
                        if n == 3:
                            residual(fin, q - 1)
                        if mid:
                            if n in (2, 3):
                                gate(t + 1, n - 2, 1 - par)
                            if n in (5, 7):
                                silu(t + 1, (n - 5) // 2)
                            if n == 9:
                                split(t + 1, 1 - par)
                            if n in (13, 15):
                                series(t + 1, (n - 13) // 2)
                        if norm:
                            if n == 10:
                                leaky(t + 2, q + 2)
                            if n == 12:
                                centre(t + 2, q + 2)
                                carry(t + 2, q + 2)

                with dve.Fori(0, LAYERS) as s:
                    t0 = s * NCH
                    for b in range(NB):
                        dve.wait_ge(x_loaded[b], 16)
                        dve.wait_ge(S["resid_done"], OPEN + s * FIN)
                        for j in range(NJ):
                            q = b * NJ + j
                            dve.bn_stats(stats[:, q, :], X[:, (q + 1) * CH:(q + 2) * CH]).then_inc(S["bn_stat"], 1)
                    dve.wait_ge(S["bn_stat"], OPEN + (s + 1) * NCH)
                    dve.wait_ge(S["weights_loaded"], OPEN + (s + 1) * 16 * NW)
                    for k in range(TAPS):
                        dve.tensor_tensor(w_cv[:, k, :], w_z[:, 0:E],
                                          cw_rows.rearrange("p (e k) -> p k e", k=TAPS)[:, k, :],
                                          ALU.mult).then_inc(S["folded"], 1)
                    dve.bn_aggr(bn[:, 0:2], stats[:, :, :]).then_inc(S["bn_agg"], 1)
                    for h in range(HALVES):
                        dve.tensor_scalar(D_diag[:, h, :], ident[:, :], D_c[h], None, ALU.mult).then_inc(S["d_diag"], 1)
                    dve.wait_ge(S["bn_rstd"], OPEN + s + 1)
                    dve.tensor_tensor(bn_scale, bn_rs, vec[:, 0:1], ALU.mult).then_inc(S["bn_part"], 1)
                    dve.wait_ge(S["bn_part"], OPEN + 2 * s + 1)
                    dve.tensor_tensor(bn_ms, bn_mean, bn_scale, ALU.mult).then_inc(S["bn_part"], 1)
                    dve.wait_ge(S["bn_part"], OPEN + 2 * s + 2)
                    dve.tensor_tensor(bn_shift, vec[:, 1:2], bn_ms, ALU.subtract).then_inc(S["bn_ready"], 1)
                    leaky(t0, 0)
                    leaky(t0 + 1, 1)
                    centre(t0, 0)
                    carry(t0, 0)
                    for h in range(HALVES):
                        gate(t0, h, 0)
                    for h in range(HALVES):
                        silu(t0, h)
                    split(t0, 0)
                    for h in range(HALVES):
                        series(t0, h)
                    centre(t0 + 1, 1)
                    carry(t0 + 1, 1)
                    with dve.Fori(0, NCH // 2 - 1) as pair:
                        for par in range(2):
                            ssm(s, 2 * pair + par, par, True, True)
                    ssm(s, NCH - 2, 0, True, False)
                    ssm(s, NCH - 1, 1, False, False)
                    gated(s * FIN + FIN, t0 + NCH, 1)
                    residual(s * FIN + FIN, NCH - 1)

            @block.gpsimd
            def _(pool):
                TT = pool.tensor_tensor

                def scale_rows(tp):
                    pool.wait_ge(S["rstd_ready"], OPEN + tp + 1)
                    pool.wait_ge(S["sq_ready"], OPEN + tp + 1)
                    TT(D[:, :], D[:, :], L3[:, :], ALU.mult).then_inc(S["dn_ready"], 1)

                def ratio(tp, h):
                    pool.wait_ge(S[f"sw{h}"], OPEN + tp + 1)
                    pool.wait_ge(S[f"so{1 - h}"], OPEN + tp + h)
                    TT(ps[:, :], pz[:, :], pw[:, :], ALU.mult).then_inc(S[f"ss{h}"], 1)

                def series(tp, h):
                    pool.wait_ge(S[f"sp{h}"], OPEN + tp + 1)
                    TT(pp[:, :], pp[:, :], pq[:, :], ALU.mult).then_inc(S[f"sm{h}"], 1)

                def steps(tp, h, par):
                    pool.wait_ge(S[f"so{h}"], OPEN + tp + 1)
                    TT(dt_s[:, par, h, :], pp[:, :], pr[:, h, :], ALU.add).then_inc(S[f"dt_ready{h}"], 1)
                    pool.wait_ge(S[f"dt_ready{h}"], OPEN + tp + 1)
                    TT(dtx[:, par, h, :], dt_s[:, par, h, :], xm[:, h, :], ALU.mult).then_inc(S[f"dtx_ready{h}"], 1)

                def read_out(t, n):
                    pool.wait_ge(S["c_copied"], OPEN + t * N + n + 1)
                    for h in range(HALVES):
                        k = 2 * n + h
                        pool.wait_ge(S["h_done"], OPEN + RING + t * PAIRS + k + 1)
                        pool.wait_ge(S["sum_done"], OPEN + t * PAIRS + k + 1)
                        TT(hc[:, k % HRING, :], state[:, k % RING, :], csb[:, n % CRING, :],
                           ALU.mult).then_inc(S["hc_done"], 1)

                def ssm(s, q, par, mid, norm):
                    t = s * NCH + q
                    for n in range(N):
                        read_out(t, n)
                        if mid:
                            if n in (11, 13):
                                ratio(t + 1, (n - 11) // 2)
                            if n in (12, 14):
                                series(t + 1, (n - 12) // 2)
                            if n in (13, 15):
                                steps(t + 1, (n - 13) // 2, 1 - par)
                        if norm and n == 14:
                            scale_rows(t + 2)

                with pool.Fori(0, LAYERS) as s:
                    t0 = s * NCH
                    scale_rows(t0)
                    for h in range(HALVES):
                        ratio(t0, h)
                        series(t0, h)
                        steps(t0, h, 0)
                    scale_rows(t0 + 1)
                    with pool.Fori(0, NCH // 2 - 1) as pair:
                        for par in range(2):
                            ssm(s, 2 * pair + par, par, True, True)
                    ssm(s, NCH - 2, 0, True, False)
                    ssm(s, NCH - 1, 1, False, False)

        stage_memory.close()

        KTs = sb("KTs", [P, L])
        QTs = sb("QTs", [P, L])
        Vs = sb("Vs", [P, KT, P])
        XR = sb("XR", [P, L])
        raw5 = sb("raw5", [P, 5, P])
        tr4 = sb("tr4", [P, 4, P])
        WvT = sb("WvT", [P, P])
        MQ = sb("MQ", [P, P])
        MK = sb("MK", [P, P])
        e1 = sb("e1", [P, 2, CH])
        probs = sb("probs", [P, 4, CH])
        acc = sb("acc", [P, 2, CH])
        q2b = sb("q2b", [PARTS, L], BF16)
        nk2 = sb("nk2", [P, KT])
        xn = sb("xn", [P, CH])
        D, T1, T2, T3, T4 = (sb(f"at{i}", [P, CH]) for i in range(5))
        ew = sb("ew", [P, NX, C])
        eb = sb("eb", [NX, C])
        rw = sb("rw", [P, NX])
        rb = sb("rb", [1, NX])
        tiny = sb("tiny", [P, 10, SUB, NX])
        v_sh, v_e, v_is, v_cand, v_oh1, v_e2, v_oh2, v_g, v_r, v_w = (tiny[:, i, :, :] for i in range(10))
        red = sb("red", [P, 8, SUB])
        r_m, r_m1, r_i1, r_m2, r_i2, r_den, r_rec = (red[:, i, :] for i in range(7))
        g3 = sb("g3", [P, SUB, PARTS, NX], BF16)
        g3t = sb("g3t", [PARTS * NX, CH], BF16)
        gft = sb("gft", [NX, CH])
        sel8 = sb("sel8", [PARTS * NX, NX, P], BF16)
        gx = sb("gx", [P, 2, CH])
        bank2b = bank[2][:, 0:CH // 2].bitcast(BF16)
        raw = [raw5[:, i, :] for i in range(5)]
        tr = [tr4[:, i, :] for i in range(4)]

        with nc.Block() as block:
            @block.sync
            def _(sp):
                for dst, src in ((raw[0], rotation.rearrange("(a b) -> a b", b=P)),
                                 (raw[1], entangle.rearrange("(a b) -> a b", b=P)),
                                 (raw[2], Wq), (raw[3], Wk), (raw[4], Wv),
                                 (rw[:, :], router_w), (rb[:, :], router_b.rearrange("(a e) -> a e", a=1)),
                                 (eb[:, :], expert_b), (ew[:, :, :], expert_w.rearrange("e c d -> c e d"))):
                    sp.dma_start(dst, src).then_inc(S["w_att"], 16)
                sp.dma_start(XR[:, :], x_in[:, 0, :]).then_inc(S["xr_loaded"], 16)

            @block.tensor
            def _(pe):
                pe.wait_ge(S["w_att"], OPEN + 9 * 16)
                for i in range(5):
                    pe.transpose(bank[i][:, 0:P], raw[i], ident[:, :]).then_inc(S["w_tr"], 1)
                pe.wait_ge(S["w_trc"], OPEN + 5)
                for i in range(2):
                    pe.matmul(bank[5 + i][:, 0:P], tr[i], tr[2 + i], start=True, stop=True).then_inc(S["w_mm"], 1)

            @block.vector
            def _(dve):
                for i, dst in enumerate(tr + [WvT[:, :]]):
                    dve.wait_ge(S["w_tr"], OPEN + i + 1)
                    dve.tensor_copy(dst, bank[i][:, 0:P]).then_inc(S["w_trc"], 1)
                for i, dst in enumerate((MQ[:, :], MK[:, :])):
                    dve.wait_ge(S["w_mm"], OPEN + i + 1)
                    dve.tensor_copy(dst, bank[5 + i][:, 0:P])

        with nc.Block() as block:
            @block.sync
            def _(sp):
                with sp.Fori(1, NB) as b:
                    sp.wait_ge(S["a_x"], OPEN + b * NJ)
                    sp.dma_start(XR[:, :], x_in[:, bass.ds(b, 1), :].rearrange("p a c -> p (a c)")).then_inc(S["xr_loaded"], 16)

            def cols_of(a, j):
                return a[:, bass.ds(j * CH, CH)]

            @block.tensor
            def _(pe):
                mm = pe.matmul
                with pe.Fori(0, NB) as b:
                    with pe.Fori(0, NJ) as j:
                        c = b * NJ + j
                        pe.wait_ge(S["a_x"], OPEN + c + 1)
                        mm(bank[7][:, :], mean_w[:, :], chunk(c), start=True, stop=True).then_inc(S["a_mean"], 1)
                        pe.wait_ge(S["a_sq"], OPEN + c + 1)
                        mm(bank[6][:, :], mean_w[:, :], T1[:, :], start=True, stop=True).then_inc(S["a_var"], 1)
                        pe.wait_ge(S["a_xn"], OPEN + c + 1)
                        mm(bank[4][:, :], MQ[:, :], xn[:, :], start=True, stop=True).then_inc(S["a_q"], 1)
                        mm(bank[5][:, :], MK[:, :], xn[:, :], start=True, stop=True).then_inc(S["a_k"], 1)
                        for i in range(SUB):
                            last = mm(bank[3][:, i * P:(i + 1) * P], xn[:, i * P:(i + 1) * P], WvT[:, :], start=True, stop=True)
                        last.then_inc(S["a_v"], 1)
                        pe.wait_ge(S["a_qs"], OPEN + c + 1)
                        mm(bank[1][0:PARTS, :], neghalf_c, T4[:, :], start=True, stop=True).then_inc(S["a_q2"], 1)
                        pe.wait_ge(S["a_ks"], OPEN + c + 1)
                        for i in range(SUB):
                            last = mm(bank[2][:, i:i + 1], T2[:, i * P:(i + 1) * P], negone_c, start=True, stop=True)
                        last.then_inc(S["a_k2"], 1)
                    with pe.Fori(0, NJ) as j:
                        c = b * NJ + j
                        pe.wait_ge(S["a_k2c"], OPEN + (b + 1) * NJ)
                        pe.wait_ge(S["a_kc"], OPEN + (b + 1) * NJ)
                        pe.wait_ge(S["a_qc"], OPEN + (b + 1) * NJ)
                        pe.wait_ge(S["a_vc"], OPEN + (b + 1) * NJ)
                        for k in range(KT + 2):
                            if k < KT:
                                pe.wait_ge(S["e1_done"], OPEN + c * KT + max(k - 2, 0))
                                mm(bank[k % 3][:, :], KTs[:, k * P:(k + 1) * P], cols_of(QTs, j), start=True, stop=False)
                                mm(bank[k % 3][:, :], onesb[:, :], cols_of(q2b, j), start=False,
                                   stop=True).then_inc(S["qk_ready"], 1)
                            if k >= 2:
                                m = k - 2
                                if m == 0:
                                    pe.wait_ge(S["o_done"], OPEN + c)
                                pe.wait_ge(S["p_ready"], OPEN + c * KT + m + 1)
                                mm(bank[3][:, :], Vs[:, m, :], probs[:, m % 4, :], start=m == 0,
                                   stop=m == KT - 1).then_inc(S["pv_done"], 1)
                        pe.wait_ge(S["acc_done"], OPEN + (c + 1) * KT)
                        for i in range(2):
                            last = mm(bank[4][:, :], ones[:, :], acc[:, i, :], start=i == 0, stop=i == 1)
                        last.then_inc(S["den_ready"], 1)

            @block.scalar
            def _(act):
                go = act.activation
                with act.Fori(0, NB) as b:
                    with act.Fori(0, NJ) as j:
                        c = b * NJ + j
                        act.wait_ge(S["a_d"], OPEN + c + 1)
                        go(T1[:, :], D[:, :], ACT.Square).then_inc(S["a_sq"], 1)
                        act.wait_ge(S["a_var"], OPEN + c + 1)
                        act.wait_ge(S["a_k2"], OPEN + c)
                        go(T2[:, :], bank[6][:, :], ACT.Ln, bias=eps_c).then_inc(S["a_ln"], 1)
                        act.wait_ge(S["a_ln"], OPEN + c + 1)
                        go(T3[:, :], T2[:, :], ACT.Exp, scale=-0.5).then_inc(S["a_rs"], 1)
                        act.wait_ge(S["a_q"], OPEN + c + 1)
                        act.wait_ge(S["a_q2"], OPEN + c)
                        go(T4[:, :], bank[4][:, :], ACT.Square).then_inc(S["a_qs"], 1)
                        act.copy(cols_of(QTs, j), bank[4][:, :]).then_inc(S["a_qc"], 1)
                        act.wait_ge(S["a_k"], OPEN + c + 1)
                        act.wait_ge(S["a_rs"], OPEN + c + 1)
                        go(T2[:, :], bank[5][:, :], ACT.Square).then_inc(S["a_ks"], 1)
                    with act.Fori(0, NJ) as j:
                        c = b * NJ + j
                        act.wait_ge(S["a_k2c"], OPEN + (b + 1) * NJ)
                        for k in range(KT + 1):
                            if k < KT:
                                act.wait_ge(S["qk_ready"], OPEN + c * KT + k + 1)
                                act.wait_ge(S["p_ready"], OPEN + c * KT + max(k - 1, 0))
                                go(e1[:, k % 2, :], bank[k % 3][:, :], ACT.Exp, bias=nk2[:, k:k + 1],
                                   scale=2.0).then_inc(S["e1_done"], 1)
                            if k >= 1:
                                m = k - 1
                                act.wait_ge(S["e1_done"], OPEN + c * KT + m + 1)
                                act.wait_ge(S["pv_done"], OPEN + c * KT + max(m - 3, 0))
                                act.wait_ge(S["acc_done"], OPEN + c * KT + max(m - 3, 0))
                                go(probs[:, m % 4, :], e1[:, m % 2, :], ACT.Exp).then_inc(S["p_ready"], 1)

            @block.vector
            def _(dve):
                with dve.Fori(0, NB) as b:
                    with dve.Fori(0, NJ) as j:
                        c = b * NJ + j
                        dve.wait_ge(S["xr_loaded"], OPEN + (b + 1) * 16)
                        dve.tensor_tensor(chunk(c), chunk(c), cols_of(XR, j), ALU.add).then_inc(S["a_x"], 1)
                        dve.wait_ge(S["a_mean"], OPEN + c + 1)
                        dve.tensor_tensor(D[:, :], chunk(c), bank[7][:, :], ALU.subtract).then_inc(S["a_d"], 1)
                        dve.wait_ge(S["a_rs"], OPEN + c + 1)
                        dve.wait_ge(S["a_v"], OPEN + c)
                        dve.wait_ge(S["a_qc"], OPEN + c)
                        dve.wait_ge(S["a_ks"], OPEN + c)
                        dve.wait_ge(S["a_d"], OPEN + c + 1)
                        dve.tensor_tensor(xn[:, :], D[:, :], T3[:, :], ALU.mult).then_inc(S["a_xn"], 1)
                        dve.wait_ge(S["a_ks"], OPEN + c + 1)
                        dve.tensor_scalar(cols_of(KTs, j), bank[5][:, :], 1.0, None, ALU.mult).then_inc(S["a_kc"], 1)
                        dve.wait_ge(S["a_v"], OPEN + c + 1)
                        dve.tensor_scalar(cols_of(Vs[:, :, :].rearrange("p k d -> p (k d)"), j), bank[3][:, :], 1.0, None, ALU.mult).then_inc(S["a_vc"], 1)
                        p, r = cols_of(q2b, j), D
                        dve.wait_ge(S["a_q2"], OPEN + c + 1)
                        dve.tensor_scalar(p, bank[1][0:3, :], 1.0, None, ALU.mult).then_inc(S["a_split"], 1)
                        dve.wait_ge(S["a_split"], OPEN + 5 * c + 1)
                        dve.wait_ge(S["a_xn"], OPEN + c + 1)
                        dve.tensor_tensor(r[0:2, :], bank[1][0:2, :], p[0:2, :], ALU.subtract).then_inc(S["a_split"], 1)
                        dve.wait_ge(S["a_split"], OPEN + 5 * c + 2)
                        dve.tensor_scalar(p[0:2, :], r[0:2, :], 1.0, None, ALU.mult).then_inc(S["a_split"], 1)
                        dve.wait_ge(S["a_split"], OPEN + 5 * c + 3)
                        dve.tensor_tensor(r[0:1, :], r[0:1, :], p[0:1, :], ALU.subtract).then_inc(S["a_split"], 1)
                        dve.wait_ge(S["a_split"], OPEN + 5 * c + 4)
                        dve.tensor_scalar(p[0:1, :], r[0:1, :], 1.0, None, ALU.mult).then_inc(S["a_split"], 1)
                        dve.wait_ge(S["a_k2"], OPEN + c + 1)
                        dve.tensor_scalar(nk2[:, bass.ds(j * SUB, SUB)], bank[2][:, 0:SUB], 1.0, None, ALU.mult).then_inc(S["a_k2c"], 1)
                    with dve.Fori(0, NJ) as j:
                        c = b * NJ + j
                        for k in range(KT):
                            dve.wait_ge(S["p_ready"], OPEN + c * KT + k + 1)
                            if k < 2:
                                if k == 0:
                                    dve.wait_ge(S["den_ready"], OPEN + c)
                                dve.tensor_copy(acc[:, k, :], probs[:, k % 4, :]).then_inc(S["acc_done"], 1)
                            else:
                                dve.wait_ge(S["acc_done"], OPEN + c * KT + k - 1)
                                dve.tensor_tensor(acc[:, k % 2, :], acc[:, k % 2, :], probs[:, k % 4, :],
                                                  ALU.add).then_inc(S["acc_done"], 1)
                        dve.wait_ge(S["den_ready"], OPEN + c + 1)
                        dve.reciprocal(T1[:, :], bank[4][:, :]).then_inc(S["rec_done"], 1)
                        dve.wait_ge(S["rec_done"], OPEN + c + 1)
                        dve.wait_ge(S["pv_done"], OPEN + (c + 1) * KT)
                        dve.tensor_tensor(T2[:, :], T1[:, :], bank[3][:, :], ALU.mult).then_inc(S["o_done"], 1)
                        dve.wait_ge(S["o_done"], OPEN + c + 1)
                        dve.tensor_tensor(chunk(c), chunk(c), T2[:, :], ALU.add).then_inc(S["att_done"], 1)

        def bc(a):
            return a.rearrange("p (s o) -> p s o", o=1).to_broadcast([P, SUB, NX])

        with nc.Block() as block:
            @block.gpsimd
            def _(pool):
                pool.memset(sel8[:, :, :], 0.0).then_inc(S["w_cst"], 1)
                for k in range(PARTS):
                    pool.wait_ge(S["w_cst"], OPEN + 1 + k)
                    pool.affine_select(out=sel8[:, :, :], in_=sel8[:, :, :], compare_op=ALU.not_equal, fill=1.0, base=-NX * k,
                                       pattern=[[-1, NX], [0, P]], channel_multiplier=1).then_inc(S["w_cst"], 1)

            @block.sync
            def _(sp):
                with sp.Fori(0, NB) as b:
                    with sp.Fori(0, NJ) as j:
                        c = b * NJ + j
                        sp.wait_ge(S["f_out"], OPEN + c + 1)
                        sp.dma_start(out_v[:, bass.ds(b, 1), bass.ds(j * CH, CH)].rearrange("p a c -> p (a c)"),
                                     chunk(c)).then_inc(S["stored"], 16)
                sp.wait_ge(S["stored"], OPEN + NCH * 16)

            @block.tensor
            def _(pe):
                mm = pe.matmul
                pe.wait_ge(S["w_cst"], OPEN + 1 + PARTS)
                with pe.Fori(0, NCH) as c:
                    mm(bank[7][:, :], mean_w[:, :], chunk(c), start=True, stop=True).then_inc(S["f_mean"], 1)
                    pe.wait_ge(S["f_sq"], OPEN + c + 1)
                    mm(bank[6][:, :], mean_w[:, :], T1[:, :], start=True, stop=True).then_inc(S["f_var"], 1)
                    pe.wait_ge(S["f_xn"], OPEN + c + 1)
                    for i in range(SUB):
                        o = bank[1][:, i * NX:(i + 1) * NX]
                        mm(o, xn[:, i * P:(i + 1) * P], rw[:, :], start=True, stop=False)
                        last = mm(o, ones[0:1, :], rb[:, :], start=False, stop=True)
                    last.then_inc(S["f_log"], 1)
                    pe.wait_ge(S["f_g3"], OPEN + c + 1)
                    for i in range(SUB):
                        last = pe.transpose(bank2b[0:PARTS * NX, i * P:(i + 1) * P],
                                            g3[:, i, :, :].rearrange("p k e -> p (k e)"), identb[:, :])
                    last.then_inc(S["f_tr"], 1)
                    for i in range(SUB):
                        last = pe.transpose(bank[3][0:NX, i * P:(i + 1) * P], v_g[:, i, :], ident[:, :])
                    last.then_inc(S["f_trf"], 1)
                    pe.wait_ge(S["f_gt"], OPEN + c + 1)
                    for e in range(NX + 1):
                        if e < NX:
                            pe.wait_ge(S["f_gx"], OPEN + c * NX + max(e - 1, 0))
                            mm(bank[4 + e % 2][:, :], sel8[:, e, :], g3t[:, :], start=True, stop=True).then_inc(S["f_rep"], 1)
                        if e >= 1:
                            pe.wait_ge(S["f_gx"], OPEN + c * NX + e)
                            mm(bank[0][:, :], ew[:, e - 1, :], gx[:, (e - 1) % 2, :], start=e == 1,
                               stop=False).then_inc(S["f_mm"], 1)
                    pe.wait_ge(S["f_gtf"], OPEN + c + 1)
                    mm(bank[0][:, :], eb[:, :], gft[:, :], start=False, stop=True).then_inc(S["f_mm"], 1)
                    pe.wait_ge(S["f_out"], OPEN + c + 1)

            @block.scalar
            def _(act):
                go = act.activation
                with act.Fori(0, NCH) as c:
                    act.wait_ge(S["f_d"], OPEN + c + 1)
                    go(T1[:, :], D[:, :], ACT.Square).then_inc(S["f_sq"], 1)
                    act.wait_ge(S["f_var"], OPEN + c + 1)
                    go(T2[:, :], bank[6][:, :], ACT.Ln, bias=eps_c).then_inc(S["f_ln"], 1)
                    act.wait_ge(S["f_ln"], OPEN + c + 1)
                    go(T3[:, :], T2[:, :], ACT.Exp, scale=-0.5).then_inc(S["f_rs"], 1)
                    act.wait_ge(S["f_ch"], OPEN + c + 1)
                    go(v_e, v_sh, ACT.Exp).then_inc(S["f_exp"], 1)
                    act.wait_ge(S["f_tr"], OPEN + c + 1)
                    act.copy(g3t[:, :], bank2b[0:PARTS * NX, :]).then_inc(S["f_gt"], 1)
                    act.wait_ge(S["f_trf"], OPEN + c + 1)
                    act.copy(gft[:, :], bank[3][0:NX, :]).then_inc(S["f_gtf"], 1)

            @block.vector
            def _(dve):
                NCHAIN = 22

                for e in range(NX):
                    dve.memset(v_w[:, :, e:e + 1], float(NX - e))
                with dve.Fori(0, NCH) as c:
                    done = [0]

                    def link(ins):
                        done[0] += 1
                        ins.then_inc(S["f_chain"], 1)
                        dve.wait_ge(S["f_chain"], OPEN + c * NCHAIN + done[0])
                    TT, TR = dve.tensor_tensor, dve.tensor_reduce
                    dve.wait_ge(S["f_mean"], OPEN + c + 1)
                    dve.tensor_tensor(D[:, :], chunk(c), bank[7][:, :], ALU.subtract).then_inc(S["f_d"], 1)
                    dve.wait_ge(S["f_rs"], OPEN + c + 1)
                    dve.wait_ge(S["f_d"], OPEN + c + 1)
                    TT(xn[:, :], D[:, :], T3[:, :], ALU.mult).then_inc(S["f_xn"], 1)
                    dve.wait_ge(S["f_log"], OPEN + c + 1)
                    logits = bank[1][:, 0:SUB * NX].rearrange("p (s e) -> p s e", e=NX)
                    link(TR(r_m, logits, AX_X, ALU.max))
                    TT(v_sh, logits, bc(r_m), ALU.subtract).then_inc(S["f_ch"], 1)
                    dve.wait_ge(S["f_exp"], OPEN + c + 1)
                    link(TR(r_m1, v_e, AX_X, ALU.max))
                    link(TT(v_is, v_e, bc(r_m1), ALU.is_equal))
                    link(TT(v_cand, v_is, v_w, ALU.mult))
                    link(TR(r_i1, v_cand, AX_X, ALU.max))
                    link(TT(v_oh1, v_cand, bc(r_i1), ALU.is_equal))
                    link(dve.scalar_tensor_tensor(out=v_e2, in0=v_oh1, scalar=-2.0, in1=v_e, op0=ALU.mult, op1=ALU.add))
                    link(TR(r_m2, v_e2, AX_X, ALU.max))
                    link(TT(v_is, v_e2, bc(r_m2), ALU.is_equal))
                    link(TT(v_cand, v_is, v_w, ALU.mult))
                    link(TR(r_i2, v_cand, AX_X, ALU.max))
                    link(TT(v_oh2, v_cand, bc(r_i2), ALU.is_equal))
                    link(TT(r_den, r_m1, r_m2, ALU.add))
                    link(dve.reciprocal(r_rec, r_den))
                    link(TT(v_oh1, v_oh1, v_oh2, ALU.add))
                    link(TT(v_e2, v_e, v_oh1, ALU.mult))
                    link(TT(v_g, v_e2, bc(r_rec), ALU.mult))
                    link(dve.tensor_copy(g3[:, :, 2, :], v_g))
                    link(TT(v_r, v_g, g3[:, :, 2, :], ALU.subtract))
                    link(dve.tensor_copy(g3[:, :, 1, :], v_r))
                    link(TT(v_r, v_r, g3[:, :, 1, :], ALU.subtract))
                    dve.tensor_copy(g3[:, :, 0, :], v_r).then_inc(S["f_g3"], 1)
                    link(dve.tensor_copy(r_m, r_m))
                    assert done[0] == NCHAIN
                    for e in range(NX):
                        dve.wait_ge(S["f_rep"], OPEN + c * NX + e + 1)
                        if e >= 2:
                            dve.wait_ge(S["f_mm"], OPEN + c * (NX + 1) + e - 1)
                        TT(gx[:, e % 2, :], xn[:, :], bank[4 + e % 2][:, :], ALU.mult).then_inc(S["f_gx"], 1)
                    dve.wait_ge(S["f_mm"], OPEN + (c + 1) * (NX + 1))
                    TT(chunk(c), chunk(c), bank[0][:, :], ALU.add).then_inc(S["f_out"], 1)




_INS = ['x', 'L0_conv_bn_gamma', 'L0_conv_bn_beta', 'L0_conv_ln_gamma', 'L0_conv_ln_beta', 'L0_conv_W_in',
        'L0_conv_conv_w', 'L0_conv_conv_b', 'L0_conv_W_xp', 'L0_conv_W_dt', 'L0_conv_b_dt', 'L0_conv_A_log',
        'L0_conv_Dp', 'L0_conv_W_out', 'L1_attn_rotation_params', 'L1_attn_entangle_params', 'L1_attn_Wq',
        'L1_attn_Wk', 'L1_attn_Wv', 'L1_ffn_router_w', 'L1_ffn_router_b', 'L1_ffn_expert_w', 'L1_ffn_expert_b']
_OUTS = [((4, 128, 64, 64), 'float32')]


def kernel(**inputs):
    import numpy as _np
    import concourse.bacc as _bacc
    from concourse import mybir as _mybir
    from concourse.bass_utils import run_bass_kernel_spmd as _run

    nc = _bacc.Bacc("TRN2", target_bir_lowering=False, num_devices=1)
    arrays, args = {}, []
    for name in _INS:
        a = _np.ascontiguousarray(inputs[name])
        arrays[f"in_{name}_dram"] = a
        args.append(nc.dram_tensor(f"in_{name}_dram", a.shape, _mybir.dt.from_np(a.dtype), kind="ExternalInput").ap())
    for i, (shape, dtype) in enumerate(_OUTS):
        dt = _mybir.dt.from_np(_np.dtype(dtype))
        args.append(nc.dram_tensor(f"out_{i}_dram", shape, dt, kind="ExternalOutput").ap())
    hybrid_kernel(nc, *args)
    r = _run(nc, [arrays], core_ids=[0])
    got = tuple(r.results[0][f"out_{i}_dram"] for i in range(len(_OUTS)))
    return got[0]
```

```python
from contextlib import ExitStack

import concourse.bass as bass
from concourse import mybir

ALU = mybir.AluOpType
ACT = mybir.ActivationFunctionType
AX_X = mybir.AxisListType.X
F32 = mybir.dt.float32
BF16 = mybir.dt.bfloat16

P = 128
CH = 512
TABLES = "natural_log_exp_and_others"
SLOPE = 0.01
EPS = 1e-5
RING = 8
HRING = 4
CRING = 4
OPEN = 1
ATANH = (1.99999967, 0.66676006, 0.39589371, 0.34226697)


def hybrid_kernel(nc, x, bn_gamma, bn_beta, ln_gamma, ln_beta, W_in, conv_w, conv_b, W_xp, W_dt, b_dt, A_log, Dp,
                  W_out, rotation, entangle, Wq, Wk, Wv, router_w, router_b, expert_w, expert_b, out):
    NB, C, HH, WW = x.shape
    L = HH * WW
    LAYERS, _, E2 = W_in.shape
    E = E2 // 2
    TAPS = conv_w.shape[2]
    R = W_dt.shape[1]
    N = A_log.shape[2]
    NX = router_w.shape[1]
    HALVES = E // P
    NJ = L // CH
    NCH = NB * NJ
    KT = L // P
    SUB = CH // P
    BC = 2 * N
    PARTS = 3
    ROWS = PARTS * BC
    PAIRS = N * HALVES
    GROUP = RING // HALVES
    HIST = TAPS - 1
    HALF_TAPS = range(TAPS // 2), range(TAPS // 2, TAPS)
    FIN = NCH + 1
    assert C == P and HALVES == 2 and ROWS == 96 and NCH % 2 == 0

    x_in = x.rearrange("b c h w -> c b (h w)")
    out_v = out.rearrange("b c h w -> c b (h w)")

    with ExitStack() as ctx:
        def sb(name, shape, dt=F32):
            return ctx.enter_context(nc.sbuf_tensor(name, shape, dt))

        def sem(name):
            return ctx.enter_context(nc.semaphore(name))

        bank = [ctx.enter_context(nc.psum_tensor(f"bank{i}", [P, CH], F32)) for i in range(8)]

        X = sb("X", [P, (NCH + 1) * CH])
        ident = sb("ident", [P, P])
        identb = sb("identb", [P, P], BF16)
        mean_w = sb("mean_w", [P, P])
        ones = sb("ones", [P, P])
        onesb = sb("onesb", [PARTS, P], BF16)
        cols = sb("cols", [P, 8])
        eps_c, one_c, negone_c, two_c, atanh2_c = (cols[:, i:i + 1] for i in range(5))
        neghalf_c = cols[:, 5:8]

        zeros, consts = sem("zeros"), sem("consts")
        x_loaded = [sem(f"x_loaded{b}") for b in range(NB)]
        names = """weights_loaded folded d_diag a_exp a_ready nb_ready bn_stat bn_agg bn_lnv bn_rstd
            bn_part bn_ready aff_done u_ready mean_ready d_ready sq_ready var_ready lnv_ready rstd_ready dn_ready
            carry_ready un_ready z_ready0 z_ready1 ze0 ze1 zl0 zl1 zg0 zg1 zs_ready0 zs_ready1 cv_ready0 cv_ready1
            ce0 ce1 cl0 cl1 cg0 cg1 xm_ready0 xm_ready1 dbl_ready s_hi s_r1 s_mid s_r2 s_ready r_ready
            dp_ready0 dp_ready1 sa0 sa1 sr0 sr1 sz0 sz1 sl0 sl1 sw0 sw1 ss0 ss1 sq0 sq1 sp0 sp1 sm0 sm1 sn0 sn1
            so0 so1 dt_ready0 dt_ready1 dtx_ready0 dtx_ready1 b_ready c_ready c_copied u_done h_done da_ready hc_done
            sum_done skip_done kept hinit_done y_done out_ready resid_done
            w_att w_tr w_trc w_mm xr_loaded
            a_x a_mean a_d a_sq a_var a_ln a_rs a_xn a_q a_k a_v a_qc a_qs a_kc a_ks a_vc a_k2 a_q2 a_k2c
            a_split qk_ready e1_done p_ready pv_done acc_done den_ready rec_done o_done att_done
            f_mean f_d f_sq f_var f_ln f_rs f_xn f_log f_ch f_exp f_chain f_g3 f_tr f_trf f_gt f_gtf f_rep f_gx f_mm
            f_out stored w_cst""".split()
        S = {n: sem(n) for n in names}

        def chunk(q, n=1):
            return X[:, bass.ds((q + 1) * CH, n * CH)]

        stage_memory = ExitStack()

        def sbs(name, shape, dt=F32):
            return stage_memory.enter_context(nc.sbuf_tensor(name, shape, dt))

        decay = sbs("decay", [P, RING, CH])
        state = sbs("state", [P, RING, CH])
        hc = sbs("hc", [P, HRING, CH])
        csb = sbs("csb", [P, CRING, CH])
        dt_s = sbs("dt_s", [P, 2, HALVES, CH])
        dtx = sbs("dtx", [P, 2, HALVES, CH])
        xm = sbs("xm", [P, HALVES, CH])
        zs = sbs("zs", [P, 2, HALVES, CH])
        yg = sbs("yg", [P, HALVES, CH])
        bc3 = sbs("bc3", [ROWS, 2, CH], BF16)
        un = sbs("un", [P, HIST + CH])
        D, SQ, RS = (sbs(f"ln{i}", [P, CH]) for i in range(3))
        EG = sbs("sig", [P, CH])
        sg = sbs("sg", [P, HALVES, CH])
        rrow = sbs("rrow", [P, CH])
        rest = rrow[0:2 * BC, :]
        pa, pz, pw = (sbs(f"sp_{n}", [P, CH]) for n in "azw")
        ps, pq, pp, pr = (sbs(f"sp_{n}", [P, HALVES, CH]) for n in "sqpr")
        sel = sbs("sel", [ROWS, BC, P], BF16)
        D_diag = sbs("D_diag", [P, HALVES, P])
        first = sbs("first", [P, NCH])
        w_z = sbs("w_z", [P, E2])
        cw_rows = decay[:, 0:E * TAPS // CH, :].rearrange("p a c -> p (a c)")
        w_cv = sbs("w_cv", [P, TAPS, E])
        w_xp = sbs("w_xp", [P, HALVES, ROWS + R])
        w_dt = sbs("w_dt", [P, E])
        w_out = sbs("w_out", [P, HALVES, C])
        vec = sbs("vec", [P, 4])
        evec = sbs("evec", [P, 4, HALVES])
        A_s = sbs("A_s", [P, HALVES, N])
        Aexp = sbs("Aexp", [P, HALVES, N])
        stats = sbs("stats", [P, NCH, 6])
        bn = sbs("bn", [P, 8])
        kept = sbs("kept", [P, PAIRS])
        hinit = sbs("hinit", [P, PAIRS])

        conv_b_c = [evec[:, 0, h:h + 1] for h in range(HALVES)]
        dt_b_c = [evec[:, 1, h:h + 1] for h in range(HALVES)]
        D_c = [evec[:, 2, h:h + 1] for h in range(HALVES)]
        nconv_b_c = [evec[:, 3, h:h + 1] for h in range(HALVES)]
        bn_mean, bn_var, bn_ln, bn_rs, bn_scale, bn_ms, bn_shift = (bn[:, i:i + 1] for i in range(7))

        psum_y = bank[0:2]
        psum_bc = bank[2:5]
        psum_u = bank[5]
        bank_a, bank_b = prep = bank[6:8]
        bc_bank = [n % 3 for n in range(N - 1)] + [1]
        bc_last = [min(d for d in range(1, N) if bc_bank[(n - d) % N] == bc_bank[n]) for n in range(N)]
        assert N % 3 == 1 and min(bc_last) >= 2

        with nc.Block() as block:
            @block.sync
            def _(sp):
                for b in range(NB):
                    sp.dma_start(X[:, (1 + b * NJ) * CH:(1 + (b + 1) * NJ) * CH], x_in[:, b, :]).then_inc(x_loaded[b], 16)
                for n in names:
                    sp.sem_inc(S[n], OPEN)

            @block.gpsimd
            def _(pool):
                pool.memset(ident[:, :], 0.0).then_inc(zeros, 1)
                pool.memset(identb[:, :], 0.0).then_inc(zeros, 1)
                pool.memset(sel[:, :, :], 0.0).then_inc(zeros, 1)
                pool.wait_ge(zeros, 3)
                for m in (ident, identb):
                    pool.affine_select(out=m[:, :], in_=m[:, :], compare_op=ALU.not_equal, fill=1.0, base=0,
                                       pattern=[[-1, P]], channel_multiplier=1).then_inc(zeros, 1)
                pool.wait_ge(zeros, 5)
                for k in range(PARTS):
                    pool.affine_select(out=sel[:, :, :], in_=sel[:, :, :], compare_op=ALU.not_equal, fill=1.0,
                                       base=-BC * k, pattern=[[-1, BC], [0, P]],
                                       channel_multiplier=1).then_inc(zeros, 1)
                    pool.wait_ge(zeros, 6 + k)

            @block.vector
            def _(dve):
                dve.memset(mean_w[:, :], 1.0 / C)
                dve.memset(ones[:, :], 1.0)
                dve.memset(onesb[:, :], 1.0)
                dve.memset(eps_c, EPS)
                dve.memset(one_c, 1.0)
                dve.memset(negone_c, -1.0)
                dve.memset(two_c, 2.0)
                dve.memset(atanh2_c, ATANH[2])
                dve.memset(neghalf_c, -0.5)
                dve.memset(first[:, :], 1.0).then_inc(consts, 1)
                dve.wait_ge(consts, 1)
                dve.memset(first[:, :].rearrange("p (b j) -> p b j", j=NJ)[:, :, 0:1], 0.0)
                dve.memset(X[:, 0:CH], 0.0)
                dve.memset(un[:, :], 0.0)
                dve.memset(kept[:, :], 0.0)
                for h in range(HALVES):
                    dve.memset(psum_y[h][:, :], 0.0)
                    dve.memset(zs[:, 1, h, :], 0.0)
                dve.sem_inc(S["h_done"], RING)
                dve.sem_inc(S["hc_done"], RING)
                dve.sem_inc(S["sum_done"], HRING)

            @block.scalar
            def _(act):
                act.preload_act_table_set(TABLES)

        with nc.Block() as block:

            @block.sync
            def _(sp):
                with sp.Fori(0, LAYERS) as s:
                    sp.wait_ge(S["resid_done"], OPEN + s * FIN)
                    w = S["weights_loaded"]

                    def of(a, pattern, **kw):
                        return a[bass.ds(s, 1)].rearrange(pattern, **kw)
                    for i, a in enumerate((bn_gamma, bn_beta, ln_gamma, ln_beta)):
                        sp.dma_start(vec[:, i:i + 1], of(a, "a c -> c a")).then_inc(w, 16)
                    sp.dma_start(w_z[:, :], of(W_in, "a c e -> (a c) e")).then_inc(w, 16)
                    sp.dma_start(cw_rows, of(conv_w, "a e k -> a (e k)").to_broadcast([P, E * TAPS])).then_inc(w, 16)
                    for i, a in enumerate((conv_b, b_dt, Dp)):
                        sp.dma_start(evec[:, i, :], of(a, "a (h p) -> (a p) h", p=P),
                                     allow_slow_non_contiguous=True).then_inc(w, 16)
                    for k in range(PARTS):
                        sp.dma_start(w_xp[:, :, k * BC:(k + 1) * BC],
                                     of(W_xp, "a (h p) r -> (a p) h r", p=P)[:, :, R:R + BC]).then_inc(w, 16)
                    sp.dma_start(w_xp[:, :, ROWS:ROWS + R],
                                 of(W_xp, "a (h p) r -> (a p) h r", p=P)[:, :, 0:R]).then_inc(w, 16)
                    sp.dma_start(w_dt[ROWS:ROWS + R, :], of(W_dt, "a r e -> (a r) e")).then_inc(w, 16)
                    sp.dma_start(A_s[:, :, :], of(A_log, "a (h p) n -> (a p) h n", p=P)).then_inc(w, 16)
                    sp.dma_start(w_out[:, :, :], of(W_out, "a (h p) c -> (a p) h c", p=P)).then_inc(w, 16)
            NW = 4 + 1 + 1 + 3 + PARTS + 1 + 1 + 1 + 1

            @block.tensor
            def _(pe):
                mm = pe.matmul

                def mean(tp, q, read):
                    pe.wait_ge(S["u_ready"], OPEN + tp + 1)
                    pe.wait_ge(S[read], OPEN + tp)
                    mm(bank_b[:, :], mean_w[:, :], chunk(q), start=True, stop=True).then_inc(S["mean_ready"], 1)

                def var(tp):
                    pe.wait_ge(S["sq_ready"], OPEN + tp + 1)
                    pe.wait_ge(S["sr1"], OPEN + tp)
                    mm(bank_b[:, :], mean_w[:, :], SQ[:, :], start=True, stop=True).then_inc(S["var_ready"], 1)

                def gate(tp, h, fin, lns):
                    if h == 0:
                        pe.wait_ge(S["sr0"], OPEN + tp + 1)
                        pe.wait_ge(S["resid_done"], OPEN + fin)
                    else:
                        pe.wait_ge(S["sr1"], OPEN + tp + 1)
                        pe.wait_ge(S["lnv_ready"], OPEN + lns)
                    mm(prep[h][:, :], w_z[:, E + h * P:E + (h + 1) * P], un[:, HIST:HIST + CH],
                       start=True, stop=True).then_inc(S[f"z_ready{h}"], 1)

                def conv(tp, h, taps=range(TAPS)):
                    if 0 in taps:
                        pe.wait_ge(S["un_ready"], OPEN + tp + 1)
                        pe.wait_ge(S[f"zs_ready{h}"], OPEN + tp)
                    for k in taps:
                        last = mm(prep[h][:, :], w_cv[:, k, h * P:(h + 1) * P], un[:, k:k + CH],
                                  start=k == 0, stop=k == TAPS - 1)
                    if TAPS - 1 in taps:
                        last.then_inc(S[f"cv_ready{h}"], 1)

                def dbl(tp):
                    pe.wait_ge(S["xm_ready0"], OPEN + tp + 1)
                    pe.wait_ge(S["xm_ready1"], OPEN + tp + 1)
                    for h in range(HALVES):
                        last = mm(bank_a[0:ROWS + R, :], w_xp[:, h, :], xm[:, h, :],
                                  start=h == 0, stop=h == HALVES - 1)
                    last.then_inc(S["dbl_ready"], 1)

                def step(tp, h, centred):
                    pe.wait_ge(S["r_ready"], OPEN + tp + 1)
                    if h == 0:
                        pe.wait_ge(S["s_r1"], OPEN + tp + 1)
                    else:
                        pe.wait_ge(S["xm_ready1"], OPEN + tp + 1)
                        pe.wait_ge(S["d_ready"], OPEN + centred)
                    mm(prep[h][:, :], w_dt[ROWS:ROWS + R, h * P:(h + 1) * P], rrow[ROWS:ROWS + R, :],
                       start=True, stop=True).then_inc(S[f"dp_ready{h}"], 1)

                def finish(fin, steps):
                    pe.wait_ge(S["y_done"], OPEN + fin * HALVES)
                    pe.wait_ge(S["sr0"], OPEN + steps)
                    for h in range(HALVES):
                        last = mm(bank_a[:, :], w_out[:, h, :], yg[:, h, :],
                                  start=h == 0, stop=h == HALVES - 1)
                    last.then_inc(S["out_ready"], 1)

                def spread_c(t, n, par):
                    if n == 0:
                        pe.wait_ge(S["s_ready"], OPEN + t + 1)
                    pe.wait_ge(S["h_done"], OPEN + RING + t * PAIRS + 2 * (n - bc_last[n] + 1))
                    mm(psum_bc[bc_bank[n]][:, :], sel[:, N + n, :], bc3[:, par, :], start=True,
                       stop=True).then_inc(S["c_ready"], 1)

                def spread_b(t, n, par):
                    pe.wait_ge(S["c_copied"], OPEN + t * N + n + 1)
                    mm(psum_bc[bc_bank[n]][:, :], sel[:, n, :], bc3[:, par, :], start=True,
                       stop=True).then_inc(S["b_ready"], 1)

                def skip(fin):
                    pe.wait_ge(S["y_done"], OPEN + fin * HALVES)
                    for h in range(HALVES):
                        mm(psum_y[h][:, :], D_diag[:, h, :], xm[:, h, :], start=True,
                           stop=False).then_inc(S["skip_done"], 1)

                def gather(t, n):
                    for h in range(HALVES):
                        k = 2 * n + h
                        pe.wait_ge(S["hc_done"], OPEN + RING + t * PAIRS + k + 1)
                        mm(psum_y[h][:, :], ident[:, :], hc[:, k % HRING, :], start=False,
                           stop=n == N - 1).then_inc(S["sum_done"], 1)

                def ssm(s, q, par, mid, norm):
                    t = s * NCH + q
                    fin = s * FIN + q + 1
                    for m in range(2, N + 2):
                        if m == 2:
                            skip(fin)
                        if m + 1 < N:
                            spread_b(t, m + 1, par)
                        elif mid:
                            spread_b(t + 1, m + 1 - N, 1 - par)
                        gather(t, m - 2)
                        if m + 2 < N:
                            spread_c(t, m + 2, par)
                        elif mid:
                            spread_c(t + 1, m + 2 - N, 1 - par)
                        if mid and m == 4:
                            dbl(t + 1)
                        if norm and m == 4:
                            mean(t + 2, q + 2, "xm_ready1")
                        if mid and m in (6, 7):
                            step(t + 1, m - 6, t + 2 + norm)
                        if m == 9:
                            finish(fin, t + 1 + mid)
                        if norm and m == 10:
                            var(t + 2)
                        if mid and m in (11, 12):
                            gate(t + 1, m - 11, fin, t + 2 + norm)
                        if norm and m in (15, 16):
                            conv(t + 2, 0, HALF_TAPS[m - 15])
                        if norm and m in (16, 17):
                            conv(t + 2, 1, HALF_TAPS[m - 16])

                def opening(s):
                    t0 = s * NCH
                    mean(t0, 0, "zs_ready1")
                    var(t0)
                    for h in range(HALVES):
                        conv(t0, h)
                    dbl(t0)
                    for h in range(HALVES):
                        step(t0, h, t0 + 1)
                    for h in range(HALVES):
                        gate(t0, h, s * FIN, t0 + 1)
                    mean(t0 + 1, 1, "zs_ready1")
                    var(t0 + 1)
                    spread_c(t0, 0, 0)
                    spread_c(t0, 1, 0)
                    spread_b(t0, 0, 0)
                    conv(t0 + 1, 0)
                    for m in range(2):
                        conv(t0 + 1, 1, HALF_TAPS[m])
                        spread_b(t0, m + 1, 0)
                        spread_c(t0, m + 2, 0)

                with pe.Fori(0, LAYERS) as s:
                    pe.wait_ge(S["weights_loaded"], OPEN + (s + 1) * 16 * NW)
                    pe.wait_ge(S["folded"], OPEN + (s + 1) * TAPS)
                    pe.wait_ge(S["d_diag"], OPEN + (s + 1) * HALVES)
                    opening(s)
                    with pe.Fori(0, NCH // 2 - 1) as pair:
                        for par in range(2):
                            ssm(s, 2 * pair + par, par, True, True)
                    ssm(s, NCH - 2, 0, True, False)
                    ssm(s, NCH - 1, 1, False, False)
                    pe.wait_ge(S["resid_done"], OPEN + s * FIN + NCH)
                    finish(s * FIN + FIN, s * NCH + NCH)

            @block.scalar
            def _(act):
                go = act.activation

                def affine(tp, q):
                    go(chunk(q), chunk(q), ACT.Identity, bias=bn_shift, scale=bn_scale).then_inc(S["aff_done"], 1)

                def square(tp):
                    act.wait_ge(S["d_ready"], OPEN + tp + 1)
                    act.wait_ge(S["var_ready"], OPEN + tp)
                    go(SQ[:, :], D[:, :], ACT.Square).then_inc(S["sq_ready"], 1)

                def rstd(tp):
                    act.wait_ge(S["var_ready"], OPEN + tp + 1)
                    act.wait_ge(S["dn_ready"], OPEN + tp)
                    go(RS[:, :], bank_b[:, :], ACT.Ln, bias=eps_c).then_inc(S["lnv_ready"], 1)
                    act.wait_ge(S["lnv_ready"], OPEN + tp + 1)
                    go(RS[:, :], RS[:, :], ACT.Exp, scale=-0.5).then_inc(S["rstd_ready"], 1)

                def normed(tp):
                    act.wait_ge(S["dn_ready"], OPEN + tp + 1)
                    act.wait_ge(S["carry_ready"], OPEN + tp + 1)
                    go(un[:, HIST:HIST + CH], D[:, :], ACT.Identity, bias=vec[:, 3:4],
                       scale=vec[:, 2:3]).then_inc(S["un_ready"], 1)

                def sigmoid(tp, src, h, ready, e, l, g, bias):
                    act.wait_ge(S[ready], OPEN + tp + 1)
                    if bias is None:
                        go(EG[:, :], src[:, :], ACT.Exp, scale=-1.0).then_inc(S[e], 1)
                    else:
                        go(EG[:, :], src[:, :], ACT.Exp, bias=bias, scale=-1.0).then_inc(S[e], 1)
                    act.wait_ge(S[e], OPEN + tp + 1)
                    go(EG[:, :], EG[:, :], ACT.Ln, bias=one_c).then_inc(S[l], 1)
                    act.wait_ge(S[l], OPEN + tp + 1)
                    go(sg[:, h, :], EG[:, :], ACT.Exp, scale=-1.0).then_inc(S[g], 1)

                def z_sigmoid(tp, h):
                    act.wait_ge(S[f"xm_ready{h}"], OPEN + tp + 1)
                    act.wait_ge(S["zg0" if h else "cg1"], OPEN + tp + 1)
                    sigmoid(tp, prep[h], h, f"z_ready{h}", f"ze{h}", f"zl{h}", f"zg{h}", None)

                def x_sigmoid(tp, h):
                    act.wait_ge(S[f"zs_ready{h}"], OPEN + tp)
                    act.wait_ge(S["cg0" if h else "zg1"], OPEN + tp + h)
                    sigmoid(tp, prep[h], h, f"cv_ready{h}", f"ce{h}", f"cl{h}", f"cg{h}", nconv_b_c[h])

                def rows(tp):
                    act.wait_ge(S["dbl_ready"], OPEN + tp + 1)
                    act.wait_ge(S["dp_ready1"], OPEN + tp)
                    act.copy(rrow[ROWS:ROWS + R, :], bank_a[ROWS:ROWS + R, :]).then_inc(S["r_ready"], 1)

                def soft_z(tp, h):
                    act.wait_ge(S[f"dp_ready{h}"], OPEN + tp + 1)
                    act.wait_ge(S[f"sw{1 - h}"], OPEN + tp + h)
                    src = prep[h]
                    go(pa[:, :], src[:, :], ACT.Abs, bias=dt_b_c[h]).then_inc(S[f"sa{h}"], 1)
                    act.wait_ge(S[f"dt_ready{h}"], OPEN + tp)
                    go(pr[:, h, :], src[:, :], ACT.Relu, bias=dt_b_c[h]).then_inc(S[f"sr{h}"], 1)
                    act.wait_ge(S[f"sa{h}"], OPEN + tp + 1)
                    act.wait_ge(S[f"ss{1 - h}"], OPEN + tp + h)
                    go(pz[:, :], pa[:, :], ACT.Exp, scale=-1.0).then_inc(S[f"sz{h}"], 1)

                def soft_w(tp, h):
                    act.wait_ge(S[f"sz{h}"], OPEN + tp + 1)
                    go(pa[:, :], pz[:, :], ACT.Ln, bias=two_c).then_inc(S[f"sl{h}"], 1)
                    act.wait_ge(S[f"sl{h}"], OPEN + tp + 1)
                    go(pw[:, :], pa[:, :], ACT.Exp, scale=-1.0).then_inc(S[f"sw{h}"], 1)

                def series(tp, h):
                    act.wait_ge(S[f"ss{h}"], OPEN + tp + 1)
                    act.wait_ge(S[f"dt_ready{h}"], OPEN + tp)
                    go(pq[:, h, :], ps[:, h, :], ACT.Square).then_inc(S[f"sq{h}"], 1)
                    act.wait_ge(S[f"sq{h}"], OPEN + tp + 1)
                    go(pp[:, h, :], pq[:, h, :], ACT.Identity, bias=atanh2_c, scale=ATANH[3]).then_inc(S[f"sp{h}"], 1)

                def decays(t, n, par):
                    for h in range(HALVES):
                        if n == 0:
                            act.wait_ge(S[f"dt_ready{h}"], OPEN + t + 1)
                        k = 2 * n + h
                        act.wait_ge(S["h_done"], OPEN + t * PAIRS + k + 1)
                        go(decay[:, k % RING, :], dt_s[:, par, h, :], ACT.Exp,
                           scale=A_s[:, h, n:n + 1]).then_inc(S["da_ready"], 1)

                def c_copy(t, n):
                    act.wait_ge(S["c_ready"], OPEN + t * N + n + 1)
                    act.wait_ge(S["hc_done"], OPEN + RING + t * PAIRS + 2 * (n - CRING + 1))
                    act.copy(csb[:, n % CRING, :], psum_bc[bc_bank[n]][:, :]).then_inc(S["c_copied"], 1)

                def ssm(s, q, par, mid, norm):
                    t = s * NCH + q
                    for n in range(N):
                        if n + 1 < N:
                            c_copy(t, n + 1)
                            decays(t, n + 1, par)
                        elif mid:
                            c_copy(t + 1, 0)
                        if norm and n == 2:
                            affine(t + 2, q + 2)
                        if mid:
                            if n in (1, 2):
                                x_sigmoid(t + 1, n - 1)
                            if n == 5:
                                rows(t + 1)
                            if n in (7, 9):
                                soft_z(t + 1, (n - 7) // 2)
                            if n in (8, 10):
                                soft_w(t + 1, (n - 8) // 2)
                        if norm:
                            if n == 8:
                                square(t + 2)
                            if n == 11:
                                rstd(t + 2)
                            if n == 14:
                                normed(t + 2)
                        if mid:
                            if n in (10, 11):
                                series(t + 1, n - 10)
                            if n in (12, 13):
                                z_sigmoid(t + 1, n - 12)
                            if n == N - 1:
                                decays(t + 1, 0, 1 - par)

                with act.Fori(0, LAYERS) as s:
                    t0 = s * NCH
                    act.wait_ge(S["weights_loaded"], OPEN + (s + 1) * 16 * NW)
                    go(Aexp[:, :, :], A_s[:, :, :], ACT.Exp).then_inc(S["a_exp"], 1)
                    act.wait_ge(S["a_exp"], OPEN + s + 1)
                    act.mul(A_s[:, :, :], Aexp[:, :, :], -1.0).then_inc(S["a_ready"], 1)
                    act.mul(evec[:, 3, :], evec[:, 0, :], -1.0).then_inc(S["nb_ready"], 1)
                    act.wait_ge(S["bn_agg"], OPEN + s + 1)
                    go(bn_ln, bn_var, ACT.Ln, bias=eps_c).then_inc(S["bn_lnv"], 1)
                    act.wait_ge(S["bn_lnv"], OPEN + s + 1)
                    go(bn_rs, bn_ln, ACT.Exp, scale=-0.5).then_inc(S["bn_rstd"], 1)
                    act.wait_ge(S["bn_ready"], OPEN + s + 1)
                    act.wait_ge(S["a_ready"], OPEN + s + 1)
                    act.wait_ge(S["nb_ready"], OPEN + s + 1)
                    affine(t0, 0)
                    affine(t0 + 1, 1)
                    square(t0)
                    rstd(t0)
                    normed(t0)
                    for h in range(HALVES):
                        x_sigmoid(t0, h)
                    rows(t0)
                    for h in range(HALVES):
                        soft_z(t0, h)
                        soft_w(t0, h)
                        series(t0, h)
                    for h in range(HALVES):
                        z_sigmoid(t0, h)
                    square(t0 + 1)
                    rstd(t0 + 1)
                    normed(t0 + 1)
                    c_copy(t0, 0)
                    decays(t0, 0, 0)
                    with act.Fori(0, NCH // 2 - 1) as pair:
                        for par in range(2):
                            ssm(s, 2 * pair + par, par, True, True)
                    ssm(s, NCH - 2, 0, True, False)
                    ssm(s, NCH - 1, 1, False, False)

            @block.vector
            def _(dve):
                def leaky(tp, q):
                    dve.wait_ge(S["aff_done"], OPEN + tp + 1)
                    dve.scalar_tensor_tensor(out=chunk(q), in0=chunk(q), scalar=SLOPE, in1=chunk(q), op0=ALU.mult,
                                             op1=ALU.max).then_inc(S["u_ready"], 1)

                def centre(tp, q):
                    dve.wait_ge(S["mean_ready"], OPEN + tp + 1)
                    dve.wait_ge(S["un_ready"], OPEN + tp)
                    dve.tensor_tensor(D[:, :], chunk(q), bank_b[:, :], ALU.subtract).then_inc(S["d_ready"], 1)

                def carry(tp, q):
                    dve.wait_ge(S["z_ready1"], OPEN + tp)
                    dve.tensor_scalar(un[:, 0:HIST], un[:, CH:CH + HIST], first[:, bass.ds(q, 1)], None,
                                      ALU.mult).then_inc(S["carry_ready"], 1)

                def gate(tp, h, par):
                    dve.wait_ge(S[f"zg{h}"], OPEN + tp + 1)
                    dve.tensor_tensor(zs[:, par, h, :], sg[:, h, :], prep[h][:, :],
                                      ALU.mult).then_inc(S[f"zs_ready{h}"], 1)

                def silu(tp, h):
                    dve.wait_ge(S[f"cg{h}"], OPEN + tp + 1)
                    dve.wait_ge(S["skip_done"], OPEN + tp * HALVES)
                    dve.wait_ge(S[f"dtx_ready{h}"], OPEN + tp)
                    dve.scalar_tensor_tensor(out=xm[:, h, :], in0=prep[h][:, :], scalar=conv_b_c[h],
                                             in1=sg[:, h, :], op0=ALU.add, op1=ALU.mult).then_inc(S[f"xm_ready{h}"], 1)

                def split(tp, par):
                    dve.wait_ge(S["dbl_ready"], OPEN + tp + 1)
                    p = bc3[:, par, :]
                    dve.tensor_copy(p, bank_a[0:ROWS, :]).then_inc(S["s_hi"], 1)
                    dve.wait_ge(S["s_hi"], OPEN + tp + 1)
                    dve.tensor_tensor(rest, bank_a[0:2 * BC, :], p[0:2 * BC, :], ALU.subtract).then_inc(S["s_r1"], 1)
                    dve.wait_ge(S["s_r1"], OPEN + tp + 1)
                    dve.tensor_copy(p[0:2 * BC, :], rest).then_inc(S["s_mid"], 1)
                    dve.wait_ge(S["s_mid"], OPEN + tp + 1)
                    dve.tensor_tensor(rest[0:BC, :], rest[0:BC, :], p[0:BC, :], ALU.subtract).then_inc(S["s_r2"], 1)
                    dve.wait_ge(S["s_r2"], OPEN + tp + 1)
                    dve.tensor_copy(p[0:BC, :], rest[0:BC, :]).then_inc(S["s_ready"], 1)

                def series(tp, h):
                    dve.wait_ge(S[f"sm{h}"], OPEN + tp + 1)
                    dve.scalar_tensor_tensor(out=pp[:, h, :], in0=pp[:, h, :], scalar=ATANH[1], in1=pq[:, h, :], op0=ALU.add,
                                             op1=ALU.mult).then_inc(S[f"sn{h}"], 1)
                    dve.wait_ge(S[f"sn{h}"], OPEN + tp + 1)
                    dve.scalar_tensor_tensor(out=pp[:, h, :], in0=pp[:, h, :], scalar=ATANH[0], in1=ps[:, h, :], op0=ALU.add,
                                             op1=ALU.mult).then_inc(S[f"so{h}"], 1)

                def inputs(t, n, par):
                    dve.wait_ge(S["b_ready"], OPEN + t * N + n + 1)
                    if n == 0:
                        dve.wait_ge(S["dtx_ready0"], OPEN + t + 1)
                        dve.wait_ge(S["dtx_ready1"], OPEN + t + 1)
                    dve.wait_ge(S["h_done"], OPEN + RING + t * PAIRS + 2 * n - 1)
                    for h in range(HALVES):
                        dve.tensor_tensor((psum_u, psum_bc[bc_bank[n]])[h][:, :], dtx[:, par, h, :], psum_bc[bc_bank[n]][:, :],
                                          ALU.mult).then_inc(S["u_done"], 1)

                def scans(t, n):
                    for h in range(HALVES):
                        k = 2 * n + h
                        dve.wait_ge(S["da_ready"], OPEN + t * PAIRS + k + 1)
                        dve.wait_ge(S["u_done"], OPEN + t * PAIRS + k + 1)
                        dve.wait_ge(S["hc_done"], OPEN + t * PAIRS + k + 1)
                        dve.tensor_tensor_scan(state[:, k % RING, :], decay[:, k % RING, :],
                                               (psum_u, psum_bc[bc_bank[n]])[h][:, :], hinit[:, k:k + 1], ALU.mult,
                                               ALU.add).then_inc(S["h_done"], 1)

                def keep(t, n):
                    g = n // GROUP
                    dve.wait_ge(S["h_done"], OPEN + RING + t * PAIRS + (g + 1) * RING)
                    dve.tensor_copy(kept[:, g * RING:(g + 1) * RING], state[:, :, CH - 1]).then_inc(S["kept"], 1)

                def start(t, q):
                    dve.wait_ge(S["kept"], OPEN + t * (N // GROUP))
                    dve.tensor_scalar(hinit[:, :], kept[:, :], first[:, bass.ds(q, 1)], None,
                                      ALU.mult).then_inc(S["hinit_done"], 1)
                    dve.wait_ge(S["hinit_done"], OPEN + t + 1)

                def gated(fin, t, par):
                    dve.wait_ge(S["sum_done"], OPEN + HRING + t * PAIRS)
                    dve.wait_ge(S["out_ready"], OPEN + fin - 1)
                    for h in range(HALVES):
                        dve.tensor_tensor(yg[:, h, :], zs[:, par, h, :], psum_y[h][:, :],
                                          ALU.mult).then_inc(S["y_done"], 1)

                def residual(fin, q):
                    dve.wait_ge(S["out_ready"], OPEN + fin)
                    dve.tensor_tensor(chunk(q), chunk(q), bank_a[:, :], ALU.add).then_inc(S["resid_done"], 1)

                def ssm(s, q, par, mid, norm):
                    t = s * NCH + q
                    fin = s * FIN + q + 1
                    start(t, q)
                    for n in range(N):
                        inputs(t, n, par)
                        if n == 2:
                            gated(fin, t, 1 - par)
                        scans(t, n)
                        if n % GROUP == GROUP - 1:
                            keep(t, n)
                        if mid:
                            if n in (2, 3):
                                silu(t + 1, n - 2)
                            if n == 5:
                                split(t + 1, 1 - par)
                            if n in (12, 13):
                                series(t + 1, n - 12)
                            if n in (13, 14):
                                gate(t + 1, n - 13, 1 - par)
                        if norm:
                            if n == 3:
                                leaky(t + 2, q + 2)
                            if n == 6:
                                centre(t + 2, q + 2)
                            if n == 13:
                                carry(t + 2, q + 2)
                        if n == 10:
                            residual(fin, q - 1)

                with dve.Fori(0, LAYERS) as s:
                    t0 = s * NCH
                    for b in range(NB):
                        dve.wait_ge(x_loaded[b], 16)
                        dve.wait_ge(S["resid_done"], OPEN + s * FIN)
                        for j in range(NJ):
                            q = b * NJ + j
                            dve.bn_stats(stats[:, q, :], X[:, (q + 1) * CH:(q + 2) * CH]).then_inc(S["bn_stat"], 1)
                    dve.wait_ge(S["bn_stat"], OPEN + (s + 1) * NCH)
                    dve.wait_ge(S["weights_loaded"], OPEN + (s + 1) * 16 * NW)
                    for k in range(TAPS):
                        dve.tensor_tensor(w_cv[:, k, :], w_z[:, 0:E],
                                          cw_rows.rearrange("p (e k) -> p k e", k=TAPS)[:, k, :],
                                          ALU.mult).then_inc(S["folded"], 1)
                    dve.bn_aggr(bn[:, 0:2], stats[:, :, :]).then_inc(S["bn_agg"], 1)
                    for h in range(HALVES):
                        dve.tensor_scalar(D_diag[:, h, :], ident[:, :], D_c[h], None, ALU.mult).then_inc(S["d_diag"], 1)
                    dve.wait_ge(S["bn_rstd"], OPEN + s + 1)
                    dve.tensor_tensor(bn_scale, bn_rs, vec[:, 0:1], ALU.mult).then_inc(S["bn_part"], 1)
                    dve.wait_ge(S["bn_part"], OPEN + 2 * s + 1)
                    dve.tensor_tensor(bn_ms, bn_mean, bn_scale, ALU.mult).then_inc(S["bn_part"], 1)
                    dve.wait_ge(S["bn_part"], OPEN + 2 * s + 2)
                    dve.tensor_tensor(bn_shift, vec[:, 1:2], bn_ms, ALU.subtract).then_inc(S["bn_ready"], 1)
                    leaky(t0, 0)
                    leaky(t0 + 1, 1)
                    centre(t0, 0)
                    carry(t0, 0)
                    for h in range(HALVES):
                        silu(t0, h)
                    split(t0, 0)
                    for h in range(HALVES):
                        series(t0, h)
                    for h in range(HALVES):
                        gate(t0, h, 0)
                    centre(t0 + 1, 1)
                    carry(t0 + 1, 1)
                    with dve.Fori(0, NCH // 2 - 1) as pair:
                        for par in range(2):
                            ssm(s, 2 * pair + par, par, True, True)
                    ssm(s, NCH - 2, 0, True, False)
                    ssm(s, NCH - 1, 1, False, False)
                    gated(s * FIN + FIN, t0 + NCH, 1)
                    residual(s * FIN + FIN, NCH - 1)

            @block.gpsimd
            def _(pool):
                TT = pool.tensor_tensor

                def scale_rows(tp):
                    pool.wait_ge(S["rstd_ready"], OPEN + tp + 1)
                    pool.wait_ge(S["sq_ready"], OPEN + tp + 1)
                    TT(D[:, :], D[:, :], RS[:, :], ALU.mult).then_inc(S["dn_ready"], 1)

                def ratio(tp, h):
                    pool.wait_ge(S[f"sw{h}"], OPEN + tp + 1)
                    pool.wait_ge(S[f"so{h}"], OPEN + tp)
                    TT(ps[:, h, :], pz[:, :], pw[:, :], ALU.mult).then_inc(S[f"ss{h}"], 1)

                def series(tp, h):
                    pool.wait_ge(S[f"sp{h}"], OPEN + tp + 1)
                    TT(pp[:, h, :], pp[:, h, :], pq[:, h, :], ALU.mult).then_inc(S[f"sm{h}"], 1)

                def steps(tp, h, par):
                    pool.wait_ge(S[f"so{h}"], OPEN + tp + 1)
                    TT(dt_s[:, par, h, :], pp[:, h, :], pr[:, h, :], ALU.add).then_inc(S[f"dt_ready{h}"], 1)
                    pool.wait_ge(S[f"dt_ready{h}"], OPEN + tp + 1)
                    TT(dtx[:, par, h, :], dt_s[:, par, h, :], xm[:, h, :], ALU.mult).then_inc(S[f"dtx_ready{h}"], 1)

                def read_out(t, n):
                    pool.wait_ge(S["c_copied"], OPEN + t * N + n + 1)
                    for h in range(HALVES):
                        k = 2 * n + h
                        pool.wait_ge(S["h_done"], OPEN + RING + t * PAIRS + k + 1)
                        pool.wait_ge(S["sum_done"], OPEN + t * PAIRS + k + 1)
                        TT(hc[:, k % HRING, :], state[:, k % RING, :], csb[:, n % CRING, :],
                           ALU.mult).then_inc(S["hc_done"], 1)

                def ssm(s, q, par, mid, norm):
                    t = s * NCH + q
                    for n in range(N):
                        read_out(t, n)
                        if mid and n in (8, 10):
                            ratio(t + 1, (n - 8) // 2)
                        if norm and n == 12:
                            scale_rows(t + 2)
                        if mid:
                            if n in (11, 12):
                                series(t + 1, n - 11)
                            if n in (13, 14):
                                steps(t + 1, n - 13, 1 - par)

                with pool.Fori(0, LAYERS) as s:
                    t0 = s * NCH
                    scale_rows(t0)
                    for h in range(HALVES):
                        ratio(t0, h)
                        series(t0, h)
                        steps(t0, h, 0)
                    scale_rows(t0 + 1)
                    with pool.Fori(0, NCH // 2 - 1) as pair:
                        for par in range(2):
                            ssm(s, 2 * pair + par, par, True, True)
                    ssm(s, NCH - 2, 0, True, False)
                    ssm(s, NCH - 1, 1, False, False)

        stage_memory.close()

        KTs = sb("KTs", [P, L])
        QTs = sb("QTs", [P, L])
        Vs = sb("Vs", [P, KT, P])
        XR = sb("XR", [P, L])
        raw5 = sb("raw5", [P, 5, P])
        tr4 = sb("tr4", [P, 4, P])
        WvT = sb("WvT", [P, P])
        MQ = sb("MQ", [P, P])
        MK = sb("MK", [P, P])
        e1 = sb("e1", [P, 2, CH])
        probs = sb("probs", [P, 4, CH])
        acc = sb("acc", [P, 2, CH])
        q2b = sb("q2b", [PARTS, L], BF16)
        nk2 = sb("nk2", [P, KT])
        xn = sb("xn", [P, CH])
        D, T1, T2, T3, T4 = (sb(f"at{i}", [P, CH]) for i in range(5))
        ew = sb("ew", [P, NX, C])
        eb = sb("eb", [NX, C])
        rw = sb("rw", [P, NX])
        rb = sb("rb", [1, NX])
        TS = NJ * SUB
        tiny = sb("tiny", [P, 10, TS, NX])
        v_sh, v_e, v_is, v_cand, v_oh1, v_e2, v_oh2, v_g, v_r, v_w = (tiny[:, i, :, :] for i in range(10))
        red = sb("red", [P, 8, TS])
        r_m, r_m1, r_i1, r_m2, r_i2, r_den, r_rec = (red[:, i, :] for i in range(7))
        g3 = sb("g3", [P, TS, PARTS, NX], BF16)
        g3t = sb("g3t", [PARTS * NX, L], BF16)
        sel8 = sb("sel8", [PARTS * NX, NX, P], BF16)
        gx = sb("gx", [P, 2, CH])
        XN, DF, RS = KTs, QTs, XR
        SQ = Vs[:, :, :].rearrange("p k d -> p (k d)")
        gft = XR[0:NX, :]
        raw = [raw5[:, i, :] for i in range(5)]
        tr = [tr4[:, i, :] for i in range(4)]

        with nc.Block() as block:
            @block.sync
            def _(sp):
                for dst, src in ((raw[0], rotation.rearrange("(a b) -> a b", b=P)),
                                 (raw[1], entangle.rearrange("(a b) -> a b", b=P)),
                                 (raw[2], Wq), (raw[3], Wk), (raw[4], Wv),
                                 (rw[:, :], router_w), (rb[:, :], router_b.rearrange("(a e) -> a e", a=1)),
                                 (eb[:, :], expert_b), (ew[:, :, :], expert_w.rearrange("e c d -> c e d"))):
                    sp.dma_start(dst, src).then_inc(S["w_att"], 16)
                sp.dma_start(XR[:, :], x_in[:, 0, :]).then_inc(S["xr_loaded"], 16)

            @block.tensor
            def _(pe):
                pe.wait_ge(S["w_att"], OPEN + 9 * 16)
                for i in range(5):
                    pe.transpose(bank[i][:, 0:P], raw[i], ident[:, :]).then_inc(S["w_tr"], 1)
                pe.wait_ge(S["w_trc"], OPEN + 5)
                for i in range(2):
                    pe.matmul(bank[5 + i][:, 0:P], tr[i], tr[2 + i], start=True, stop=True).then_inc(S["w_mm"], 1)

            @block.vector
            def _(dve):
                for i, dst in enumerate(tr + [WvT[:, :]]):
                    dve.wait_ge(S["w_tr"], OPEN + i + 1)
                    dve.tensor_copy(dst, bank[i][:, 0:P]).then_inc(S["w_trc"], 1)
                for i, dst in enumerate((MQ[:, :], MK[:, :])):
                    dve.wait_ge(S["w_mm"], OPEN + i + 1)
                    dve.tensor_copy(dst, bank[5 + i][:, 0:P])

        with nc.Block() as block:
            @block.sync
            def _(sp):
                with sp.Fori(1, NB) as b:
                    sp.wait_ge(S["a_x"], OPEN + b * NJ)
                    sp.dma_start(XR[:, :], x_in[:, bass.ds(b, 1), :].rearrange("p a c -> p (a c)")).then_inc(S["xr_loaded"], 16)

            def cols_of(a, j):
                return a[:, bass.ds(j * CH, CH)]

            @block.tensor
            def _(pe):
                mm = pe.matmul
                with pe.Fori(0, NB) as b:
                    with pe.Fori(0, NJ) as j:
                        c = b * NJ + j
                        pe.wait_ge(S["a_x"], OPEN + c + 1)
                        mm(bank[7][:, :], mean_w[:, :], chunk(c), start=True, stop=True).then_inc(S["a_mean"], 1)
                        pe.wait_ge(S["a_sq"], OPEN + c + 1)
                        mm(bank[6][:, :], mean_w[:, :], T1[:, :], start=True, stop=True).then_inc(S["a_var"], 1)
                        pe.wait_ge(S["a_xn"], OPEN + c + 1)
                        mm(bank[4][:, :], MQ[:, :], xn[:, :], start=True, stop=True).then_inc(S["a_q"], 1)
                        mm(bank[5][:, :], MK[:, :], xn[:, :], start=True, stop=True).then_inc(S["a_k"], 1)
                        for i in range(SUB):
                            last = mm(bank[3][:, i * P:(i + 1) * P], xn[:, i * P:(i + 1) * P], WvT[:, :], start=True, stop=True)
                        last.then_inc(S["a_v"], 1)
                        pe.wait_ge(S["a_qs"], OPEN + c + 1)
                        mm(bank[1][0:PARTS, :], neghalf_c, T4[:, :], start=True, stop=True).then_inc(S["a_q2"], 1)
                        pe.wait_ge(S["a_ks"], OPEN + c + 1)
                        for i in range(SUB):
                            last = mm(bank[2][:, i:i + 1], T2[:, i * P:(i + 1) * P], negone_c, start=True, stop=True)
                        last.then_inc(S["a_k2"], 1)
                    with pe.Fori(0, NJ) as j:
                        c = b * NJ + j
                        pe.wait_ge(S["a_k2c"], OPEN + (b + 1) * NJ)
                        pe.wait_ge(S["a_kc"], OPEN + (b + 1) * NJ)
                        pe.wait_ge(S["a_qc"], OPEN + (b + 1) * NJ)
                        pe.wait_ge(S["a_vc"], OPEN + (b + 1) * NJ)
                        for k in range(KT + 2):
                            if k < KT:
                                pe.wait_ge(S["e1_done"], OPEN + c * KT + max(k - 2, 0))
                                mm(bank[k % 3][:, :], KTs[:, k * P:(k + 1) * P], cols_of(QTs, j), start=True, stop=False)
                                mm(bank[k % 3][:, :], onesb[:, :], cols_of(q2b, j), start=False,
                                   stop=True).then_inc(S["qk_ready"], 1)
                            if k >= 2:
                                m = k - 2
                                if m == 0:
                                    pe.wait_ge(S["o_done"], OPEN + c)
                                pe.wait_ge(S["p_ready"], OPEN + c * KT + m + 1)
                                mm(bank[3][:, :], Vs[:, m, :], probs[:, m % 4, :], start=m == 0,
                                   stop=m == KT - 1).then_inc(S["pv_done"], 1)
                        pe.wait_ge(S["acc_done"], OPEN + (c + 1) * KT)
                        for i in range(2):
                            last = mm(bank[4][:, :], ones[:, :], acc[:, i, :], start=i == 0, stop=i == 1)
                        last.then_inc(S["den_ready"], 1)

            @block.scalar
            def _(act):
                go = act.activation
                with act.Fori(0, NB) as b:
                    with act.Fori(0, NJ) as j:
                        c = b * NJ + j
                        act.wait_ge(S["a_d"], OPEN + c + 1)
                        go(T1[:, :], D[:, :], ACT.Square).then_inc(S["a_sq"], 1)
                        act.wait_ge(S["a_var"], OPEN + c + 1)
                        act.wait_ge(S["a_k2"], OPEN + c)
                        go(T2[:, :], bank[6][:, :], ACT.Ln, bias=eps_c).then_inc(S["a_ln"], 1)
                        act.wait_ge(S["a_ln"], OPEN + c + 1)
                        go(T3[:, :], T2[:, :], ACT.Exp, scale=-0.5).then_inc(S["a_rs"], 1)
                        act.wait_ge(S["a_q"], OPEN + c + 1)
                        act.wait_ge(S["a_q2"], OPEN + c)
                        go(T4[:, :], bank[4][:, :], ACT.Square).then_inc(S["a_qs"], 1)
                        act.copy(cols_of(QTs, j), bank[4][:, :]).then_inc(S["a_qc"], 1)
                        act.wait_ge(S["a_k"], OPEN + c + 1)
                        act.wait_ge(S["a_rs"], OPEN + c + 1)
                        go(T2[:, :], bank[5][:, :], ACT.Square).then_inc(S["a_ks"], 1)
                    with act.Fori(0, NJ) as j:
                        c = b * NJ + j
                        act.wait_ge(S["a_k2c"], OPEN + (b + 1) * NJ)
                        for k in range(KT + 1):
                            if k < KT:
                                act.wait_ge(S["qk_ready"], OPEN + c * KT + k + 1)
                                act.wait_ge(S["p_ready"], OPEN + c * KT + max(k - 1, 0))
                                go(e1[:, k % 2, :], bank[k % 3][:, :], ACT.Exp, bias=nk2[:, k:k + 1],
                                   scale=2.0).then_inc(S["e1_done"], 1)
                            if k >= 1:
                                m = k - 1
                                act.wait_ge(S["e1_done"], OPEN + c * KT + m + 1)
                                act.wait_ge(S["pv_done"], OPEN + c * KT + max(m - 3, 0))
                                act.wait_ge(S["acc_done"], OPEN + c * KT + max(m - 3, 0))
                                go(probs[:, m % 4, :], e1[:, m % 2, :], ACT.Exp).then_inc(S["p_ready"], 1)

            @block.vector
            def _(dve):
                with dve.Fori(0, NB) as b:
                    with dve.Fori(0, NJ) as j:
                        c = b * NJ + j
                        dve.wait_ge(S["xr_loaded"], OPEN + (b + 1) * 16)
                        dve.tensor_tensor(chunk(c), chunk(c), cols_of(XR, j), ALU.add).then_inc(S["a_x"], 1)
                        dve.wait_ge(S["a_mean"], OPEN + c + 1)
                        dve.tensor_tensor(D[:, :], chunk(c), bank[7][:, :], ALU.subtract).then_inc(S["a_d"], 1)
                        dve.wait_ge(S["a_rs"], OPEN + c + 1)
                        dve.wait_ge(S["a_v"], OPEN + c)
                        dve.wait_ge(S["a_qc"], OPEN + c)
                        dve.wait_ge(S["a_ks"], OPEN + c)
                        dve.wait_ge(S["a_d"], OPEN + c + 1)
                        dve.tensor_tensor(xn[:, :], D[:, :], T3[:, :], ALU.mult).then_inc(S["a_xn"], 1)
                        dve.wait_ge(S["a_ks"], OPEN + c + 1)
                        dve.tensor_scalar(cols_of(KTs, j), bank[5][:, :], 1.0, None, ALU.mult).then_inc(S["a_kc"], 1)
                        dve.wait_ge(S["a_v"], OPEN + c + 1)
                        dve.tensor_scalar(cols_of(Vs[:, :, :].rearrange("p k d -> p (k d)"), j), bank[3][:, :], 1.0, None, ALU.mult).then_inc(S["a_vc"], 1)
                        p, r = cols_of(q2b, j), D
                        dve.wait_ge(S["a_q2"], OPEN + c + 1)
                        dve.tensor_scalar(p, bank[1][0:3, :], 1.0, None, ALU.mult).then_inc(S["a_split"], 1)
                        dve.wait_ge(S["a_split"], OPEN + 5 * c + 1)
                        dve.wait_ge(S["a_xn"], OPEN + c + 1)
                        dve.tensor_tensor(r[0:2, :], bank[1][0:2, :], p[0:2, :], ALU.subtract).then_inc(S["a_split"], 1)
                        dve.wait_ge(S["a_split"], OPEN + 5 * c + 2)
                        dve.tensor_scalar(p[0:2, :], r[0:2, :], 1.0, None, ALU.mult).then_inc(S["a_split"], 1)
                        dve.wait_ge(S["a_split"], OPEN + 5 * c + 3)
                        dve.tensor_tensor(r[0:1, :], r[0:1, :], p[0:1, :], ALU.subtract).then_inc(S["a_split"], 1)
                        dve.wait_ge(S["a_split"], OPEN + 5 * c + 4)
                        dve.tensor_scalar(p[0:1, :], r[0:1, :], 1.0, None, ALU.mult).then_inc(S["a_split"], 1)
                        dve.wait_ge(S["a_k2"], OPEN + c + 1)
                        dve.tensor_scalar(nk2[:, bass.ds(j * SUB, SUB)], bank[2][:, 0:SUB], 1.0, None, ALU.mult).then_inc(S["a_k2c"], 1)
                    with dve.Fori(0, NJ) as j:
                        c = b * NJ + j
                        for k in range(KT):
                            dve.wait_ge(S["p_ready"], OPEN + c * KT + k + 1)
                            if k < 2:
                                if k == 0:
                                    dve.wait_ge(S["den_ready"], OPEN + c)
                                dve.tensor_copy(acc[:, k, :], probs[:, k % 4, :]).then_inc(S["acc_done"], 1)
                            else:
                                dve.wait_ge(S["acc_done"], OPEN + c * KT + k - 1)
                                dve.tensor_tensor(acc[:, k % 2, :], acc[:, k % 2, :], probs[:, k % 4, :],
                                                  ALU.add).then_inc(S["acc_done"], 1)
                        dve.wait_ge(S["den_ready"], OPEN + c + 1)
                        dve.reciprocal(T1[:, :], bank[4][:, :]).then_inc(S["rec_done"], 1)
                        dve.wait_ge(S["rec_done"], OPEN + c + 1)
                        dve.wait_ge(S["pv_done"], OPEN + (c + 1) * KT)
                        dve.tensor_tensor(T2[:, :], T1[:, :], bank[3][:, :], ALU.mult).then_inc(S["o_done"], 1)
                        dve.wait_ge(S["o_done"], OPEN + c + 1)
                        dve.tensor_tensor(chunk(c), chunk(c), T2[:, :], ALU.add).then_inc(S["att_done"], 1)

        def spread(a):
            return a.rearrange("p (s o) -> p s o", o=1).to_broadcast([P, TS, NX])

        def part(a, j):
            return a[:, j * CH:(j + 1) * CH]

        with nc.Block() as block:
            OUTS = 2

            @block.gpsimd
            def _(pool):
                pool.memset(sel8[:, :, :], 0.0).then_inc(S["w_cst"], 1)
                for k in range(PARTS):
                    pool.wait_ge(S["w_cst"], OPEN + 1 + k)
                    pool.affine_select(out=sel8[:, :, :], in_=sel8[:, :, :], compare_op=ALU.not_equal, fill=1.0, base=-NX * k,
                                       pattern=[[-1, NX], [0, P]], channel_multiplier=1).then_inc(S["w_cst"], 1)

            @block.sync
            def _(sp):
                with sp.Fori(0, NB) as b:
                    with sp.Fori(0, NJ) as j:
                        c = b * NJ + j
                        sp.wait_ge(S["f_out"], OPEN + OUTS + c + 1)
                        sp.dma_start(out_v[:, bass.ds(b, 1), bass.ds(j * CH, CH)].rearrange("p a c -> p (a c)"),
                                     chunk(c)).then_inc(S["stored"], 16)
                sp.wait_ge(S["stored"], OPEN + NCH * 16)

            @block.tensor
            def _(pe):
                mm = pe.matmul
                pe.wait_ge(S["w_cst"], OPEN + 1 + PARTS)
                with pe.Fori(0, NB) as b:
                    c0 = b * NJ
                    for j in range(NJ):
                        if j >= 2:
                            pe.wait_ge(S["f_d"], OPEN + c0 + j - 1)
                        mm(bank[6 + j % 2][:, :], mean_w[:, :], chunk(c0 + j), start=True,
                           stop=True).then_inc(S["f_mean"], 1)
                    for j in range(NJ):
                        pe.wait_ge(S["f_sq"], OPEN + c0 + j + 1)
                        if j >= 2:
                            pe.wait_ge(S["f_ln"], OPEN + c0 + j - 1)
                        mm(bank[4 + j % 2][:, :], mean_w[:, :], part(SQ, j), start=True,
                           stop=True).then_inc(S["f_var"], 1)
                    pe.wait_ge(S["f_out"], OPEN + OUTS + c0)
                    for j in range(NJ):
                        pe.wait_ge(S["f_xn"], OPEN + c0 + j + 1)
                        for i in range(j * SUB, (j + 1) * SUB):
                            o = bank[1][:, i * NX:(i + 1) * NX]
                            mm(o, XN[:, i * P:(i + 1) * P], rw[:, :], start=True, stop=False)
                            last = mm(o, ones[0:1, :], rb[:, :], start=False, stop=True)
                    last.then_inc(S["f_log"], 1)
                    pe.wait_ge(S["f_g3"], OPEN + b + 1)
                    for j in range(NJ):
                        if j >= 2:
                            pe.wait_ge(S["f_gt"], OPEN + c0 + j - 1)
                            pe.wait_ge(S["f_gtf"], OPEN + c0 + j - 1)
                        tb = bank[(2, 6)[j % 2]][:, 0:CH // 2].bitcast(BF16)
                        tf = bank[(3, 7)[j % 2]]
                        for i in range(SUB):
                            last = pe.transpose(tb[0:PARTS * NX, i * P:(i + 1) * P],
                                                g3[:, j * SUB + i, :, :].rearrange("p k e -> p (k e)"), identb[:, :])
                        last.then_inc(S["f_tr"], 1)
                        for i in range(SUB):
                            last = pe.transpose(tf[0:NX, i * P:(i + 1) * P], v_g[:, j * SUB + i, :], ident[:, :])
                        last.then_inc(S["f_trf"], 1)
                    pe.wait_ge(S["f_gt"], OPEN + c0 + NJ)
                    pe.wait_ge(S["f_gtf"], OPEN + c0 + NJ)
                    for j in range(NJ):
                        c = c0 + j
                        for e in range(NX + 1):
                            if e < NX:
                                pe.wait_ge(S["f_gx"], OPEN + c * NX + max(e - 1, 0))
                                mm(bank[4 + e % 2][:, :], sel8[:, e, :], part(g3t, j), start=True,
                                   stop=True).then_inc(S["f_rep"], 1)
                            if e == 1:
                                pe.wait_ge(S["f_out"], OPEN + c + 1)
                            if e >= 1:
                                pe.wait_ge(S["f_gx"], OPEN + c * NX + e)
                                mm(bank[j % 2][:, :], ew[:, e - 1, :], gx[:, (e - 1) % 2, :], start=e == 1,
                                   stop=False).then_inc(S["f_mm"], 1)
                        mm(bank[j % 2][:, :], eb[:, :], part(gft, j), start=False,
                           stop=True).then_inc(S["f_mm"], 1)

            @block.scalar
            def _(act):
                go = act.activation
                with act.Fori(0, NB) as b:
                    c0 = b * NJ
                    for j in range(NJ):
                        act.wait_ge(S["f_d"], OPEN + c0 + j + 1)
                        go(part(SQ, j), part(DF, j), ACT.Square).then_inc(S["f_sq"], 1)
                    for j in range(NJ):
                        act.wait_ge(S["f_var"], OPEN + c0 + j + 1)
                        go(part(RS, j), bank[4 + j % 2][:, :], ACT.Ln, bias=eps_c).then_inc(S["f_ln"], 1)
                        act.wait_ge(S["f_ln"], OPEN + c0 + j + 1)
                        go(part(RS, j), part(RS, j), ACT.Exp, scale=-0.5).then_inc(S["f_rs"], 1)
                    act.wait_ge(S["f_ch"], OPEN + b + 1)
                    go(v_e, v_sh, ACT.Exp).then_inc(S["f_exp"], 1)
                    for j in range(NJ):
                        act.wait_ge(S["f_tr"], OPEN + c0 + j + 1)
                        tb = bank[(2, 6)[j % 2]][:, 0:CH // 2].bitcast(BF16)
                        act.copy(part(g3t, j), tb[0:PARTS * NX, :]).then_inc(S["f_gt"], 1)
                        act.wait_ge(S["f_trf"], OPEN + c0 + j + 1)
                        act.copy(part(gft, j), bank[(3, 7)[j % 2]][0:NX, :]).then_inc(S["f_gtf"], 1)

            @block.vector
            def _(dve):
                NCHAIN = 22

                for e in range(NX):
                    dve.memset(v_w[:, :, e:e + 1], float(NX - e))
                dve.sem_inc(S["f_out"], OUTS)
                with dve.Fori(0, NB) as b:
                    c0 = b * NJ
                    done = [0]

                    def link(ins):
                        done[0] += 1
                        ins.then_inc(S["f_chain"], 1)
                        dve.wait_ge(S["f_chain"], OPEN + b * NCHAIN + done[0])
                    TT, TR = dve.tensor_tensor, dve.tensor_reduce
                    dve.wait_ge(S["f_xn"], OPEN + c0)
                    for j in range(NJ):
                        dve.wait_ge(S["f_mean"], OPEN + c0 + j + 1)
                        TT(part(DF, j), chunk(c0 + j), bank[6 + j % 2][:, :], ALU.subtract).then_inc(S["f_d"], 1)
                    dve.wait_ge(S["f_d"], OPEN + c0 + NJ)
                    for j in range(NJ):
                        dve.wait_ge(S["f_rs"], OPEN + c0 + j + 1)
                        TT(part(XN, j), part(DF, j), part(RS, j), ALU.mult).then_inc(S["f_xn"], 1)
                    dve.wait_ge(S["f_log"], OPEN + b + 1)
                    logits = bank[1][:, 0:TS * NX].rearrange("p (s e) -> p s e", e=NX)
                    link(TR(r_m, logits, AX_X, ALU.max))
                    TT(v_sh, logits, spread(r_m), ALU.subtract).then_inc(S["f_ch"], 1)
                    dve.wait_ge(S["f_exp"], OPEN + b + 1)
                    link(TR(r_m1, v_e, AX_X, ALU.max))
                    link(TT(v_is, v_e, spread(r_m1), ALU.is_equal))
                    link(TT(v_cand, v_is, v_w, ALU.mult))
                    link(TR(r_i1, v_cand, AX_X, ALU.max))
                    link(TT(v_oh1, v_cand, spread(r_i1), ALU.is_equal))
                    link(dve.scalar_tensor_tensor(out=v_e2, in0=v_oh1, scalar=-2.0, in1=v_e, op0=ALU.mult, op1=ALU.add))
                    link(TR(r_m2, v_e2, AX_X, ALU.max))
                    link(TT(v_is, v_e2, spread(r_m2), ALU.is_equal))
                    link(TT(v_cand, v_is, v_w, ALU.mult))
                    link(TR(r_i2, v_cand, AX_X, ALU.max))
                    link(TT(v_oh2, v_cand, spread(r_i2), ALU.is_equal))
                    link(TT(r_den, r_m1, r_m2, ALU.add))
                    link(dve.reciprocal(r_rec, r_den))
                    link(TT(v_oh1, v_oh1, v_oh2, ALU.add))
                    link(TT(v_e2, v_e, v_oh1, ALU.mult))
                    link(TT(v_g, v_e2, spread(r_rec), ALU.mult))
                    link(dve.tensor_copy(g3[:, :, 2, :], v_g))
                    link(TT(v_r, v_g, g3[:, :, 2, :], ALU.subtract))
                    link(dve.tensor_copy(g3[:, :, 1, :], v_r))
                    link(TT(v_r, v_r, g3[:, :, 1, :], ALU.subtract))
                    link(dve.tensor_copy(g3[:, :, 0, :], v_r))
                    assert done[0] == NCHAIN
                    dve.sem_inc(S["f_g3"], 1)
                    for j in range(NJ):
                        c = c0 + j
                        for e in range(NX):
                            dve.wait_ge(S["f_rep"], OPEN + c * NX + e + 1)
                            dve.wait_ge(S["f_mm"], OPEN + c * (NX + 1) + max(e - 1, 0))
                            TT(gx[:, e % 2, :], part(XN, j), bank[4 + e % 2][:, :],
                               ALU.mult).then_inc(S["f_gx"], 1)
                        dve.wait_ge(S["f_mm"], OPEN + (c + 1) * (NX + 1))
                        TT(chunk(c), chunk(c), bank[j % 2][:, :], ALU.add).then_inc(S["f_out"], 1)


_INS = ['x', 'L0_conv_bn_gamma', 'L0_conv_bn_beta', 'L0_conv_ln_gamma', 'L0_conv_ln_beta', 'L0_conv_W_in',
        'L0_conv_conv_w', 'L0_conv_conv_b', 'L0_conv_W_xp', 'L0_conv_W_dt', 'L0_conv_b_dt', 'L0_conv_A_log',
        'L0_conv_Dp', 'L0_conv_W_out', 'L1_attn_rotation_params', 'L1_attn_entangle_params', 'L1_attn_Wq',
        'L1_attn_Wk', 'L1_attn_Wv', 'L1_ffn_router_w', 'L1_ffn_router_b', 'L1_ffn_expert_w', 'L1_ffn_expert_b']
_OUTS = [((4, 128, 64, 64), 'float32')]


def kernel(**inputs):
    import numpy as _np
    import concourse.bacc as _bacc
    from concourse import mybir as _mybir
    from concourse.bass_utils import run_bass_kernel_spmd as _run

    nc = _bacc.Bacc("TRN2", target_bir_lowering=False, num_devices=1)
    arrays, args = {}, []
    for name in _INS:
        a = _np.ascontiguousarray(inputs[name])
        arrays[f"in_{name}_dram"] = a
        args.append(nc.dram_tensor(f"in_{name}_dram", a.shape, _mybir.dt.from_np(a.dtype), kind="ExternalInput").ap())
    for i, (shape, dtype) in enumerate(_OUTS):
        dt = _mybir.dt.from_np(_np.dtype(dtype))
        args.append(nc.dram_tensor(f"out_{i}_dram", shape, dt, kind="ExternalOutput").ap())
    hybrid_kernel(nc, *args)
    r = _run(nc, [arrays], core_ids=[0])
    got = tuple(r.results[0][f"out_{i}_dram"] for i in range(len(_OUTS)))
    return got[0]
```

```python
import math
from contextlib import ExitStack

import concourse.bass as bass
from concourse import mybir

ALU = mybir.AluOpType
ACT = mybir.ActivationFunctionType
AX_X = mybir.AxisListType.X
F32 = mybir.dt.float32
BF16 = mybir.dt.bfloat16

P = 128
CH = 512
TABLES = "natural_log_exp_and_others"
SLOPE = 0.01
EPS = 1e-5
RING = 8
HRING = 4
CRING = 4
OPEN = 1
ATANH = (1.99999967, 0.66676006, 0.39589371, 0.34226697)
HALF = ATANH[2] / ATANH[3] / 2
SQ_ADD = ATANH[1] / ATANH[3] - HALF ** 2
TOP_ADD = ATANH[0] / ATANH[3]


def hybrid_kernel(nc, x, bn_gamma, bn_beta, ln_gamma, ln_beta, W_in, conv_w, conv_b, W_xp, W_dt, b_dt, A_log, Dp,
                  W_out, rotation, entangle, Wq, Wk, Wv, router_w, router_b, expert_w, expert_b, out):
    NB, C, HH, WW = x.shape
    L = HH * WW
    LAYERS, _, E2 = W_in.shape
    E = E2 // 2
    TAPS = conv_w.shape[2]
    R = W_dt.shape[1]
    N = A_log.shape[2]
    NX = router_w.shape[1]
    HALVES = E // P
    NJ = L // CH
    NCH = NB * NJ
    KT = L // P
    SUB = CH // P
    BC = 2 * N
    PARTS = 3
    ROWS = PARTS * BC
    PAIRS = N * HALVES
    GROUP = RING // HALVES
    HIST = TAPS - 1
    HALF_TAPS = range(TAPS // 2), range(TAPS // 2, TAPS)
    FIN = NCH + 1
    assert C == P and HALVES == 2 and ROWS == 96 and NCH % 2 == 0

    x_in = x.rearrange("b c h w -> c b (h w)")
    out_v = out.rearrange("b c h w -> c b (h w)")

    with ExitStack() as ctx:
        def sb(name, shape, dt=F32):
            return ctx.enter_context(nc.sbuf_tensor(name, shape, dt))

        def sem(name):
            return ctx.enter_context(nc.semaphore(name))

        bank = [ctx.enter_context(nc.psum_tensor(f"bank{i}", [P, CH], F32)) for i in range(8)]

        X = sb("X", [P, (NCH + 1) * CH])
        ident = sb("ident", [P, P])
        identb = sb("identb", [P, P], BF16)
        mean_w = sb("mean_w", [P, P])
        ones = sb("ones", [P, P])
        onesb = sb("onesb", [PARTS, P], BF16)
        cols = sb("cols", [P, 9])
        eps_c, one_c, negone_c, two_c, half_c = (cols[:, i:i + 1] for i in range(5))
        lead_c = cols[:, 8:9]
        neghalf_c = cols[:, 5:8]

        zeros, consts = sem("zeros"), sem("consts")
        x_loaded = [sem(f"x_loaded{b}") for b in range(NB)]
        names = """weights_loaded folded d_diag a_exp a_ready nb_ready bn_stat bn_agg bn_lnv bn_rstd
            bn_part bn_ready aff_done u_ready mean_ready d_ready sq_ready var_ready lnv_ready rstd_ready dn_ready
            carry_ready un_ready z_ready0 z_ready1 ze0 ze1 zl0 zl1 zg0 zg1 zs_ready0 zs_ready1 cv_ready0 cv_ready1
            ce0 ce1 cl0 cl1 cg0 cg1 xm_ready0 xm_ready1 dbl_ready s_hi s_r1 s_mid s_r2 s_ready r_ready
            dp_ready0 dp_ready1 f_lt f_lb sa0 sa1 sr0 sr1 sz0 sz1 sl0 sl1 sw0 sw1 ss0 ss1 sq0 sq1 sp0 sp1 sn0 sn1
            so0 so1 dt_ready0 dt_ready1 dtx_ready0 dtx_ready1 b_ready c_ready c_copied u_done h_done da_ready hc_done
            sum_done skip_done kept hinit_done y_done out_ready resid_done
            w_att w_tr w_trc w_mm xr_loaded
            a_x a_mean a_d a_sq a_var a_ln a_rs a_xn a_q a_k a_v a_qc a_qs a_kc a_ks a_vc a_k2 a_q2 a_k2c
            a_split qk_ready e1_done p_ready pv_done acc_done den_ready rec_done o_done att_done
            f_mean f_d f_sq f_var f_ln f_rs f_xn f_log f_ch f_exp f_chain f_g3 f_tr f_trf f_gt f_gtf f_rep f_gx f_mm
            f_out stored w_cst""".split()
        S = {n: sem(n) for n in names}

        def chunk(q, n=1):
            return X[:, bass.ds((q + 1) * CH, n * CH)]

        stage_memory = ExitStack()

        def sbs(name, shape, dt=F32):
            return stage_memory.enter_context(nc.sbuf_tensor(name, shape, dt))

        decay = sbs("decay", [P, RING, CH])
        state = sbs("state", [P, RING, CH])
        hc = sbs("hc", [P, HRING, CH])
        csb = sbs("csb", [P, CRING, CH])
        dt_s = sbs("dt_s", [P, 2, HALVES, CH])
        dtx = sbs("dtx", [P, 2, HALVES, CH])
        xm = sbs("xm", [P, HALVES, CH])
        zs = sbs("zs", [P, 2, HALVES, CH])
        yg = sbs("yg", [P, HALVES, CH])
        bc3 = sbs("bc3", [ROWS, 2, CH], BF16)
        un = sbs("un", [P, HIST + CH])
        D, SQ, RS = (sbs(f"ln{i}", [P, CH]) for i in range(3))
        EG = sbs("sig", [P, CH])
        sg = sbs("sg", [P, HALVES, CH])
        rrow = sbs("rrow", [P, CH])
        rest = rrow[0:2 * BC, :]
        pa, pz, pw = (sbs(f"sp_{n}", [P, CH]) for n in "azw")
        ps, pq, pp, pr = (sbs(f"sp_{n}", [P, HALVES, CH]) for n in "sqpr")
        sel = sbs("sel", [ROWS, BC, P], BF16)
        D_diag = sbs("D_diag", [P, HALVES, P])
        first = sbs("first", [P, NCH])
        w_z = sbs("w_z", [P, E2])
        cw_rows = decay[:, 0:E * TAPS // CH, :].rearrange("p a c -> p (a c)")
        w_cv = sbs("w_cv", [P, TAPS, E])
        w_xp = sbs("w_xp", [P, HALVES, ROWS + R])
        w_dt = sbs("w_dt", [P, E])
        w_out = sbs("w_out", [P, HALVES, C])
        vec = sbs("vec", [P, 4])
        evec = sbs("evec", [P, 4, HALVES])
        A_s = sbs("A_s", [P, HALVES, N])
        Aexp = sbs("Aexp", [P, HALVES, N])
        stats = sbs("stats", [P, NCH, 6])
        bn = sbs("bn", [P, 8])
        kept = sbs("kept", [P, PAIRS])
        hinit = sbs("hinit", [P, PAIRS])

        conv_b_c = [evec[:, 0, h:h + 1] for h in range(HALVES)]
        dt_b_c = [evec[:, 1, h:h + 1] for h in range(HALVES)]
        D_c = [evec[:, 2, h:h + 1] for h in range(HALVES)]
        nconv_b_c = [evec[:, 3, h:h + 1] for h in range(HALVES)]
        bn_mean, bn_var, bn_ln, bn_rs, bn_scale, bn_ms, bn_shift = (bn[:, i:i + 1] for i in range(7))

        psum_y = bank[0:2]
        psum_bc = bank[2:5]
        psum_u = bank[5]
        bank_a, bank_b = prep = bank[6:8]
        bc_bank = [n % 3 for n in range(N - 1)] + [1]
        bc_last = [min(d for d in range(1, N) if bc_bank[(n - d) % N] == bc_bank[n]) for n in range(N)]
        assert N % 3 == 1 and min(bc_last) == 2

        with nc.Block() as block:
            @block.sync
            def _(sp):
                for b in range(NB):
                    sp.dma_start(X[:, (1 + b * NJ) * CH:(1 + (b + 1) * NJ) * CH], x_in[:, b, :]).then_inc(x_loaded[b], 16)
                for n in names:
                    sp.sem_inc(S[n], OPEN)

            @block.gpsimd
            def _(pool):
                pool.memset(ident[:, :], 0.0).then_inc(zeros, 1)
                pool.memset(identb[:, :], 0.0).then_inc(zeros, 1)
                pool.memset(sel[:, :, :], 0.0).then_inc(zeros, 1)
                pool.wait_ge(zeros, 3)
                for m in (ident, identb):
                    pool.affine_select(out=m[:, :], in_=m[:, :], compare_op=ALU.not_equal, fill=1.0, base=0,
                                       pattern=[[-1, P]], channel_multiplier=1).then_inc(zeros, 1)
                pool.wait_ge(zeros, 5)
                for k in range(PARTS):
                    pool.affine_select(out=sel[:, :, :], in_=sel[:, :, :], compare_op=ALU.not_equal, fill=1.0,
                                       base=-BC * k, pattern=[[-1, BC], [0, P]],
                                       channel_multiplier=1).then_inc(zeros, 1)
                    pool.wait_ge(zeros, 6 + k)

            @block.vector
            def _(dve):
                dve.memset(mean_w[:, :], 1.0 / C)
                dve.memset(ones[:, :], 1.0)
                dve.memset(onesb[:, :], 1.0)
                dve.memset(eps_c, EPS)
                dve.memset(one_c, 1.0)
                dve.memset(negone_c, -1.0)
                dve.memset(two_c, 2.0)
                dve.memset(half_c, HALF)
                dve.memset(lead_c, math.log(ATANH[3]))
                dve.memset(neghalf_c, -0.5)
                dve.memset(first[:, :], 1.0).then_inc(consts, 1)
                dve.wait_ge(consts, 1)
                dve.memset(first[:, :].rearrange("p (b j) -> p b j", j=NJ)[:, :, 0:1], 0.0)
                dve.memset(X[:, 0:CH], 0.0)
                dve.memset(un[:, :], 0.0)
                dve.memset(kept[:, :], 0.0)
                for h in range(HALVES):
                    dve.memset(psum_y[h][:, :], 0.0)
                    dve.memset(zs[:, 1, h, :], 0.0)
                dve.sem_inc(S["h_done"], RING)
                dve.sem_inc(S["hc_done"], RING)
                dve.sem_inc(S["sum_done"], HRING)

            @block.scalar
            def _(act):
                act.preload_act_table_set(TABLES)

        with nc.Block() as block:

            @block.sync
            def _(sp):
                with sp.Fori(0, LAYERS) as s:
                    sp.wait_ge(S["resid_done"], OPEN + s * FIN)
                    w = S["weights_loaded"]

                    def of(a, pattern, **kw):
                        return a[bass.ds(s, 1)].rearrange(pattern, **kw)
                    for i, a in enumerate((bn_gamma, bn_beta, ln_gamma, ln_beta)):
                        sp.dma_start(vec[:, i:i + 1], of(a, "a c -> c a")).then_inc(w, 16)
                    sp.dma_start(w_z[:, :], of(W_in, "a c e -> (a c) e")).then_inc(w, 16)
                    sp.dma_start(cw_rows, of(conv_w, "a e k -> a (e k)").to_broadcast([P, E * TAPS])).then_inc(w, 16)
                    for i, a in enumerate((conv_b, b_dt, Dp)):
                        sp.dma_start(evec[:, i, :], of(a, "a (h p) -> (a p) h", p=P),
                                     allow_slow_non_contiguous=True).then_inc(w, 16)
                    for k in range(PARTS):
                        sp.dma_start(w_xp[:, :, k * BC:(k + 1) * BC],
                                     of(W_xp, "a (h p) r -> (a p) h r", p=P)[:, :, R:R + BC]).then_inc(w, 16)
                    sp.dma_start(w_xp[:, :, ROWS:ROWS + R],
                                 of(W_xp, "a (h p) r -> (a p) h r", p=P)[:, :, 0:R]).then_inc(w, 16)
                    sp.dma_start(w_dt[ROWS:ROWS + R, :], of(W_dt, "a r e -> (a r) e")).then_inc(w, 16)
                    sp.dma_start(A_s[:, :, :], of(A_log, "a (h p) n -> (a p) h n", p=P)).then_inc(w, 16)
                    sp.dma_start(w_out[:, :, :], of(W_out, "a (h p) c -> (a p) h c", p=P)).then_inc(w, 16)
            NW = 4 + 1 + 1 + 3 + PARTS + 1 + 1 + 1 + 1

            @block.tensor
            def _(pe):
                mm = pe.matmul

                def mean(tp, q, read):
                    pe.wait_ge(S["u_ready"], OPEN + tp + 1)
                    pe.wait_ge(S[read], OPEN + tp)
                    mm(bank_b[:, :], mean_w[:, :], chunk(q), start=True, stop=True).then_inc(S["mean_ready"], 1)

                def var(tp):
                    pe.wait_ge(S["sq_ready"], OPEN + tp + 1)
                    pe.wait_ge(S["sr1"], OPEN + tp)
                    mm(bank_b[:, :], mean_w[:, :], SQ[:, :], start=True, stop=True).then_inc(S["var_ready"], 1)

                def gate(tp, h, fin, lns):
                    if h == 0:
                        pe.wait_ge(S["sr0"], OPEN + tp + 1)
                        pe.wait_ge(S["resid_done"], OPEN + fin)
                    else:
                        pe.wait_ge(S["sr1"], OPEN + tp + 1)
                        pe.wait_ge(S["lnv_ready"], OPEN + lns)
                    mm(prep[h][:, :], w_z[:, E + h * P:E + (h + 1) * P], un[:, HIST:HIST + CH],
                       start=True, stop=True).then_inc(S[f"z_ready{h}"], 1)

                def conv(tp, h, taps=range(TAPS)):
                    if 0 in taps:
                        pe.wait_ge(S["un_ready"], OPEN + tp + 1)
                        pe.wait_ge(S[f"zs_ready{h}"], OPEN + tp)
                    for k in taps:
                        last = mm(prep[h][:, :], w_cv[:, k, h * P:(h + 1) * P], un[:, k:k + CH],
                                  start=k == 0, stop=k == TAPS - 1)
                    if TAPS - 1 in taps:
                        last.then_inc(S[f"cv_ready{h}"], 1)

                def dbl(tp):
                    pe.wait_ge(S["xm_ready0"], OPEN + tp + 1)
                    pe.wait_ge(S["xm_ready1"], OPEN + tp + 1)
                    for h in range(HALVES):
                        last = mm(bank_a[0:ROWS + R, :], w_xp[:, h, :], xm[:, h, :],
                                  start=h == 0, stop=h == HALVES - 1)
                    last.then_inc(S["dbl_ready"], 1)

                def step(tp, h, centred):
                    pe.wait_ge(S["r_ready"], OPEN + tp + 1)
                    if h == 0:
                        pe.wait_ge(S["s_r1"], OPEN + tp + 1)
                    else:
                        pe.wait_ge(S["xm_ready1"], OPEN + tp + 1)
                        pe.wait_ge(S["d_ready"], OPEN + centred)
                    mm(prep[h][:, :], w_dt[ROWS:ROWS + R, h * P:(h + 1) * P], rrow[ROWS:ROWS + R, :],
                       start=True, stop=True).then_inc(S[f"dp_ready{h}"], 1)

                def finish(fin, steps):
                    pe.wait_ge(S["y_done"], OPEN + fin * HALVES)
                    pe.wait_ge(S["sr0"], OPEN + steps)
                    for h in range(HALVES):
                        last = mm(bank_a[:, :], w_out[:, h, :], yg[:, h, :],
                                  start=h == 0, stop=h == HALVES - 1)
                    last.then_inc(S["out_ready"], 1)

                def spread_c(t, n, par):
                    if n == 0:
                        pe.wait_ge(S["s_ready"], OPEN + t + 1)
                    pe.wait_ge(S["h_done"], OPEN + RING + t * PAIRS + 2 * (n - bc_last[n] + 1))
                    mm(psum_bc[bc_bank[n]][:, :], sel[:, N + n, :], bc3[:, par, :], start=True,
                       stop=True).then_inc(S["c_ready"], 1)

                def spread_b(t, n, par):
                    pe.wait_ge(S["c_copied"], OPEN + t * N + n + 1)
                    mm(psum_bc[bc_bank[n]][:, :], sel[:, n, :], bc3[:, par, :], start=True,
                       stop=True).then_inc(S["b_ready"], 1)

                def skip(fin):
                    pe.wait_ge(S["y_done"], OPEN + fin * HALVES)
                    for h in range(HALVES):
                        mm(psum_y[h][:, :], D_diag[:, h, :], xm[:, h, :], start=True,
                           stop=False).then_inc(S["skip_done"], 1)

                def gather(t, n):
                    for h in range(HALVES):
                        k = 2 * n + h
                        pe.wait_ge(S["hc_done"], OPEN + RING + t * PAIRS + k + 1)
                        mm(psum_y[h][:, :], ident[:, :], hc[:, k % HRING, :], start=False,
                           stop=n == N - 1).then_inc(S["sum_done"], 1)

                def ssm(s, q, par, mid, norm):
                    t = s * NCH + q
                    fin = s * FIN + q + 1
                    for m in range(2, N + 2):
                        if m == 2:
                            skip(fin)
                        if m + 1 < N:
                            spread_b(t, m + 1, par)
                        elif mid:
                            spread_b(t + 1, m + 1 - N, 1 - par)
                        gather(t, m - 2)
                        over, n = divmod(m + 2, N)
                        ahead = (t + over, n, par if over == 0 else 1 - par)
                        if (mid or over == 0) and bc_last[n] > 2:
                            spread_c(*ahead)
                        if mid and m == 4:
                            dbl(t + 1)
                        if norm and m == 5:
                            mean(t + 2, q + 2, "xm_ready1")
                        if mid and m in (6, 7):
                            step(t + 1, m - 6, t + 2 + norm)
                        if m == 9:
                            finish(fin, t + 1 + mid)
                        if norm and m == 10:
                            var(t + 2)
                        if mid and m in (11, 12):
                            gate(t + 1, m - 11, fin, t + 2 + norm)
                        if norm and m in (15, 16):
                            conv(t + 2, 0, HALF_TAPS[m - 15])
                        if norm and m in (16, 17):
                            conv(t + 2, 1, HALF_TAPS[m - 16])
                        if (mid or over == 0) and bc_last[n] == 2:
                            spread_c(*ahead)

                def opening(s):
                    t0 = s * NCH
                    mean(t0, 0, "zs_ready1")
                    var(t0)
                    for h in range(HALVES):
                        conv(t0, h)
                    dbl(t0)
                    for h in range(HALVES):
                        step(t0, h, t0 + 1)
                    for h in range(HALVES):
                        gate(t0, h, s * FIN, t0 + 1)
                    mean(t0 + 1, 1, "zs_ready1")
                    var(t0 + 1)
                    spread_c(t0, 0, 0)
                    spread_c(t0, 1, 0)
                    spread_b(t0, 0, 0)
                    conv(t0 + 1, 0)
                    for m in range(2):
                        conv(t0 + 1, 1, HALF_TAPS[m])
                        spread_b(t0, m + 1, 0)
                        spread_c(t0, m + 2, 0)

                with pe.Fori(0, LAYERS) as s:
                    pe.wait_ge(S["weights_loaded"], OPEN + (s + 1) * 16 * NW)
                    pe.wait_ge(S["folded"], OPEN + (s + 1) * TAPS)
                    pe.wait_ge(S["d_diag"], OPEN + (s + 1) * HALVES)
                    opening(s)
                    with pe.Fori(0, NCH // 2 - 1) as pair:
                        for par in range(2):
                            ssm(s, 2 * pair + par, par, True, True)
                    ssm(s, NCH - 2, 0, True, False)
                    ssm(s, NCH - 1, 1, False, False)
                    pe.wait_ge(S["resid_done"], OPEN + s * FIN + NCH)
                    finish(s * FIN + FIN, s * NCH + NCH)

            @block.scalar
            def _(act):
                go = act.activation

                def affine(tp, q):
                    go(chunk(q), chunk(q), ACT.Identity, bias=bn_shift, scale=bn_scale).then_inc(S["aff_done"], 1)

                def square(tp):
                    act.wait_ge(S["d_ready"], OPEN + tp + 1)
                    act.wait_ge(S["var_ready"], OPEN + tp)
                    go(SQ[:, :], D[:, :], ACT.Square).then_inc(S["sq_ready"], 1)

                def rstd(tp):
                    act.wait_ge(S["var_ready"], OPEN + tp + 1)
                    act.wait_ge(S["dn_ready"], OPEN + tp)
                    go(RS[:, :], bank_b[:, :], ACT.Ln, bias=eps_c).then_inc(S["lnv_ready"], 1)
                    act.wait_ge(S["lnv_ready"], OPEN + tp + 1)
                    go(RS[:, :], RS[:, :], ACT.Exp, scale=-0.5).then_inc(S["rstd_ready"], 1)

                def normed(tp):
                    act.wait_ge(S["dn_ready"], OPEN + tp + 1)
                    act.wait_ge(S["carry_ready"], OPEN + tp + 1)
                    go(un[:, HIST:HIST + CH], D[:, :], ACT.Identity, bias=vec[:, 3:4],
                       scale=vec[:, 2:3]).then_inc(S["un_ready"], 1)

                def sigmoid(tp, src, h, ready, e, l, g, bias):
                    act.wait_ge(S[ready], OPEN + tp + 1)
                    if bias is None:
                        go(EG[:, :], src[:, :], ACT.Exp, scale=-1.0).then_inc(S[e], 1)
                    else:
                        go(EG[:, :], src[:, :], ACT.Exp, bias=bias, scale=-1.0).then_inc(S[e], 1)
                    act.wait_ge(S[e], OPEN + tp + 1)
                    go(EG[:, :], EG[:, :], ACT.Ln, bias=one_c).then_inc(S[l], 1)
                    act.wait_ge(S[l], OPEN + tp + 1)
                    go(sg[:, h, :], EG[:, :], ACT.Exp, scale=-1.0).then_inc(S[g], 1)

                def z_sigmoid(tp, h):
                    act.wait_ge(S[f"xm_ready{h}"], OPEN + tp + 1)
                    act.wait_ge(S["zg0" if h else "cg1"], OPEN + tp + 1)
                    sigmoid(tp, prep[h], h, f"z_ready{h}", f"ze{h}", f"zl{h}", f"zg{h}", None)

                def x_sigmoid(tp, h):
                    act.wait_ge(S[f"zs_ready{h}"], OPEN + tp)
                    act.wait_ge(S["cg0" if h else "zg1"], OPEN + tp + h)
                    sigmoid(tp, prep[h], h, f"cv_ready{h}", f"ce{h}", f"cl{h}", f"cg{h}", nconv_b_c[h])

                def rows(tp):
                    act.wait_ge(S["dbl_ready"], OPEN + tp + 1)
                    act.wait_ge(S["dp_ready1"], OPEN + tp)
                    act.copy(rrow[ROWS:ROWS + R, :], bank_a[ROWS:ROWS + R, :]).then_inc(S["r_ready"], 1)

                def soft_z(tp, h):
                    act.wait_ge(S[f"dp_ready{h}"], OPEN + tp + 1)
                    act.wait_ge(S[f"sw{1 - h}"], OPEN + tp + h)
                    src = prep[h]
                    go(pa[:, :], src[:, :], ACT.Abs, bias=dt_b_c[h]).then_inc(S[f"sa{h}"], 1)
                    act.wait_ge(S[f"dt_ready{h}"], OPEN + tp)
                    go(pr[:, h, :], src[:, :], ACT.Relu, bias=dt_b_c[h]).then_inc(S[f"sr{h}"], 1)
                    act.wait_ge(S[f"sa{h}"], OPEN + tp + 1)
                    act.wait_ge(S[f"ss{1 - h}"], OPEN + tp + h)
                    go(pz[:, :], pa[:, :], ACT.Exp, scale=-1.0).then_inc(S[f"sz{h}"], 1)

                def soft_w(tp, h):
                    act.wait_ge(S[f"sz{h}"], OPEN + tp + 1)
                    go(pa[:, :], pz[:, :], ACT.Ln, bias=two_c).then_inc(S[f"sl{h}"], 1)
                    act.wait_ge(S[f"sl{h}"], OPEN + tp + 1)
                    go(pw[:, :], pa[:, :], ACT.Exp, bias=lead_c, scale=-1.0).then_inc(S[f"sw{h}"], 1)

                def series(tp, h):
                    act.wait_ge(S[f"ss{h}"], OPEN + tp + 1)
                    act.wait_ge(S[f"dt_ready{h}"], OPEN + tp)
                    go(pq[:, h, :], ps[:, h, :], ACT.Square, scale=1.0 / ATANH[3]).then_inc(S[f"sq{h}"], 1)
                    act.wait_ge(S[f"sq{h}"], OPEN + tp + 1)
                    go(pp[:, h, :], pq[:, h, :], ACT.Square, bias=half_c).then_inc(S[f"sp{h}"], 1)

                def decays(t, n, par):
                    for h in range(HALVES):
                        if n == 0:
                            act.wait_ge(S[f"dt_ready{h}"], OPEN + t + 1)
                        k = 2 * n + h
                        act.wait_ge(S["h_done"], OPEN + t * PAIRS + k + 1)
                        go(decay[:, k % RING, :], dt_s[:, par, h, :], ACT.Exp,
                           scale=A_s[:, h, n:n + 1]).then_inc(S["da_ready"], 1)

                def c_copy(t, n):
                    act.wait_ge(S["c_ready"], OPEN + t * N + n + 1)
                    act.wait_ge(S["hc_done"], OPEN + RING + t * PAIRS + 2 * (n - CRING + 1))
                    act.copy(csb[:, n % CRING, :], psum_bc[bc_bank[n]][:, :]).then_inc(S["c_copied"], 1)

                def ssm(s, q, par, mid, norm):
                    t = s * NCH + q
                    for n in range(N):
                        if n + 1 < N:
                            c_copy(t, n + 1)
                            decays(t, n + 1, par)
                        elif mid:
                            c_copy(t + 1, 0)
                        if norm and n == 2:
                            affine(t + 2, q + 2)
                        if mid:
                            if n in (1, 2):
                                x_sigmoid(t + 1, n - 1)
                            if n == 5:
                                rows(t + 1)
                            if n in (7, 9):
                                soft_z(t + 1, (n - 7) // 2)
                            if n in (8, 10):
                                soft_w(t + 1, (n - 8) // 2)
                        if norm:
                            if n == 8:
                                square(t + 2)
                            if n == 11:
                                rstd(t + 2)
                            if n == 14:
                                normed(t + 2)
                        if mid:
                            if n in (9, 11):
                                series(t + 1, (n - 9) // 2)
                            if n in (12, 13):
                                z_sigmoid(t + 1, n - 12)
                            if n == N - 1:
                                decays(t + 1, 0, 1 - par)

                with act.Fori(0, LAYERS) as s:
                    t0 = s * NCH
                    act.wait_ge(S["weights_loaded"], OPEN + (s + 1) * 16 * NW)
                    go(Aexp[:, :, :], A_s[:, :, :], ACT.Exp).then_inc(S["a_exp"], 1)
                    act.wait_ge(S["a_exp"], OPEN + s + 1)
                    act.mul(A_s[:, :, :], Aexp[:, :, :], -1.0).then_inc(S["a_ready"], 1)
                    act.mul(evec[:, 3, :], evec[:, 0, :], -1.0).then_inc(S["nb_ready"], 1)
                    act.wait_ge(S["bn_agg"], OPEN + s + 1)
                    go(bn_ln, bn_var, ACT.Ln, bias=eps_c).then_inc(S["bn_lnv"], 1)
                    act.wait_ge(S["bn_lnv"], OPEN + s + 1)
                    go(bn_rs, bn_ln, ACT.Exp, scale=-0.5).then_inc(S["bn_rstd"], 1)
                    act.wait_ge(S["bn_ready"], OPEN + s + 1)
                    act.wait_ge(S["a_ready"], OPEN + s + 1)
                    act.wait_ge(S["nb_ready"], OPEN + s + 1)
                    affine(t0, 0)
                    affine(t0 + 1, 1)
                    square(t0)
                    rstd(t0)
                    normed(t0)
                    for h in range(HALVES):
                        x_sigmoid(t0, h)
                    rows(t0)
                    for h in range(HALVES):
                        soft_z(t0, h)
                        soft_w(t0, h)
                        series(t0, h)
                    for h in range(HALVES):
                        z_sigmoid(t0, h)
                    square(t0 + 1)
                    rstd(t0 + 1)
                    normed(t0 + 1)
                    c_copy(t0, 0)
                    decays(t0, 0, 0)
                    with act.Fori(0, NCH // 2 - 1) as pair:
                        for par in range(2):
                            ssm(s, 2 * pair + par, par, True, True)
                    ssm(s, NCH - 2, 0, True, False)
                    ssm(s, NCH - 1, 1, False, False)

            @block.vector
            def _(dve):
                def leaky(tp, q):
                    dve.wait_ge(S["aff_done"], OPEN + tp + 1)
                    dve.scalar_tensor_tensor(out=chunk(q), in0=chunk(q), scalar=SLOPE, in1=chunk(q), op0=ALU.mult,
                                             op1=ALU.max).then_inc(S["u_ready"], 1)

                def centre(tp, q):
                    dve.wait_ge(S["mean_ready"], OPEN + tp + 1)
                    dve.wait_ge(S["un_ready"], OPEN + tp)
                    dve.tensor_tensor(D[:, :], chunk(q), bank_b[:, :], ALU.subtract).then_inc(S["d_ready"], 1)

                def carry(tp, q):
                    dve.wait_ge(S["z_ready1"], OPEN + tp)
                    dve.tensor_scalar(un[:, 0:HIST], un[:, CH:CH + HIST], first[:, bass.ds(q, 1)], None,
                                      ALU.mult).then_inc(S["carry_ready"], 1)

                def gate(tp, h, par):
                    dve.wait_ge(S[f"zg{h}"], OPEN + tp + 1)
                    dve.tensor_tensor(zs[:, par, h, :], sg[:, h, :], prep[h][:, :],
                                      ALU.mult).then_inc(S[f"zs_ready{h}"], 1)

                def silu(tp, h):
                    dve.wait_ge(S[f"cg{h}"], OPEN + tp + 1)
                    dve.wait_ge(S["skip_done"], OPEN + tp * HALVES)
                    dve.wait_ge(S[f"dtx_ready{h}"], OPEN + tp)
                    dve.scalar_tensor_tensor(out=xm[:, h, :], in0=prep[h][:, :], scalar=conv_b_c[h],
                                             in1=sg[:, h, :], op0=ALU.add, op1=ALU.mult).then_inc(S[f"xm_ready{h}"], 1)

                def split(tp, par):
                    dve.wait_ge(S["dbl_ready"], OPEN + tp + 1)
                    p = bc3[:, par, :]
                    dve.tensor_copy(p, bank_a[0:ROWS, :]).then_inc(S["s_hi"], 1)
                    dve.wait_ge(S["s_hi"], OPEN + tp + 1)
                    dve.tensor_tensor(rest, bank_a[0:2 * BC, :], p[0:2 * BC, :], ALU.subtract).then_inc(S["s_r1"], 1)
                    dve.wait_ge(S["s_r1"], OPEN + tp + 1)
                    dve.tensor_copy(p[0:2 * BC, :], rest).then_inc(S["s_mid"], 1)
                    dve.wait_ge(S["s_mid"], OPEN + tp + 1)
                    dve.tensor_tensor(rest[0:BC, :], rest[0:BC, :], p[0:BC, :], ALU.subtract).then_inc(S["s_r2"], 1)
                    dve.wait_ge(S["s_r2"], OPEN + tp + 1)
                    dve.tensor_copy(p[0:BC, :], rest[0:BC, :]).then_inc(S["s_ready"], 1)

                def series(tp, h):
                    dve.wait_ge(S[f"sp{h}"], OPEN + tp + 1)
                    dve.scalar_tensor_tensor(out=pp[:, h, :], in0=pp[:, h, :], scalar=SQ_ADD, in1=pq[:, h, :], op0=ALU.add,
                                             op1=ALU.mult).then_inc(S[f"sn{h}"], 1)
                    dve.wait_ge(S[f"sn{h}"], OPEN + tp + 1)
                    dve.scalar_tensor_tensor(out=pp[:, h, :], in0=pp[:, h, :], scalar=TOP_ADD, in1=ps[:, h, :], op0=ALU.add,
                                             op1=ALU.mult).then_inc(S[f"so{h}"], 1)

                def inputs(t, n, par):
                    dve.wait_ge(S["b_ready"], OPEN + t * N + n + 1)
                    if n == 0:
                        dve.wait_ge(S["dtx_ready0"], OPEN + t + 1)
                        dve.wait_ge(S["dtx_ready1"], OPEN + t + 1)
                    dve.wait_ge(S["h_done"], OPEN + RING + t * PAIRS + 2 * n - 1)
                    for h in range(HALVES):
                        dve.tensor_tensor((psum_u, psum_bc[bc_bank[n]])[h][:, :], dtx[:, par, h, :], psum_bc[bc_bank[n]][:, :],
                                          ALU.mult).then_inc(S["u_done"], 1)

                def scans(t, n):
                    for h in range(HALVES):
                        k = 2 * n + h
                        dve.wait_ge(S["da_ready"], OPEN + t * PAIRS + k + 1)
                        dve.wait_ge(S["u_done"], OPEN + t * PAIRS + k + 1)
                        dve.wait_ge(S["hc_done"], OPEN + t * PAIRS + k + 1)
                        dve.tensor_tensor_scan(state[:, k % RING, :], decay[:, k % RING, :],
                                               (psum_u, psum_bc[bc_bank[n]])[h][:, :], hinit[:, k:k + 1], ALU.mult,
                                               ALU.add).then_inc(S["h_done"], 1)

                def keep(t, n):
                    g = n // GROUP
                    dve.wait_ge(S["h_done"], OPEN + RING + t * PAIRS + (g + 1) * RING)
                    dve.tensor_copy(kept[:, g * RING:(g + 1) * RING], state[:, :, CH - 1]).then_inc(S["kept"], 1)

                def start(t, q):
                    dve.wait_ge(S["kept"], OPEN + t * (N // GROUP))
                    dve.tensor_scalar(hinit[:, :], kept[:, :], first[:, bass.ds(q, 1)], None,
                                      ALU.mult).then_inc(S["hinit_done"], 1)
                    dve.wait_ge(S["hinit_done"], OPEN + t + 1)

                def gated(fin, t, par):
                    dve.wait_ge(S["sum_done"], OPEN + HRING + t * PAIRS)
                    dve.wait_ge(S["out_ready"], OPEN + fin - 1)
                    for h in range(HALVES):
                        dve.tensor_tensor(yg[:, h, :], zs[:, par, h, :], psum_y[h][:, :],
                                          ALU.mult).then_inc(S["y_done"], 1)

                def residual(fin, q):
                    dve.wait_ge(S["out_ready"], OPEN + fin)
                    dve.tensor_tensor(chunk(q), chunk(q), bank_a[:, :], ALU.add).then_inc(S["resid_done"], 1)

                def ssm(s, q, par, mid, norm):
                    t = s * NCH + q
                    fin = s * FIN + q + 1
                    start(t, q)
                    for n in range(N):
                        inputs(t, n, par)
                        if n == 2:
                            gated(fin, t, 1 - par)
                        scans(t, n)
                        if n % GROUP == GROUP - 1:
                            keep(t, n)
                        if mid:
                            if n in (2, 3):
                                silu(t + 1, n - 2)
                            if n == 5:
                                split(t + 1, 1 - par)
                            if n in (10, 12):
                                series(t + 1, (n - 10) // 2)
                            if n in (13, 14):
                                gate(t + 1, n - 13, 1 - par)
                        if norm:
                            if n == 3:
                                leaky(t + 2, q + 2)
                            if n == 6:
                                centre(t + 2, q + 2)
                            if n == 13:
                                carry(t + 2, q + 2)
                        if n == 11:
                            residual(fin, q - 1)

                with dve.Fori(0, LAYERS) as s:
                    t0 = s * NCH
                    for b in range(NB):
                        dve.wait_ge(x_loaded[b], 16)
                        dve.wait_ge(S["resid_done"], OPEN + s * FIN)
                        for j in range(NJ):
                            q = b * NJ + j
                            dve.bn_stats(stats[:, q, :], X[:, (q + 1) * CH:(q + 2) * CH]).then_inc(S["bn_stat"], 1)
                    dve.wait_ge(S["bn_stat"], OPEN + (s + 1) * NCH)
                    dve.wait_ge(S["weights_loaded"], OPEN + (s + 1) * 16 * NW)
                    for k in range(TAPS):
                        dve.tensor_tensor(w_cv[:, k, :], w_z[:, 0:E],
                                          cw_rows.rearrange("p (e k) -> p k e", k=TAPS)[:, k, :],
                                          ALU.mult).then_inc(S["folded"], 1)
                    dve.bn_aggr(bn[:, 0:2], stats[:, :, :]).then_inc(S["bn_agg"], 1)
                    for h in range(HALVES):
                        dve.tensor_scalar(D_diag[:, h, :], ident[:, :], D_c[h], None, ALU.mult).then_inc(S["d_diag"], 1)
                    dve.wait_ge(S["bn_rstd"], OPEN + s + 1)
                    dve.tensor_tensor(bn_scale, bn_rs, vec[:, 0:1], ALU.mult).then_inc(S["bn_part"], 1)
                    dve.wait_ge(S["bn_part"], OPEN + 2 * s + 1)
                    dve.tensor_tensor(bn_ms, bn_mean, bn_scale, ALU.mult).then_inc(S["bn_part"], 1)
                    dve.wait_ge(S["bn_part"], OPEN + 2 * s + 2)
                    dve.tensor_tensor(bn_shift, vec[:, 1:2], bn_ms, ALU.subtract).then_inc(S["bn_ready"], 1)
                    leaky(t0, 0)
                    leaky(t0 + 1, 1)
                    centre(t0, 0)
                    carry(t0, 0)
                    for h in range(HALVES):
                        silu(t0, h)
                    split(t0, 0)
                    for h in range(HALVES):
                        series(t0, h)
                    for h in range(HALVES):
                        gate(t0, h, 0)
                    centre(t0 + 1, 1)
                    carry(t0 + 1, 1)
                    with dve.Fori(0, NCH // 2 - 1) as pair:
                        for par in range(2):
                            ssm(s, 2 * pair + par, par, True, True)
                    ssm(s, NCH - 2, 0, True, False)
                    ssm(s, NCH - 1, 1, False, False)
                    gated(s * FIN + FIN, t0 + NCH, 1)
                    residual(s * FIN + FIN, NCH - 1)

            @block.gpsimd
            def _(pool):
                TT = pool.tensor_tensor

                def scale_rows(tp):
                    pool.wait_ge(S["rstd_ready"], OPEN + tp + 1)
                    pool.wait_ge(S["sq_ready"], OPEN + tp + 1)
                    TT(D[:, :], D[:, :], RS[:, :], ALU.mult).then_inc(S["dn_ready"], 1)

                def ratio(tp, h):
                    pool.wait_ge(S[f"sw{h}"], OPEN + tp + 1)
                    pool.wait_ge(S[f"so{h}"], OPEN + tp)
                    TT(ps[:, h, :], pz[:, :], pw[:, :], ALU.mult).then_inc(S[f"ss{h}"], 1)

                def step(tp, h, par):
                    pool.wait_ge(S[f"so{h}"], OPEN + tp + 1)
                    TT(dt_s[:, par, h, :], pp[:, h, :], pr[:, h, :], ALU.add).then_inc(S[f"dt_ready{h}"], 1)

                def step_x(tp, h, par):
                    pool.wait_ge(S[f"dt_ready{h}"], OPEN + tp + 1)
                    TT(dtx[:, par, h, :], dt_s[:, par, h, :], xm[:, h, :], ALU.mult).then_inc(S[f"dtx_ready{h}"], 1)

                def read_out(t, n):
                    pool.wait_ge(S["c_copied"], OPEN + t * N + n + 1)
                    for h in range(HALVES):
                        k = 2 * n + h
                        pool.wait_ge(S["h_done"], OPEN + RING + t * PAIRS + k + 1)
                        pool.wait_ge(S["sum_done"], OPEN + t * PAIRS + k + 1)
                        TT(hc[:, k % HRING, :], state[:, k % RING, :], csb[:, n % CRING, :],
                           ALU.mult).then_inc(S["hc_done"], 1)

                def ssm(s, q, par, mid, norm):
                    t = s * NCH + q
                    for n in range(N):
                        read_out(t, n)
                        if mid:
                            if n in (8, 10):
                                ratio(t + 1, (n - 8) // 2)
                            if n in (11, 13):
                                step(t + 1, (n - 11) // 2, 1 - par)
                            if n >= 14:
                                step_x(t + 1, n - 14, 1 - par)
                        if norm and n == 12:
                            scale_rows(t + 2)

                with pool.Fori(0, LAYERS) as s:
                    t0 = s * NCH
                    scale_rows(t0)
                    for h in range(HALVES):
                        ratio(t0, h)
                        step(t0, h, 0)
                        step_x(t0, h, 0)
                    scale_rows(t0 + 1)
                    with pool.Fori(0, NCH // 2 - 1) as pair:
                        for par in range(2):
                            ssm(s, 2 * pair + par, par, True, True)
                    ssm(s, NCH - 2, 0, True, False)
                    ssm(s, NCH - 1, 1, False, False)

        stage_memory.close()

        KTs = sb("KTs", [P, L])
        QTs = sb("QTs", [P, L])
        Vs = sb("Vs", [P, KT, P])
        XR = sb("XR", [P, L])
        raw5 = sb("raw5", [P, 5, P])
        tr4 = sb("tr4", [P, 4, P])
        WvT = sb("WvT", [P, P])
        MQ = sb("MQ", [P, P])
        MK = sb("MK", [P, P])
        e1 = sb("e1", [P, 2, CH])
        probs = sb("probs", [P, 4, CH])
        acc = sb("acc", [P, 2, CH])
        q2b = sb("q2b", [PARTS, L], BF16)
        nk2 = sb("nk2", [P, KT])
        T1, T2 = (sb(f"at{i}", [P, CH]) for i in range(2))
        ksq, qsq = (sb(n, [P, 2, CH]) for n in ("ksq", "qsq"))
        rest3 = sb("rest3", [PARTS, CH])
        ew = sb("ew", [P, NX, C])
        eb = sb("eb", [NX, C])
        rw = sb("rw", [P, NX])
        rb = sb("rb", [NX, 1])
        TS = NJ * SUB
        tiny = sb("tiny", [P, 10, TS, NX])
        v_sh, v_e, v_is, v_cand, v_oh1, v_e2, v_oh2, v_g, v_r, v_w = (tiny[:, i, :, :] for i in range(10))
        red = sb("red", [P, 8, TS])
        r_m, r_m1, r_i1, r_m2, r_i2, r_den, r_rec = (red[:, i, :] for i in range(7))
        g3 = sb("g3", [P, TS, PARTS, NX], BF16)
        g3t = sb("g3t", [PARTS * NX, L], BF16)
        sel8 = sb("sel8", [PARTS * NX, NX, P], BF16)
        gx = probs[:, 0:3, :]
        XN, RS, SQ = XR, KTs, QTs
        DF = Vs[:, :, :].rearrange("p k d -> p (k d)")
        TOK, SQR = XR, QTs
        lgt = acc[0:NX, :, :]
        gft = KTs[0:NX, :]
        raw = [raw5[:, i, :] for i in range(5)]
        tr = [tr4[:, i, :] for i in range(4)]

        def part(a, j):
            return a[:, j * CH:(j + 1) * CH]

        with nc.Block() as block:
            @block.sync
            def _(sp):
                for dst, src in ((raw[0], rotation.rearrange("(a b) -> a b", b=P)),
                                 (raw[1], entangle.rearrange("(a b) -> a b", b=P)),
                                 (raw[2], Wq), (raw[3], Wk), (raw[4], Wv),
                                 (rw[:, :], router_w), (rb[:, :], router_b.rearrange("(e a) -> e a", a=1)),
                                 (eb[:, :], expert_b), (ew[:, :, :], expert_w.rearrange("e c d -> c e d"))):
                    sp.dma_start(dst, src).then_inc(S["w_att"], 16)
                sp.dma_start(XR[:, :], x_in[:, 0, :]).then_inc(S["xr_loaded"], 16)

            @block.tensor
            def _(pe):
                pe.wait_ge(S["w_att"], OPEN + 9 * 16)
                for i in range(5):
                    pe.transpose(bank[i][:, 0:P], raw[i], ident[:, :]).then_inc(S["w_tr"], 1)
                pe.wait_ge(S["w_trc"], OPEN + 5)
                for i in range(2):
                    pe.matmul(bank[5 + i][:, 0:P], tr[i], tr[2 + i], start=True, stop=True).then_inc(S["w_mm"], 1)

            @block.vector
            def _(dve):
                for i, dst in enumerate(tr + [WvT[:, :]]):
                    dve.wait_ge(S["w_tr"], OPEN + i + 1)
                    dve.tensor_copy(dst, bank[i][:, 0:P]).then_inc(S["w_trc"], 1)
                for i, dst in enumerate((MQ[:, :], MK[:, :])):
                    dve.wait_ge(S["w_mm"], OPEN + i + 1)
                    dve.tensor_copy(dst, bank[5 + i][:, 0:P])

        with nc.Block() as block:
            @block.sync
            def _(sp):
                with sp.Fori(1, NB) as b:
                    sp.wait_ge(S["a_v"], OPEN + b * NJ)
                    sp.dma_start(XR[:, :], x_in[:, bass.ds(b, 1), :].rearrange("p a c -> p (a c)")).then_inc(S["xr_loaded"], 16)

            OB = 3, 5

            def cols_of(a, j):
                return a[:, bass.ds(j * CH, CH)]

            @block.tensor
            def _(pe):
                mm = pe.matmul
                with pe.Fori(0, NB) as b:
                    c0 = b * NJ
                    for j in range(NJ):
                        pe.wait_ge(S["a_x"], OPEN + c0 + j + 1)
                        if j >= 2:
                            pe.wait_ge(S["a_d"], OPEN + c0 + j - 1)
                        mm(bank[6 + j % 2][:, :], mean_w[:, :], chunk(c0 + j), start=True,
                           stop=True).then_inc(S["a_mean"], 1)
                    for j in range(NJ):
                        pe.wait_ge(S["a_sq"], OPEN + c0 + j + 1)
                        if j >= 2:
                            pe.wait_ge(S["a_ln"], OPEN + c0 + j - 1)
                        mm(bank[4 + j % 2][:, :], mean_w[:, :], part(SQ, j), start=True,
                           stop=True).then_inc(S["a_var"], 1)
                    for j in range(NJ + 1):
                        if j < NJ:
                            pe.wait_ge(S["a_xn"], OPEN + c0 + j + 1)
                            if j >= 2:
                                pe.wait_ge(S["a_qc"], OPEN + c0 + j - 1)
                                pe.wait_ge(S["a_kc"], OPEN + c0 + j - 1)
                                pe.wait_ge(S["a_vc"], OPEN + c0 + j - 1)
                            mm(bank[j % 2][:, :], MQ[:, :], part(XN, j), start=True, stop=True).then_inc(S["a_q"], 1)
                            mm(bank[2 + j % 2][:, :], MK[:, :], part(XN, j), start=True,
                               stop=True).then_inc(S["a_k"], 1)
                            for i in range(SUB):
                                last = mm(bank[6 + j % 2][:, i * P:(i + 1) * P], part(XN, j)[:, i * P:(i + 1) * P],
                                          WvT[:, :], start=True, stop=True)
                            last.then_inc(S["a_v"], 1)
                        if j >= 1:
                            h = j - 1
                            if h == 0:
                                pe.wait_ge(S["a_ln"], OPEN + c0 + NJ)
                            else:
                                pe.wait_ge(S["a_split"], OPEN + 5 * (c0 + h - 1) + 2)
                            pe.wait_ge(S["a_qs"], OPEN + c0 + h + 1)
                            mm(bank[5][0:PARTS, :], neghalf_c, qsq[:, h % 2, :], start=True,
                               stop=True).then_inc(S["a_q2"], 1)
                            pe.wait_ge(S["a_ks"], OPEN + c0 + h + 1)
                            for i in range(SUB):
                                last = mm(bank[4][:, h * SUB + i:h * SUB + i + 1], ksq[:, h % 2, i * P:(i + 1) * P],
                                          negone_c, start=True, stop=True)
                            last.then_inc(S["a_k2"], 1)
                    with pe.Fori(0, NJ // 2) as pair:
                        for u in range(2):
                            j = 2 * pair + u
                            c = b * NJ + j
                            pe.wait_ge(S["a_k2c"], OPEN + b + 1)
                            pe.wait_ge(S["a_split"], OPEN + 5 * (b + 1) * NJ)
                            pe.wait_ge(S["a_kc"], OPEN + (b + 1) * NJ)
                            pe.wait_ge(S["a_qc"], OPEN + (b + 1) * NJ)
                            pe.wait_ge(S["a_vc"], OPEN + (b + 1) * NJ)
                            for k in range(KT + 2):
                                if k < KT:
                                    pe.wait_ge(S["e1_done"], OPEN + c * KT + max(k - 2, 0))
                                    mm(bank[k % 3][:, :], KTs[:, k * P:(k + 1) * P], cols_of(QTs, j), start=True, stop=False)
                                    mm(bank[k % 3][:, :], onesb[:, :], cols_of(q2b, j), start=False,
                                       stop=True).then_inc(S["qk_ready"], 1)
                                if k >= 2:
                                    m = k - 2
                                    if m == 0:
                                        pe.wait_ge(S["o_done"], OPEN + c)
                                    pe.wait_ge(S["p_ready"], OPEN + c * KT + m + 1)
                                    mm(bank[OB[u]][:, :], Vs[:, m, :], probs[:, m % 4, :], start=m == 0,
                                       stop=m == KT - 1).then_inc(S["pv_done"], 1)
                            pe.wait_ge(S["acc_done"], OPEN + (c + 1) * KT)
                            for i in range(2):
                                last = mm(bank[4][:, :], ones[:, :], acc[:, i, :], start=i == 0, stop=i == 1)
                            last.then_inc(S["den_ready"], 1)

            @block.scalar
            def _(act):
                go = act.activation
                with act.Fori(0, NB) as b:
                    c0 = b * NJ
                    for j in range(NJ):
                        act.wait_ge(S["a_d"], OPEN + c0 + j + 1)
                        go(part(SQ, j), part(DF, j), ACT.Square).then_inc(S["a_sq"], 1)
                    for j in range(NJ):
                        act.wait_ge(S["a_var"], OPEN + c0 + j + 1)
                        go(part(RS, j), bank[4 + j % 2][:, :], ACT.Ln, bias=eps_c).then_inc(S["a_ln"], 1)
                        act.wait_ge(S["a_ln"], OPEN + c0 + j + 1)
                        go(part(RS, j), part(RS, j), ACT.Exp, scale=-0.5).then_inc(S["a_rs"], 1)
                    for j in range(NJ):
                        act.wait_ge(S["a_q"], OPEN + c0 + j + 1)
                        if j >= 2:
                            act.wait_ge(S["a_q2"], OPEN + c0 + j - 1)
                            act.wait_ge(S["a_k2"], OPEN + c0 + j - 1)
                        go(qsq[:, j % 2, :], bank[j % 2][:, :], ACT.Square).then_inc(S["a_qs"], 1)
                        act.copy(part(QTs, j), bank[j % 2][:, :]).then_inc(S["a_qc"], 1)
                        act.wait_ge(S["a_k"], OPEN + c0 + j + 1)
                        go(ksq[:, j % 2, :], bank[2 + j % 2][:, :], ACT.Square).then_inc(S["a_ks"], 1)
                    with act.Fori(0, NJ) as j:
                        c = b * NJ + j
                        act.wait_ge(S["a_k2c"], OPEN + b + 1)
                        for k in range(KT + 1):
                            if k < KT:
                                act.wait_ge(S["qk_ready"], OPEN + c * KT + k + 1)
                                act.wait_ge(S["p_ready"], OPEN + c * KT + max(k - 1, 0))
                                go(e1[:, k % 2, :], bank[k % 3][:, :], ACT.Exp, bias=nk2[:, k:k + 1],
                                   scale=2.0).then_inc(S["e1_done"], 1)
                            if k >= 1:
                                m = k - 1
                                act.wait_ge(S["e1_done"], OPEN + c * KT + m + 1)
                                act.wait_ge(S["pv_done"], OPEN + c * KT + max(m - 3, 0))
                                act.wait_ge(S["acc_done"], OPEN + c * KT + max(m - 3, 0))
                                go(probs[:, m % 4, :], e1[:, m % 2, :], ACT.Exp).then_inc(S["p_ready"], 1)

            @block.vector
            def _(dve):
                dve.sem_inc(S["o_done"], 1)
                with dve.Fori(0, NB) as b:
                    c0 = b * NJ
                    for j in range(NJ):
                        dve.wait_ge(S["a_mean"], OPEN + c0 + j + 1)
                        dve.tensor_tensor(part(DF, j), chunk(c0 + j), bank[6 + j % 2][:, :],
                                          ALU.subtract).then_inc(S["a_d"], 1)
                    for j in range(NJ):
                        dve.wait_ge(S["a_xn"], OPEN + c0 + j + 1)
                        dve.wait_ge(S["a_ks"], OPEN + c0 + j + 1)
                        dve.tensor_scalar(part(KTs, j), bank[2 + j % 2][:, :], 1.0, None,
                                          ALU.mult).then_inc(S["a_kc"], 1)
                        dve.wait_ge(S["a_v"], OPEN + c0 + j + 1)
                        dve.tensor_scalar(part(DF, j), bank[6 + j % 2][:, :], 1.0, None,
                                          ALU.mult).then_inc(S["a_vc"], 1)
                        p, left = part(q2b, j), rest3
                        at = OPEN + 5 * (c0 + j)
                        dve.wait_ge(S["a_q2"], OPEN + c0 + j + 1)
                        dve.tensor_scalar(p, bank[5][0:3, :], 1.0, None, ALU.mult).then_inc(S["a_split"], 1)
                        dve.wait_ge(S["a_split"], at + 1)
                        dve.tensor_tensor(left[0:2, :], bank[5][0:2, :], p[0:2, :], ALU.subtract).then_inc(S["a_split"], 1)
                        dve.wait_ge(S["a_split"], at + 2)
                        dve.tensor_scalar(p[0:2, :], left[0:2, :], 1.0, None, ALU.mult).then_inc(S["a_split"], 1)
                        dve.wait_ge(S["a_split"], at + 3)
                        dve.tensor_tensor(left[0:1, :], left[0:1, :], p[0:1, :], ALU.subtract).then_inc(S["a_split"], 1)
                        dve.wait_ge(S["a_split"], at + 4)
                        dve.tensor_scalar(p[0:1, :], left[0:1, :], 1.0, None, ALU.mult).then_inc(S["a_split"], 1)
                    dve.wait_ge(S["a_k2"], OPEN + c0 + NJ)
                    dve.tensor_scalar(nk2[:, :], bank[4][:, 0:KT], 1.0, None, ALU.mult).then_inc(S["a_k2c"], 1)
                    with dve.Fori(0, NJ // 2) as pair:
                        for u in range(2):
                            j = 2 * pair + u
                            c = b * NJ + j
                            for k in range(KT):
                                dve.wait_ge(S["p_ready"], OPEN + c * KT + k + 1)
                                if k < 2:
                                    if k == 0:
                                        dve.wait_ge(S["den_ready"], OPEN + c)
                                    dve.tensor_copy(acc[:, k, :], probs[:, k % 4, :]).then_inc(S["acc_done"], 1)
                                else:
                                    dve.wait_ge(S["acc_done"], OPEN + c * KT + k - 1)
                                    dve.tensor_tensor(acc[:, k % 2, :], acc[:, k % 2, :], probs[:, k % 4, :],
                                                      ALU.add).then_inc(S["acc_done"], 1)
                            dve.wait_ge(S["den_ready"], OPEN + c + 1)
                            dve.reciprocal(T1[:, :], bank[4][:, :]).then_inc(S["rec_done"], 1)
                            dve.wait_ge(S["rec_done"], OPEN + c + 1)
                            dve.wait_ge(S["pv_done"], OPEN + (c + 1) * KT)
                            dve.tensor_tensor(T2[:, :], T1[:, :], bank[OB[u]][:, :], ALU.mult).then_inc(S["o_done"], 1)
                            dve.wait_ge(S["o_done"], OPEN + 1 + c + 1)
                            dve.tensor_tensor(chunk(c), chunk(c), T2[:, :], ALU.add).then_inc(S["att_done"], 1)

            @block.gpsimd
            def _(pool):
                with pool.Fori(0, NB) as b:
                    c0 = b * NJ
                    pool.wait_ge(S["xr_loaded"], OPEN + (b + 1) * 16)
                    for j in range(NJ):
                        pool.tensor_tensor(chunk(c0 + j), chunk(c0 + j), part(XR, j), ALU.add).then_inc(S["a_x"], 1)
                    for j in range(NJ):
                        pool.wait_ge(S["a_x"], OPEN + c0 + j + 1)
                        pool.wait_ge(S["a_rs"], OPEN + c0 + j + 1)
                        pool.tensor_tensor(part(XN, j), part(DF, j), part(RS, j), ALU.mult).then_inc(S["a_xn"], 1)

        def spread(a):
            return a.rearrange("p (s o) -> p s o", o=1).to_broadcast([P, TS, NX])

        with nc.Block() as block:
            OUTS = 2
            GB = 4

            @block.gpsimd
            def _(pool):
                pool.memset(sel8[:, :, :], 0.0).then_inc(S["w_cst"], 1)
                for k in range(PARTS):
                    pool.wait_ge(S["w_cst"], OPEN + 1 + k)
                    pool.affine_select(out=sel8[:, :, :], in_=sel8[:, :, :], compare_op=ALU.not_equal, fill=1.0, base=-NX * k,
                                       pattern=[[-1, NX], [0, P]], channel_multiplier=1).then_inc(S["w_cst"], 1)

            @block.sync
            def _(sp):
                with sp.Fori(0, NB) as b:
                    with sp.Fori(0, NJ) as j:
                        c = b * NJ + j
                        sp.wait_ge(S["f_out"], OPEN + OUTS + c + 1)
                        sp.dma_start(out_v[:, bass.ds(b, 1), bass.ds(j * CH, CH)].rearrange("p a c -> p (a c)"),
                                     chunk(c)).then_inc(S["stored"], 16)
                sp.wait_ge(S["stored"], OPEN + NCH * 16)

            @block.tensor
            def _(pe):
                mm = pe.matmul
                pe.wait_ge(S["w_cst"], OPEN + 1 + PARTS)

                def mean(c):
                    pe.wait_ge(S["f_d"], OPEN + c)
                    mm(bank[7][:, :], mean_w[:, :], chunk(c), start=True, stop=True).then_inc(S["f_mean"], 1)

                def var(c, j):
                    pe.wait_ge(S["f_sq"], OPEN + c + 1)
                    pe.wait_ge(S["f_ln"], OPEN + c)
                    mm(bank[3][:, :], mean_w[:, :], part(SQR, j), start=True, stop=True).then_inc(S["f_var"], 1)

                def batch(b, more):
                    c0 = b * NJ
                    for j in range(NJ + 1):
                        if j < NJ:
                            pe.wait_ge(S["f_xn"], OPEN + c0 + j + 1)
                            if j >= 2:
                                pe.wait_ge(S["f_lb"], OPEN + c0 + j - 1)
                            mm(bank[(2, 6)[j % 2]][0:NX, :], rw[:, :], part(TOK, j), start=True,
                               stop=True).then_inc(S["f_lt"], 1)
                        if j == 1:
                            pe.wait_ge(S["f_out"], OPEN + OUTS + c0)
                        if j >= 1:
                            pe.wait_ge(S["f_lb"], OPEN + c0 + j)
                            for i in range(SUB):
                                k = (j - 1) * SUB + i
                                last = mm(bank[1][:, k * NX:(k + 1) * NX], lgt[:, (j - 1) % 2, i * P:(i + 1) * P],
                                          ident[0:NX, 0:NX], start=True, stop=True)
                    last.then_inc(S["f_log"], 1)
                    pe.wait_ge(S["f_g3"], OPEN + b + 1)
                    for j in range(NJ):
                        if j >= 2:
                            pe.wait_ge(S["f_gt"], OPEN + c0 + j - 1)
                            pe.wait_ge(S["f_gtf"], OPEN + c0 + j - 1)
                        tb = bank[(2, 6)[j % 2]][:, 0:CH // 2].bitcast(BF16)
                        tf = bank[(3, 7)[j % 2]]
                        for i in range(SUB):
                            last = pe.transpose(tb[0:PARTS * NX, i * P:(i + 1) * P],
                                                g3[:, j * SUB + i, :, :].rearrange("p k e -> p (k e)"), identb[:, :])
                        last.then_inc(S["f_tr"], 1)
                        for i in range(SUB):
                            last = pe.transpose(tf[0:NX, i * P:(i + 1) * P], v_g[:, j * SUB + i, :], ident[:, :])
                        last.then_inc(S["f_trf"], 1)
                    pe.wait_ge(S["f_gt"], OPEN + c0 + NJ)
                    pe.wait_ge(S["f_gtf"], OPEN + c0 + NJ)
                    for g in range(NJ * NX + 2):
                        if g < NJ * NX:
                            j, e = divmod(g, NX)
                            pe.wait_ge(S["f_gx"], OPEN + c0 * NX + max(g - 2, 0))
                            mm(bank[GB + g % 3][:, :], sel8[:, e, :], part(g3t, j), start=True,
                               stop=True).then_inc(S["f_rep"], 1)
                        if g >= 2:
                            j, e = divmod(g - 2, NX)
                            if e == 0:
                                pe.wait_ge(S["f_out"], OPEN + c0 + j + 1)
                            pe.wait_ge(S["f_gx"], OPEN + c0 * NX + g - 1)
                            mm(bank[j % 2][:, :], ew[:, e, :], gx[:, (g - 2) % 3, :], start=e == 0,
                               stop=False).then_inc(S["f_mm"], 1)
                            if e == NX - 1:
                                mm(bank[j % 2][:, :], eb[:, :], part(gft, j), start=False,
                                   stop=True).then_inc(S["f_mm"], 1)
                        if more and g >= NX:
                            j = g // NX - 1
                            if g % NX == 0:
                                mean(c0 + NJ + j)
                            if g % NX == NX - 2:
                                var(c0 + NJ + j, j)
                    if more:
                        var(c0 + NJ + NJ - 1, NJ - 1)

                for j in range(NJ + 1):
                    if j < NJ:
                        mean(j)
                    if j >= 1:
                        var(j - 1, j - 1)
                with pe.Fori(0, NB - 1) as b:
                    batch(b, True)
                batch(NB - 1, False)

            @block.scalar
            def _(act):
                go = act.activation

                def norm(b):
                    for j in range(NJ):
                        c = b * NJ + j
                        act.wait_ge(S["f_d"], OPEN + c + 1)
                        go(part(SQR, j), part(TOK, j), ACT.Square).then_inc(S["f_sq"], 1)
                        act.wait_ge(S["f_var"], OPEN + c + 1)
                        go(part(SQR, j), bank[3][:, :], ACT.Ln, bias=eps_c).then_inc(S["f_ln"], 1)
                        act.wait_ge(S["f_ln"], OPEN + c + 1)
                        go(part(SQR, j), part(SQR, j), ACT.Exp, scale=-0.5).then_inc(S["f_rs"], 1)

                def batch(b, more):
                    c0 = b * NJ
                    for j in range(NJ):
                        act.wait_ge(S["f_lt"], OPEN + c0 + j + 1)
                        go(lgt[:, j % 2, :], bank[(2, 6)[j % 2]][0:NX, :], ACT.Identity,
                           bias=rb[:, :]).then_inc(S["f_lb"], 1)
                    act.wait_ge(S["f_ch"], OPEN + b + 1)
                    go(v_e, v_sh, ACT.Exp).then_inc(S["f_exp"], 1)
                    for j in range(NJ):
                        act.wait_ge(S["f_tr"], OPEN + c0 + j + 1)
                        tb = bank[(2, 6)[j % 2]][:, 0:CH // 2].bitcast(BF16)
                        act.copy(part(g3t, j), tb[0:PARTS * NX, :]).then_inc(S["f_gt"], 1)
                        act.wait_ge(S["f_trf"], OPEN + c0 + j + 1)
                        act.copy(part(gft, j), bank[(3, 7)[j % 2]][0:NX, :]).then_inc(S["f_gtf"], 1)
                    if more:
                        norm(b + 1)

                norm(0)
                with act.Fori(0, NB - 1) as b:
                    batch(b, True)
                batch(NB - 1, False)

            @block.vector
            def _(dve):
                NCHAIN = 22

                for e in range(NX):
                    dve.memset(v_w[:, :, e:e + 1], float(NX - e))
                dve.sem_inc(S["f_out"], OUTS)
                TT, TR = dve.tensor_tensor, dve.tensor_reduce

                def centre(c, j):
                    dve.wait_ge(S["f_mean"], OPEN + c + 1)
                    dve.wait_ge(S["f_gx"], OPEN + (c - NJ + 1) * NX)
                    TT(part(TOK, j), chunk(c), bank[7][:, :], ALU.subtract).then_inc(S["f_d"], 1)

                def output(c, j):
                    dve.wait_ge(S["f_mm"], OPEN + (c + 1) * (NX + 1))
                    TT(chunk(c), chunk(c), bank[j % 2][:, :], ALU.add).then_inc(S["f_out"], 1)

                def normed(c, j):
                    dve.wait_ge(S["f_d"], OPEN + c + 1)
                    dve.wait_ge(S["f_rs"], OPEN + c + 1)
                    TT(part(TOK, j), part(TOK, j), part(SQR, j), ALU.mult).then_inc(S["f_xn"], 1)

                def batch(b, more):
                    c0 = b * NJ
                    done = [0]

                    def link(ins):
                        done[0] += 1
                        ins.then_inc(S["f_chain"], 1)
                        dve.wait_ge(S["f_chain"], OPEN + b * NCHAIN + done[0])
                    dve.wait_ge(S["f_log"], OPEN + b + 1)
                    logits = bank[1][:, 0:TS * NX].rearrange("p (s e) -> p s e", e=NX)
                    link(TR(r_m, logits, AX_X, ALU.max))
                    TT(v_sh, logits, spread(r_m), ALU.subtract).then_inc(S["f_ch"], 1)
                    dve.wait_ge(S["f_exp"], OPEN + b + 1)
                    link(TR(r_m1, v_e, AX_X, ALU.max))
                    link(TT(v_is, v_e, spread(r_m1), ALU.is_equal))
                    link(TT(v_cand, v_is, v_w, ALU.mult))
                    link(TR(r_i1, v_cand, AX_X, ALU.max))
                    link(TT(v_oh1, v_cand, spread(r_i1), ALU.is_equal))
                    link(dve.scalar_tensor_tensor(out=v_e2, in0=v_oh1, scalar=-2.0, in1=v_e, op0=ALU.mult, op1=ALU.add))
                    link(TR(r_m2, v_e2, AX_X, ALU.max))
                    link(TT(v_is, v_e2, spread(r_m2), ALU.is_equal))
                    link(TT(v_cand, v_is, v_w, ALU.mult))
                    link(TR(r_i2, v_cand, AX_X, ALU.max))
                    link(TT(v_oh2, v_cand, spread(r_i2), ALU.is_equal))
                    link(TT(r_den, r_m1, r_m2, ALU.add))
                    link(dve.reciprocal(r_rec, r_den))
                    link(TT(v_oh1, v_oh1, v_oh2, ALU.add))
                    link(TT(v_e2, v_e, v_oh1, ALU.mult))
                    link(TT(v_g, v_e2, spread(r_rec), ALU.mult))
                    link(dve.tensor_copy(g3[:, :, 2, :], v_g))
                    link(TT(v_r, v_g, g3[:, :, 2, :], ALU.subtract))
                    link(dve.tensor_copy(g3[:, :, 1, :], v_r))
                    link(TT(v_r, v_r, g3[:, :, 1, :], ALU.subtract))
                    link(dve.tensor_copy(g3[:, :, 0, :], v_r))
                    assert done[0] == NCHAIN
                    dve.sem_inc(S["f_g3"], 1)
                    for j in range(NJ):
                        c = c0 + j
                        for e in range(NX):
                            g = j * NX + e
                            dve.wait_ge(S["f_rep"], OPEN + c0 * NX + g + 1)
                            if g >= 3:
                                dve.wait_ge(S["f_mm"], OPEN + c0 * (NX + 1) + g - 3 + (g - 3) // NX + 1)
                            TT(gx[:, g % 3, :], part(TOK, j), bank[GB + g % 3][:, :], ALU.mult).then_inc(S["f_gx"], 1)
                            if more and j >= 1 and e == 2:
                                centre(c + NJ - 1, j - 1)
                            if more and j >= 2 and e == 1:
                                normed(c + NJ - 2, j - 2)
                            if j >= 1 and e == 3:
                                output(c - 1, j - 1)
                    if more:
                        centre(c0 + 2 * NJ - 1, NJ - 1)
                        normed(c0 + 2 * NJ - 2, NJ - 2)
                    output(c0 + NJ - 1, NJ - 1)
                    if more:
                        normed(c0 + 2 * NJ - 1, NJ - 1)

                for j in range(NJ + 1):
                    if j < NJ:
                        dve.wait_ge(S["f_mean"], OPEN + j + 1)
                        TT(part(TOK, j), chunk(j), bank[7][:, :], ALU.subtract).then_inc(S["f_d"], 1)
                    if j >= 1:
                        normed(j - 1, j - 1)
                with dve.Fori(0, NB - 1) as b:
                    batch(b, True)
                batch(NB - 1, False)


_INS = ['x', 'L0_conv_bn_gamma', 'L0_conv_bn_beta', 'L0_conv_ln_gamma', 'L0_conv_ln_beta', 'L0_conv_W_in',
        'L0_conv_conv_w', 'L0_conv_conv_b', 'L0_conv_W_xp', 'L0_conv_W_dt', 'L0_conv_b_dt', 'L0_conv_A_log',
        'L0_conv_Dp', 'L0_conv_W_out', 'L1_attn_rotation_params', 'L1_attn_entangle_params', 'L1_attn_Wq',
        'L1_attn_Wk', 'L1_attn_Wv', 'L1_ffn_router_w', 'L1_ffn_router_b', 'L1_ffn_expert_w', 'L1_ffn_expert_b']
_OUTS = [((4, 128, 64, 64), 'float32')]


def kernel(**inputs):
    import numpy as _np
    import concourse.bacc as _bacc
    from concourse import mybir as _mybir
    from concourse.bass_utils import run_bass_kernel_spmd as _run

    nc = _bacc.Bacc("TRN2", target_bir_lowering=False, num_devices=1)
    arrays, args = {}, []
    for name in _INS:
        a = _np.ascontiguousarray(inputs[name])
        arrays[f"in_{name}_dram"] = a
        args.append(nc.dram_tensor(f"in_{name}_dram", a.shape, _mybir.dt.from_np(a.dtype), kind="ExternalInput").ap())
    for i, (shape, dtype) in enumerate(_OUTS):
        dt = _mybir.dt.from_np(_np.dtype(dtype))
        args.append(nc.dram_tensor(f"out_{i}_dram", shape, dt, kind="ExternalOutput").ap())
    hybrid_kernel(nc, *args)
    r = _run(nc, [arrays], core_ids=[0])
    got = tuple(r.results[0][f"out_{i}_dram"] for i in range(len(_OUTS)))
    return got[0]
```
